# Optimizing a Trainium2 kernel written in Bass

```python
import numpy as np
import jax
import jax.numpy as jnp

def _softmax(x, axis=-1):
    return jax.nn.softmax(x, axis=axis)

def _gelu(x):
    return jax.nn.gelu(x, approximate=True)

def _silu(x):
    return jax.nn.silu(x)

def _sigmoid(x):
    return jax.nn.sigmoid(x)

def _layernorm(x, axis=-1, eps=1e-05):
    m = jnp.mean(x, axis=axis, keepdims=True)
    v = jnp.var(x, axis=axis, keepdims=True)
    return (x - m) / jnp.sqrt(v + eps)

def _scatter_add(tgt, idx, src, axis=0):
    return tgt.at[idx].add(src)

def _segment_sum(src, seg, n):
    return jax.ops.segment_sum(src, seg, n)
kernel_name = 'mk_prb_d1_jaxref_r2_949864'

def setup_inputs(seed: int=0):
    np.random.seed(seed)
    _w = jnp.asarray

    def _L0_attn_setup():
        import jax, jax.numpy as jnp
        import numpy as np
        D_MODEL = 512
        NHEAD = 16
        WIN = 128
        key = jax.random.key(seed)
        k0, k1, k2 = jax.random.split(key, 3)
        B, S = (4, 2048)
        x = jax.random.normal(k0, (B, S, D_MODEL), dtype=jnp.float32)
        Wqkv = jax.random.normal(k1, (D_MODEL, 3 * D_MODEL), dtype=jnp.float32) * 0.02
        bqkv = jnp.zeros((3 * D_MODEL,), dtype=jnp.float32)
        Wout = jax.random.normal(k2, (D_MODEL, D_MODEL), dtype=jnp.float32) * 0.02
        bout = jnp.zeros((D_MODEL,), dtype=jnp.float32)
        return {'x': x, 'Wqkv': Wqkv, 'bqkv': bqkv, 'Wout': Wout, 'bout': bout}
    _L0_attn_in = _L0_attn_setup()

    def _L0_ffn_setup():
        import jax, jax.numpy as jnp
        import numpy as np

        def _bitlinear(x, w_latent):
            scale = jax.lax.stop_gradient(jnp.clip(jnp.mean(jnp.abs(w_latent), axis=1, keepdims=True), 1e-05, None))
            tern = jnp.clip(jnp.round(w_latent / scale), -1.0, 1.0)
            w = w_latent + jax.lax.stop_gradient(tern - w_latent)
            return x @ (w * scale).T
        key = jax.random.key(seed)
        ks = jax.random.split(key, 6)
        dim, hidden, rank = (512, 2048, 16)
        B, S = (4, 2048)
        x = jax.random.normal(ks[0], (B, S, dim), dtype=jnp.float32)
        w_fc = 0.02 * jax.random.normal(ks[1], (hidden, dim), dtype=jnp.float32)
        w_proj = 0.02 * jax.random.normal(ks[2], (dim, hidden), dtype=jnp.float32)
        u = 0.02 * jax.random.normal(ks[3], (hidden, rank), dtype=jnp.float32)
        v = 0.02 * jax.random.normal(ks[4], (rank, dim), dtype=jnp.float32)
        fast_b = jax.random.normal(ks[5], (rank, rank), dtype=jnp.float32)
        gate = jnp.float32(0.05)
        return {'x': x, 'fast_b': fast_b, 'w_fc': w_fc, 'w_proj': w_proj, 'u': u, 'v': v, 'gate': gate}
    _L0_ffn_in = _L0_ffn_setup()
    _d = {'L0_attn_x': _L0_attn_in['x'], 'L0_attn_Wqkv': _L0_attn_in['Wqkv'], 'L0_attn_bqkv': _L0_attn_in['bqkv'], 'L0_attn_Wout': _L0_attn_in['Wout'], 'L0_attn_bout': _L0_attn_in['bout'], 'L0_ffn_fast_b': _L0_ffn_in['fast_b'], 'L0_ffn_w_fc': _L0_ffn_in['w_fc'], 'L0_ffn_w_proj': _L0_ffn_in['w_proj'], 'L0_ffn_u': _L0_ffn_in['u'], 'L0_ffn_v': _L0_ffn_in['v'], 'L0_ffn_gate': _L0_ffn_in['gate']}
    _x0 = _d['L0_attn_x']
    _d['L0_attn_x'] = jax.random.normal(jax.random.fold_in(jax.random.key(seed), 1), (1, 8192, 512), dtype=_x0.dtype)
    del _x0
    return _d

def reference(L0_attn_x, L0_attn_Wqkv, L0_attn_bqkv, L0_attn_Wout, L0_attn_bout, L0_ffn_fast_b, L0_ffn_w_fc, L0_ffn_w_proj, L0_ffn_u, L0_ffn_v, L0_ffn_gate):

    def _L0_attn_ref(x, Wqkv, bqkv, Wout, bout):
        import jax, jax.numpy as jnp
        import numpy as np
        D_MODEL = 512
        NHEAD = 16
        WIN = 128
        B, S, dm = x.shape
        H, W = (NHEAD, WIN)
        Dh = dm // H
        nb = S // W
        qkv = (x @ Wqkv + bqkv).reshape(B, S, 3, H, Dh)
        q = qkv[:, :, 0].transpose(0, 2, 1, 3)
        k = qkv[:, :, 1].transpose(0, 2, 1, 3)
        v = qkv[:, :, 2].transpose(0, 2, 1, 3)
        qb = q.reshape(B, H, nb, W, Dh)
        kb = k.reshape(B, H, nb, W, Dh)
        vb = v.reshape(B, H, nb, W, Dh)
        kp = jnp.pad(kb, ((0, 0), (0, 0), (1, 1), (0, 0), (0, 0)))
        vp = jnp.pad(vb, ((0, 0), (0, 0), (1, 1), (0, 0), (0, 0)))
        kwin = jnp.concatenate([kp[:, :, :-2], kp[:, :, 1:-1], kp[:, :, 2:]], axis=3)
        vwin = jnp.concatenate([vp[:, :, :-2], vp[:, :, 1:-1], vp[:, :, 2:]], axis=3)
        scale = jnp.float32(1.0 / np.sqrt(dm))
        scores = jnp.einsum('bhnqd,bhnkd->bhnqk', qb, kwin) * scale
        n = jnp.arange(nb)[:, None, None]
        i = jnp.arange(W)[None, :, None]
        j = jnp.arange(3 * W)[None, None, :]
        qpos = n * W + i
        kpos = n * W - W + j
        mask = (jnp.abs(kpos - qpos) <= W) & (kpos >= 0) & (kpos < S)
        scores = jnp.where(mask[None, None], scores, jnp.float32(-1e+30))
        attn = jax.nn.softmax(scores, axis=-1)
        out = jnp.einsum('bhnqk,bhnkd->bhnqd', attn, vwin)
        out = out.reshape(B, H, S, Dh).transpose(0, 2, 1, 3).reshape(B, S, dm)
        return out @ Wout + bout

    def _L0_ffn_ref(x, fast_b, w_fc, w_proj, u, v, gate):
        import jax, jax.numpy as jnp
        import numpy as np

        def _bitlinear(x, w_latent):
            scale = jax.lax.stop_gradient(jnp.clip(jnp.mean(jnp.abs(w_latent), axis=1, keepdims=True), 1e-05, None))
            tern = jnp.clip(jnp.round(w_latent / scale), -1.0, 1.0)
            w = w_latent + jax.lax.stop_gradient(tern - w_latent)
            return x @ (w * scale).T
        h = _bitlinear(x, w_fc) + gate * (x @ v.T @ fast_b.T @ u.T)
        r = jnp.maximum(h, 0.0)
        return _bitlinear(r * r, w_proj)
    x = L0_attn_x
    xn = _layernorm(x, axis=-1)
    x = x + _L0_attn_ref(xn, L0_attn_Wqkv, L0_attn_bqkv, L0_attn_Wout, L0_attn_bout) + _L0_ffn_ref(xn, L0_ffn_fast_b, L0_ffn_w_fc, L0_ffn_w_proj, L0_ffn_u, L0_ffn_v, L0_ffn_gate)
    return x

_drawn_inputs = setup_inputs


def setup_inputs(seed=0):
    import zlib

    import numpy as np

    out = dict(_drawn_inputs(seed))
    spreads = {'L0_attn_bqkv': (0.0, 0.8), 'L0_attn_bout': (0.0, 2.0)}
    factors = {'L0_attn_Wqkv': 30.347,
     'L0_ffn_fast_b': 8.0,
     'L0_ffn_u': 8.0,
     'L0_ffn_v': 8.0,
     'L0_attn_Wout': 6.109}
    for name, (base, spread) in spreads.items():
        noise = np.random.default_rng([zlib.crc32(name.encode()), seed]).standard_normal(out[name].shape)
        drawn = base * np.exp(spread * noise) if base else spread * noise
        out[name] = jnp.asarray(drawn.astype(out[name].dtype))
    for name, factor in factors.items():
        out[name] = (out[name] * factor).astype(out[name].dtype)
    return out
```

```python
from contextlib import ExitStack

import concourse.bass as bass
from concourse import mybir

F32 = mybir.dt.float32
F32R = mybir.dt.float32r
BF16 = mybir.dt.bfloat16
F16 = mybir.dt.float16
ALU = mybir.AluOpType
ACT = mybir.ActivationFunctionType
AX_X = mybir.AxisListType.X

P = 128
D = 512
DC = D // P
H = 16
DH = D // H
HC = P // DH
EPS = 1e-5
MIN_SCALE = 1e-5
NEG = -1e30
SCORE_SCALE = 1.0 / float(D) ** 0.5
ROUND = 1.5 * 2.0 ** 23
VW = 1 + 3 * DH


def wait(eng, sem, value):
    if isinstance(value, int) and value <= 0:
        return
    eng.wait_ge(sem, value)


def settle(eng, ticks):
    eng.sem_inc(ticks[eng.engine], 1)


def block_rows(dram, block):
    return dram[bass.ds(block * P, P), :]


def identity_on_pool(pool, nc, ident, zeroed, ready):
    nc.gpsimd.memset(ident[:, :], 0.0).then_inc(zeroed, 1)
    pool.wait_ge(zeroed, 1)
    nc.gpsimd.affine_select(out=ident[:, :], in_=ident[:, :], compare_op=ALU.not_equal, fill=1.0,
                            base=0, pattern=[[-1, P]], channel_multiplier=1).then_inc(ready, 1)


def inverse_std(pool, nc, stats, minus_half, ln_step, value):
    pool.wait_ge(ln_step, value)
    nc.gpsimd.tensor_tensor(stats[:, 2:3], stats[:, 1:2], minus_half[:, :], ALU.pow).then_inc(ln_step, 1)



def split_attention_weights(nc, Wqkv, bqkv, Wout, bout, wqkv_hi, wqkv_lo, wout_hi, wout_lo, qk_bias, out_bias):
    with ExitStack() as ctx:
        stage = ctx.enter_context(nc.sbuf_tensor("w_stage", [P, 2, 3 * D], F32))
        wout_raw = ctx.enter_context(nc.sbuf_tensor("wout_raw", [P, DC, D], F32))
        v_bias = ctx.enter_context(nc.sbuf_tensor("v_bias", [P, DC], F32))
        v_bias_wide = ctx.enter_context(nc.sbuf_tensor("v_bias_wide", [P, DC, P], F32))
        bout_wide = ctx.enter_context(nc.sbuf_tensor("bout_wide", [P, D], F32))
        bias_ps = ctx.enter_context(nc.psum_tensor("bias_ps", [P, D], F32))
        chunk_in = [ctx.enter_context(nc.semaphore(f"wqkv_chunk_in{b}")) for b in range(2)]
        wout_in = ctx.enter_context(nc.semaphore("wout_in"))
        biases_in = ctx.enter_context(nc.semaphore("biases_in"))
        hi_done = ctx.enter_context(nc.semaphore("w_hi_done"))
        lo_done = ctx.enter_context(nc.semaphore("w_lo_done"))
        wide_done = ctx.enter_context(nc.semaphore("v_bias_wide_done"))
        bias_summed = ctx.enter_context(nc.semaphore("bias_summed"))
        block = ctx.enter_context(nc.Block())

        @block.sync
        def _(sp):
            sp.dma_start(wout_raw[:, :, :], Wout.rearrange("(c p) n -> p c n", p=P)).then_inc(wout_in, 16)
            for k in range(DC):
                if k >= 2:
                    sp.wait_ge(lo_done, k - 1)
                sp.dma_start(stage[:, k % 2, :], Wqkv[k * P:(k + 1) * P, :]).then_inc(chunk_in[k % 2], 16)

        @block.gpsimd
        def _(pool):
            with nc.allow_non_contiguous_dma("a bias vector, once"):
                pool.dma_start(v_bias[:, :], bqkv[2 * D:3 * D].rearrange("(c p) -> p c", p=P)).then_inc(biases_in, 16)
                pool.dma_start(qk_bias[:, :], bqkv[0:2 * D].rearrange("(c p) -> p c", p=P)).then_inc(biases_in, 16)
            pool.dma_start(bout_wide[:, :], bout.partition_broadcast(P)).then_inc(biases_in, 16)

        @block.scalar
        def _(act):
            for k in range(DC):
                act.wait_ge(chunk_in[k % 2], 16 * (k // 2 + 1))
                nc.scalar.copy(wqkv_hi[:, k, :], stage[:, k % 2, :]).then_inc(hi_done, 1)
            act.wait_ge(wout_in, 16)
            nc.scalar.copy(wout_hi[:, :, :], wout_raw[:, :, :]).then_inc(hi_done, 1)

        @block.vector
        def _(dve):
            dve.wait_ge(biases_in, 48)
            nc.vector.tensor_copy(v_bias_wide[:, :, :], v_bias[:, :].unsqueeze(2).to_broadcast([P, DC, P])
                                  ).then_inc(wide_done, 1)
            for k in range(DC):
                dve.wait_ge(hi_done, k + 1)
                nc.vector.tensor_tensor(wqkv_lo[:, k, :], stage[:, k % 2, :], wqkv_hi[:, k, :].bitcast(F32),
                                        ALU.subtract).then_inc(lo_done, 1)
            dve.wait_ge(hi_done, DC + 1)
            nc.vector.tensor_tensor(wout_lo[:, :, :], wout_raw[:, :, :], wout_hi[:, :, :].bitcast(F32),
                                    ALU.subtract).then_inc(lo_done, 1)
            dve.wait_ge(bias_summed, 1)
            nc.vector.tensor_tensor(out_bias[:, :], bias_ps[:, :], bout_wide[:, :], ALU.add).then_inc(lo_done, 1)

        @block.tensor
        def _(pe):
            pe.wait_ge(wide_done, 1)
            pe.wait_ge(wout_in, 16)
            for k in range(DC):
                last = nc.tensor.matmul(bias_ps[:, :], v_bias_wide[:, k, :], wout_raw[:, k, :],
                                        start=(k == 0), stop=(k == DC - 1))
            last.then_inc(bias_summed, 1)


def attention(nc, x, Wqkv, bqkv, Wout, bout, partial):
    NBLK = x.shape[0] // P
    NT = NBLK // 2
    T = 2 * P
    UNIT = 2 * HC
    STEPS = DC * UNIT
    GROUPS = STEPS // HC

    ctx = ExitStack()
    with ctx:
        def sb(name, shape, dt):
            return ctx.enter_context(nc.sbuf_tensor(name, shape, dt))

        def sem(name):
            return ctx.enter_context(nc.semaphore(name))

        wqkv_hi = sb("wqkv_hi", [P, DC, 3 * D], F32R)
        wqkv_lo = sb("wqkv_lo", [P, DC, 3 * D], F32R)
        wout_hi = sb("wout_hi", [P, DC, D], F32R)
        wout_lo = sb("wout_lo", [P, DC, D], F32R)
        qk_bias = sb("qk_bias", [P, 2 * DC], F32)
        out_bias = sb("out_bias", [P, D], F32)
        split_attention_weights(nc, Wqkv, bqkv, Wout, bout, wqkv_hi, wqkv_lo, wout_hi, wout_lo, qk_bias, out_bias)

        ident = sb("ident", [P, P], F32)
        mask = sb("mask", [P, 3 * P], F32)
        x_in = sb("x_in", [P, 2, D], F32)
        xn = sb("xn", [P, 2, D], F32)
        bn = sb("bn", [P, 2, 6], F32)
        minus_half = sb("minus_half", [P, 1], F32)
        stats = sb("stats", [P, 2, 4], F32)
        xT_hi = sb("xT_hi", [P, DC, 3 * P], F32R)
        xT_lo = sb("xT_lo", [P, DC, 3 * P], F32R)
        qk_parts = sb("qk_parts", [P, 2, 4, T], F32R)
        stack = [sb(f"stack{c}", [3 * DH, HC, T + 4 * P], F32R) for c in range(DC)]
        values = sb("values", [P, 2, 4, H, VW], BF16)
        v_rest = sb("v_rest", [P, 2, D], F32)
        neg_scores = sb("neg_scores", [P, 2, 3 * P], F32)
        neg_max = sb("neg_max", [P, 4], F32)
        probs = sb("probs", [P, 2, 3 * P], F32)
        pT_hi = sb("pT_hi", [P, 4, 3 * P], F16)
        pT_lo = sb("pT_lo", [P, 4, 3 * P], F16)
        o_sum = sb("o_sum", [P, 2, P], F32)
        o_rcp = sb("o_rcp", [P, 2, HC], F32)
        o_heads = sb("o_heads", [P, 2, 2, P], F32)
        oT_hi = sb("oT_hi", [P, DC, T], F32R)
        oT_lo = sb("oT_lo", [P, DC, T], F32R)
        x_res = sb("x_res", [P, 2, D], F32)
        y = sb("y", [P, 2, D], F32)

        job_ps = ctx.enter_context(nc.psum_tensor("job_ps", [P, 2, D], F32))
        score_ps = ctx.enter_context(nc.psum_tensor("score_ps", [P, 2, D], F32))
        pT_ps = ctx.enter_context(nc.psum_tensor("pT_ps", [P, 2, D], F32))
        o_ps = ctx.enter_context(nc.psum_tensor("o_ps", [P, 2, D], F32))

        def q_cols(c, h, b):
            return stack[c][:, h, b * P:(b + 1) * P]

        def k_cols(c, h, s0, s1):
            return stack[c][:, h, T + s0 * P:T + s1 * P]

        def pe_project_qk(bank, c, part):
            is_k, half = divmod(part, 2)
            col = is_k * D + c * P
            out = job_ps[:, bank, is_k * T:(is_k + 1) * T]
            tokens = slice(is_k * P, is_k * P + T)
            for n in range(half * 6, half * 6 + 6):
                k, pass_ = divmod(n, 3)
                w = wqkv_lo if pass_ == 2 else wqkv_hi
                a = xT_lo if pass_ == 1 else xT_hi
                last = nc.tensor.matmul(out, w[:, k, col:col + P], a[:, k, tokens],
                                        start=(n == 0), stop=(n == 3 * DC - 1))
            return last

        def pe_project_v(bank, slot, part):
            for n in range(part * 3, part * 3 + 3):
                k, pass_ = divmod(n, 3)
                w = wqkv_lo if pass_ == 2 else wqkv_hi
                a = xT_lo if pass_ == 1 else xT_hi
                last = nc.tensor.matmul(job_ps[:, bank, :], a[:, k, slot * P:(slot + 1) * P], w[:, k, 2 * D:3 * D],
                                        start=(n == 0), stop=(n == 3 * DC - 1))
            return last

        def pe_transpose_x(bank, r):
            for k in range(DC):
                last = nc.tensor.transpose(job_ps[:, bank, k * P:(k + 1) * P], xn[:, r, k * P:(k + 1) * P], ident[:, :])
            return last

        def four(bank):
            return job_ps[:, bank, :].rearrange("p (c t) -> p c t", c=DC)

        def head_columns(ap, first):
            return ap[:, :, first:first + DH]

        with ExitStack() as pro:
            def psem(name):
                return pro.enter_context(nc.semaphore(name))

            zeroed, ident_done = psem("ident_zeroed"), psem("ident_done")
            mask_set, ones_set = psem("mask_set"), psem("ones_set")
            x_here = [psem(f"pro_x_here{r}") for r in range(2)]
            ln_step, xn_done, job_filled = psem("pro_ln_step"), psem("pro_xn_done"), psem("pro_job_filled")
            hi_done, job_freed, v2_done, v_done = psem("pro_hi"), psem("pro_job_freed"), psem("pro_v2"), psem("pro_v_done")
            k0_stacked = psem("k0_stacked")
            block = pro.enter_context(nc.Block())
            K0 = [(qk_parts[:, 0, c // 2, (c % 2) * P:(c % 2 + 1) * P],
                   qk_parts[:, 0, 2 + c // 2, (c % 2) * P:(c % 2 + 1) * P]) for c in range(DC)]

            @block.sync
            def _(sp):
                for b in range(3):
                    if b == 2:
                        sp.wait_ge(xn_done, 1)
                    sp.dma_start(x_in[:, b % 2, :], block_rows(x, b)).then_inc(x_here[b % 2], 16)
                sp.wait_ge(job_freed, 4)
                for c in range(DC):
                    for h in range(HC):
                        rows = slice(h * DH, (h + 1) * DH)
                        for r, part in enumerate((0, 0, 1)):
                            sp.dma_start(k_cols(c, h, 1, 2)[r * DH:(r + 1) * DH, :].bitcast(F32),
                                         K0[c][part][rows, :].bitcast(F32)).then_inc(k0_stacked, 16)
                sp.wait_ge(k0_stacked, 16 * 3 * H)

            @block.gpsimd
            def _(pool):
                identity_on_pool(pool, nc, ident, zeroed, ident_done)
                nc.gpsimd.memset(minus_half[:, :], -0.5).then_inc(mask_set, 1)
                nc.gpsimd.memset(mask[:, :], 0.0).then_inc(mask_set, 1)
                nc.gpsimd.memset(values[:, :, :, :, 0:1], 1.0).then_inc(ones_set, 1)
                pool.wait_ge(mask_set, 2)
                nc.gpsimd.affine_select(out=mask[:, 0:P], in_=mask[:, 0:P], compare_op=ALU.is_ge, fill=NEG,
                                        base=0, pattern=[[1, P]], channel_multiplier=-1).then_inc(mask_set, 1)
                nc.gpsimd.affine_select(out=mask[:, 2 * P:3 * P], in_=mask[:, 2 * P:3 * P], compare_op=ALU.is_ge,
                                        fill=NEG, base=0, pattern=[[-1, P]], channel_multiplier=1).then_inc(mask_set, 1)
                for b in range(3):
                    inverse_std(pool, nc, stats[:, b % 2, :], minus_half, ln_step, 5 * b + 3)
                pool.wait_ge(job_freed, 5)
                slot = values[:, 0, 1, :, :]
                rest = v_rest[:, 0, :].rearrange("p (h d) -> p h d", h=H)
                nc.gpsimd.tensor_copy(head_columns(slot, 1 + DH), rest).then_inc(v2_done, 1)
                pool.wait_ge(v2_done, 1)
                nc.gpsimd.tensor_tensor(head_columns(slot, 1 + 2 * DH), rest, head_columns(slot, 1 + DH),
                                        ALU.subtract).then_inc(v_done, 1)

            @block.scalar
            def _(act):
                for b in range(3):
                    act.wait_ge(ln_step, 5 * b + 5)
                    if b == 2:
                        act.wait_ge(job_filled, 1)
                    nc.scalar.activation(xn[:, b % 2, :], x_in[:, b % 2, :], ACT.Identity,
                                         bias=stats[:, b % 2, 3:4], scale=stats[:, b % 2, 2:3]).then_inc(xn_done, 1)
                    act.wait_ge(job_filled, b + 1)
                    nc.scalar.copy(xT_hi[:, :, b * P:(b + 1) * P], four(b % 2)).then_inc(hi_done, 1)
                act.wait_ge(job_filled, 4)
                for c in range(DC):
                    nc.scalar.activation(K0[c][0], job_ps[:, 1, c * P:(c + 1) * P], ACT.Identity,
                                         bias=qk_bias[:, DC + c:DC + c + 1], scale=1.0).then_inc(hi_done, 1)
                act.wait_ge(job_filled, 5)
                act.wait_ge(ones_set, 1)
                nc.scalar.copy(head_columns(values[:, 0, 1, :, :], 1),
                               job_ps[:, 0, :].rearrange("p (h d) -> p h d", h=H)).then_inc(hi_done, 1)

            @block.vector
            def _(dve):
                for b in range(3):
                    r = b % 2
                    dve.wait_ge(x_here[r], 16 * (b // 2 + 1))
                    if b == 2:
                        dve.wait_ge(xn_done, 1)
                    nc.vector.bn_stats(bn[:, r, :], x_in[:, r, :]).then_inc(ln_step, 1)
                    dve.wait_ge(ln_step, 5 * b + 1)
                    nc.vector.bn_aggr(stats[:, r, 0:2], bn[:, r, :]).then_inc(ln_step, 1)
                    dve.wait_ge(ln_step, 5 * b + 2)
                    nc.vector.tensor_scalar(stats[:, r, 1:2], stats[:, r, 1:2], EPS, None, ALU.add
                                            ).then_inc(ln_step, 1)
                    dve.wait_ge(ln_step, 5 * b + 4)
                    nc.vector.scalar_tensor_tensor(stats[:, r, 3:4], stats[:, r, 0:1], -1.0, stats[:, r, 2:3],
                                                   ALU.mult, ALU.mult).then_inc(ln_step, 1)
                    dve.wait_ge(hi_done, b + 1)
                    nc.vector.tensor_tensor(xT_lo[:, :, b * P:(b + 1) * P], four(r),
                                            xT_hi[:, :, b * P:(b + 1) * P].bitcast(F32), ALU.subtract
                                            ).then_inc(job_freed, 1)
                dve.wait_ge(hi_done, 3 + DC)
                for c in range(DC):
                    last = nc.vector.scalar_tensor_tensor(K0[c][1], job_ps[:, 1, c * P:(c + 1) * P],
                                                          qk_bias[:, DC + c:DC + c + 1], K0[c][0].bitcast(F32),
                                                          ALU.add, ALU.subtract)
                last.then_inc(job_freed, 1)
                dve.wait_ge(hi_done, 4 + DC)
                nc.vector.tensor_tensor(v_rest[:, 0, :].rearrange("p (h d) -> p h d", h=H),
                                        job_ps[:, 0, :].rearrange("p (h d) -> p h d", h=H),
                                        head_columns(values[:, 0, 1, :, :], 1), ALU.subtract).then_inc(job_freed, 1)

            @block.tensor
            def _(pe):
                pe.wait_ge(ident_done, 1)
                for b in range(3):
                    pe.wait_ge(xn_done, b + 1)
                    if b == 2:
                        pe.wait_ge(job_freed, 1)
                    pe_transpose_x(b % 2, b % 2).then_inc(job_filled, 1)
                pe.wait_ge(job_freed, 2)
                for c in range(DC):
                    for n in range(3 * DC):
                        k, pass_ = divmod(n, 3)
                        w = wqkv_lo if pass_ == 2 else wqkv_hi
                        a = xT_lo if pass_ == 1 else xT_hi
                        last = nc.tensor.matmul(job_ps[:, 1, c * P:(c + 1) * P], w[:, k, D + c * P:D + (c + 1) * P],
                                                a[:, k, 0:P], start=(n == 0), stop=(n == 3 * DC - 1))
                last.then_inc(job_filled, 1)
                pe.wait_ge(job_freed, 3)
                for part in range(4):
                    last = pe_project_v(0, 0, part)
                last.then_inc(job_filled, 1)

        FULL = [("qk", 1), ("oT", 3), ("out", 0), ("qk", 2), ("out", 1), ("oT", 0), ("qk", 3), ("x", 0),
                ("x", 1), ("oT", 1), ("qk", 0), ("v", 0), ("oT", 2), ("v", 1)]
        HEAD = [("qk", 0), ("v", 0), ("v", 1)]
        FIRST = [j for j in FULL if j not in (("oT", 3), ("out", 0), ("out", 1))]
        LAST = [j for j in FULL if j not in (("x", 0), ("x", 1), ("qk", 0), ("v", 0), ("v", 1))]
        TAIL = [("oT", 3), ("out", 0), ("out", 1)]
        PARTS = {0: [("qk", 1, 0)], 1: [("qk", 1, 1)], 2: [("qk", 1, 2)], 3: [("qk", 1, 3)],
                 5: [("oT", 3, 0)], 6: [("out", 0, 0), ("out", 0, 1)], 7: [("out", 0, 2), ("out", 0, 3)],
                 8: [("qk", 2, 0)], 9: [("qk", 2, 1)], 10: [("qk", 2, 2)], 11: [("qk", 2, 3)],
                 12: [("out", 1, 0)], 13: [("out", 1, 1)], 14: [("out", 1, 2)], 15: [("out", 1, 3)],
                 16: [("oT", 0, 0), ("qk", 3, 0)], 17: [("qk", 3, 1)], 18: [("qk", 3, 2)], 19: [("qk", 3, 3)],
                 20: [("x", 0, 0)], 22: [("x", 1, 0)], 23: [("oT", 1, 0)],
                 24: [("qk", 0, 0)], 25: [("qk", 0, 1)], 26: [("qk", 0, 2)], 27: [("qk", 0, 3)],
                 28: [("v", 0, 0), ("v", 0, 1)], 29: [("v", 0, 2), ("v", 0, 3)],
                 30: [("oT", 2, 0), ("v", 1, 0), ("v", 1, 1)], 31: [("v", 1, 2), ("v", 1, 3)]}
        TURN, LOW, PV, FOLD = 1, 2, 3, 4
        LN_STEPS = [9, 10, 11, 15]
        LAST_PART = {"qk": 3, "out": 3, "v": 3, "oT": 0, "x": 0}

        def kind_of(i):
            if isinstance(i, int):
                return FIRST if i == 0 else LAST if i == NT - 1 else FULL
            return FULL

        def job_number(i, job):
            if isinstance(i, int) and i == 0:
                return len(HEAD) + FIRST.index(job)
            return i * len(FULL) + kind_of(i).index(job)

        def late_job_number(i, job):
            return i * len(FULL) + FULL.index(job)

        def split_number(i, job):
            two_part = [j for j in kind_of(i) if j[0] != "out"]
            per_tile = len([j for j in FULL if j[0] != "out"])
            if isinstance(i, int) and i == 0:
                return len(HEAD) + two_part.index(job)
            return i * per_tile + len(FULL) - per_tile + two_part.index(job)

        def bank_of(parity, i, job):
            if isinstance(i, int) and i == 0:
                return (len(HEAD) + FIRST.index(job)) % 2
            return kind_of(i).index(job) % 2

        def tail_number(job):
            return (NT - 1) * len(FULL) + len(LAST) + TAIL.index(job)

        def tail_split_number(job):
            per_tile = len([j for j in FULL if j[0] != "out"])
            return (NT - 1) * per_tile + len(FULL) - per_tile + len([j for j in LAST if j[0] != "out"])

        ticks = {e: sem(f"ticks_{n}") for n, e in (("dve", nc.vector.engine), ("pool", nc.gpsimd.engine),
                                                   ("sp", nc.sync.engine))}
        x_here = [sem(f"x_here{r}") for r in range(2)]
        ln_step = [sem(f"ln_step{r}") for r in range(2)]
        xn_done = sem("xn_done")
        xT_carried = sem("xT_carried")
        job_filled = sem("job_filled")
        hi_done = sem("job_hi_done")
        job_freed = sem("job_freed")
        stacked = [[sem(f"stacked{h}_{r}") for r in range(2)] for h in range(HC)]
        k_carried = sem("k_carried")
        v2_done = sem("v2_done")
        v_done = sem("v_done")
        v_carried = sem("v_carried")
        scores_done = sem("scores_done")
        neg_done = sem("neg_scores_done")
        probs_done = sem("probs_done")
        pT_done = sem("probs_transposed")
        pT_hi_done = sem("pT_hi_done")
        pT_lo_done = sem("pT_lo_done")
        pv_done = sem("pv_done")
        o_summed = sem("o_summed")
        o_done = sem("o_heads_done")
        res_here = [sem(f"x_res_here{b}") for b in range(2)]
        y_done = sem("y_done")
        y_stored = [sem(f"y_stored{b}") for b in range(2)]
        block = ctx.enter_context(nc.Block())

        def window(i, s):
            b = (s % UNIT) // HC
            first = 1 if isinstance(i, int) and i == 0 and b == 0 else b
            last = 3 if isinstance(i, int) and i == NT - 1 and b == 1 else b + 3
            return first, last

        def where(s):
            return s // UNIT, (s % UNIT) // HC, s % HC

        def back(i, s, n):
            return (i, s - n) if s >= n else (i - 1, s - n + STEPS)

        def exists(i):
            return not (isinstance(i, int) and i < 0)

        def parity_back(par, s, n):
            return par if s >= n else 1 - par

        def tiles(eng, tile):
            tile(0, 0)
            with eng.Fori(0, (NT - 2) // 2) as pair:
                for u in range(2):
                    tile(2 * pair + 1 + u, (1 + u) % 2)
            tile(NT - 1, (NT - 1) % 2)

        assert NT % 2 == 0 and len(FULL) % 2 == 0 and len(HEAD) + len(FIRST) == len(FULL)

        @block.sync
        def _(sp):
            def stack_qk(i, c):
                r = c % 2
                settle(sp, ticks)
                wait(sp, k_carried, DC * (i - 1) + c + 1)
                settle(sp, ticks)
                for h in range(HC):
                    rows = slice(h * DH, (h + 1) * DH)
                    ready = stacked[h][r]
                    q_k = stack[c][:, h, :].bitcast(F32).rearrange("p (n t) -> p n t", t=T)
                    parts = qk_parts[rows, r, :, :].bitcast(F32)
                    for row, pair in enumerate((slice(0, 3, 2), slice(1, 3), slice(0, 4, 3))):
                        sp.dma_start(q_k[row * DH:(row + 1) * DH, 0:3:2, :], parts[:, pair, :]).then_inc(ready, 16)

            for b in range(2):
                sp.sem_inc(y_stored[b], 16)
            wait(sp, job_freed, 1)
            stack_qk(0, 0)

            def tile(i, par):
                first = isinstance(i, int) and i == 0
                last = isinstance(i, int) and i == NT - 1
                if not last:
                    for r in range(2):
                        if not first:
                            sp.wait_ge(xn_done, 2 * i - 1 + r)
                            settle(sp, ticks)
                        src = (2 * i + 3 + r) % NBLK
                        sp.dma_start(x_in[:, r, :], block_rows(x, src)).then_inc(x_here[r], 16)
                if not first:
                    for b in range(2):
                        sp.wait_ge(y_stored[b], 16 * i)
                        settle(sp, ticks)
                        sp.dma_start(x_res[:, b, :], block_rows(x, 2 * (i - 1) + b)).then_inc(res_here[b], 16)
                sp.wait_ge(job_freed, job_number(i, ("qk", 1)) + 1)
                stack_qk(i, 1)
                if not first:
                    sp.wait_ge(y_done, 2 * (i - 1) + 1)
                    settle(sp, ticks)
                    sp.dma_start(block_rows(partial, 2 * (i - 1)), y[:, 0, :]).then_inc(y_stored[0], 16)
                sp.wait_ge(job_freed, job_number(i, ("qk", 2)) + 1)
                stack_qk(i, 2)
                if not first:
                    sp.wait_ge(y_done, 2 * (i - 1) + 2)
                    settle(sp, ticks)
                    sp.dma_start(block_rows(partial, 2 * (i - 1) + 1), y[:, 1, :]).then_inc(y_stored[1], 16)
                sp.wait_ge(job_freed, job_number(i, ("qk", 3)) + 1)
                stack_qk(i, 3)
                if not last:
                    sp.wait_ge(job_freed, job_number(i, ("qk", 0)) + 1)
                    stack_qk(i + 1, 0)

            tiles(sp, tile)
            for b in range(2):
                sp.wait_ge(y_stored[b], 16 * NT)
                sp.dma_start(x_res[:, b, :], block_rows(x, 2 * (NT - 1) + b)).then_inc(res_here[b], 16)
            for b in range(2):
                sp.wait_ge(y_done, 2 * (NT - 1) + b + 1)
                sp.dma_start(block_rows(partial, 2 * (NT - 1) + b), y[:, b, :]).then_inc(y_stored[b], 16)
            for b in range(2):
                sp.wait_ge(y_stored[b], 16 * (NT + 1))

        @block.gpsimd
        def _(pool):
            def carry_keys(i, c):
                pool.wait_ge(scores_done, STEPS * i + UNIT * (c + 1))
                settle(pool, ticks)
                nc.gpsimd.tensor_copy(stack[c][:, :, T:T + 2 * P],
                                      stack[c][:, :, T + 2 * P:T + 4 * P].bitcast(F32)).then_inc(k_carried, 1)

            def finish_values(parity, r, number, count):
                slot = values[:, parity, 2 + r, :, :]
                rest = v_rest[:, r, :].rearrange("p (h d) -> p h d", h=H)
                pool.wait_ge(job_freed, number + 1)
                settle(pool, ticks)
                nc.gpsimd.tensor_copy(head_columns(slot, 1 + DH), rest).then_inc(v2_done, 1)
                pool.wait_ge(v2_done, count + 1)
                nc.gpsimd.tensor_tensor(head_columns(slot, 1 + 2 * DH), rest, head_columns(slot, 1 + DH),
                                        ALU.subtract).then_inc(v_done, 1)

            def normalise(i, g):
                c, b = g // 2, g % 2
                pool.wait_ge(o_summed, GROUPS * i + g + 1)
                if c >= 2:
                    pool.wait_ge(job_filled, job_number(i, ("oT", c - 2)) + 1)
                elif not (isinstance(i, int) and i == 0):
                    pool.wait_ge(job_filled, (late_job_number(i - 1, ("oT", 2)) if c == 0 else
                                              job_number(i, ("oT", 3))) + 1)
                nc.gpsimd.tensor_tensor(o_heads[:, c % 2, b, :].rearrange("p (h d) -> p h d", h=HC),
                                        o_sum[:, g % 2, :].rearrange("p (h d) -> p h d", h=HC),
                                        o_rcp[:, g % 2, :].unsqueeze(2).to_broadcast([P, HC, DH]), ALU.mult
                                        ).then_inc(o_done, 1)

            finish_values(0, 0, 1, 0)
            finish_values(0, 1, 2, 1)

            def tile(i, par):
                first = isinstance(i, int) and i == 0
                last = isinstance(i, int) and i == NT - 1

                def add_x(b):
                    pool.wait_ge(job_freed, job_number(i, ("out", b)) + 1)
                    pool.wait_ge(res_here[b], 16 * i)
                    nc.gpsimd.tensor_tensor(y[:, b, :], y[:, b, :], x_res[:, b, :], ALU.add).then_inc(y_done, 1)

                if not first:
                    normalise(i - 1, GROUPS - 1)
                normalise(i, 0)
                if not first:
                    add_x(0)
                if not last:
                    carry_keys(i, 0)
                normalise(i, 1)
                if not last:
                    for r in range(2):
                        inverse_std(pool, nc, stats[:, r, :], minus_half, ln_step[r], 5 * i + 3)
                normalise(i, 2)
                if not first:
                    add_x(1)
                if not last:
                    carry_keys(i, 1)
                normalise(i, 3)
                if not last:
                    pool.wait_ge(job_filled, job_number(i, ("qk", 3)) + 1)
                    settle(pool, ticks)
                    nc.gpsimd.tensor_copy(xT_hi[:, :, 0:P], xT_hi[:, :, 2 * P:3 * P].bitcast(F32)).then_inc(xT_carried, 1)
                    nc.gpsimd.tensor_copy(xT_lo[:, :, 0:P], xT_lo[:, :, 2 * P:3 * P].bitcast(F32)).then_inc(xT_carried, 1)
                normalise(i, 4)
                if not last:
                    carry_keys(i, 2)
                normalise(i, 5)
                if not last:
                    finish_values(1 - par, 0, job_number(i, ("v", 0)), 2 * i + 2)
                    finish_values(1 - par, 1, job_number(i, ("v", 1)), 2 * i + 3)
                normalise(i, 6)
                if not last:
                    carry_keys(i, 3)

            tiles(pool, tile)
            normalise(NT - 1, GROUPS - 1)
            for b in range(2):
                pool.wait_ge(job_freed, tail_number(("out", b)) + 1)
                pool.wait_ge(res_here[b], 16 * NT)
                nc.gpsimd.tensor_tensor(y[:, b, :], y[:, b, :], x_res[:, b, :], ALU.add).then_inc(y_done, 1)

        @block.scalar
        def _(act):
            def split_hi(number, bank, out, in_):
                act.wait_ge(job_filled, number + 1)
                nc.scalar.copy(out, in_).then_inc(hi_done, 1)

            def qk_hi(i, c, number, bank):
                r = c % 2
                act.wait_ge(job_filled, number + 1)
                for h in range(HC):
                    wait(act, stacked[h][r], 48 * (2 * i + c // 2))
                nc.scalar.activation(qk_parts[:, r, 0, :], job_ps[:, bank, 0:T], ACT.Identity,
                                     bias=qk_bias[:, c:c + 1], scale=1.0)
                nc.scalar.activation(qk_parts[:, r, 2, :], job_ps[:, bank, T:2 * T], ACT.Identity,
                                     bias=qk_bias[:, DC + c:DC + c + 1], scale=1.0).then_inc(hi_done, 1)

            def v1(i, parity, r, number, bank):
                act.wait_ge(job_filled, number + 1)
                wait(act, pv_done, STEPS * (i - 1))
                nc.scalar.copy(head_columns(values[:, parity, 2 + r, :, :], 1),
                               job_ps[:, bank, :].rearrange("p (h d) -> p h d", h=H)).then_inc(hi_done, 1)

            def exp(i, s):
                _, b, _ = where(s)
                w0, w1 = window(i, s)
                n, r = STEPS * i + s, s % 2
                cols = slice((w0 - b) * P, (w1 - b) * P)
                act.wait_ge(neg_done, n + 1)
                wait(act, pT_done, n - 1)
                nc.scalar.activation(probs[:, r, cols], neg_scores[:, r, cols], ACT.Exp,
                                     bias=neg_max[:, s % 4:s % 4 + 1], scale=-1.0).then_inc(probs_done, 1)

            def pT_high(i, s):
                _, b, _ = where(s)
                w0, w1 = window(i, s)
                n, r = STEPS * i + s, s % 2
                cols = slice((w0 - b) * P, (w1 - b) * P)
                act.wait_ge(pT_done, n + 1)
                wait(act, pv_done, n - 3)
                nc.scalar.copy(pT_hi[:, s % 4, cols], pT_ps[:, r, cols]).then_inc(pT_hi_done, 1)

            def job(i, par, j):
                kind, a = j
                number, bank = job_number(i, j), bank_of(par, i, j)
                if kind == "qk":
                    qk_hi(i + 1 if a == 0 else i, a, number, bank)
                elif kind == "v":
                    v1(i + 1, 1 - par, a, number, bank)
                elif kind == "oT":
                    split_hi(number, bank, oT_hi[:, a, :], job_ps[:, bank, 0:T])
                elif kind == "x":
                    act.wait_ge(job_filled, number + 1)
                    if a == 1:
                        act.wait_ge(xT_carried, 2 * i + 2)
                    nc.scalar.copy(xT_hi[:, :, (1 + a) * P:(2 + a) * P], four(bank)).then_inc(hi_done, 1)

            def normalise_x(i, r):
                act.wait_ge(ln_step[r], 5 * i + 5)
                if not (isinstance(i, int) and i == 0):
                    act.wait_ge(job_filled, late_job_number(i - 1, ("x", r)) + 1)
                nc.scalar.activation(xn[:, r, :], x_in[:, r, :], ACT.Identity,
                                     bias=stats[:, r, 3:4], scale=stats[:, r, 2:3]).then_inc(xn_done, 1)

            qk_hi(0, 0, 0, 0)
            v1(0, 0, 0, 1, 1)
            v1(0, 0, 1, 2, 0)

            def tile(i, par):
                for s in range(STEPS):
                    exp(i, s)
                    pi, ps = back(i, s, TURN)
                    if exists(pi):
                        pT_high(pi, ps)
                    for kind, a, part in PARTS.get(s, ()):
                        if part == LAST_PART[kind] and kind != "out" and (kind, a) in kind_of(i):
                            job(i, par, (kind, a))
                    if ("x", 0) in kind_of(i) and s in (16, 18):
                        normalise_x(i, (s - 16) // 2)

            tiles(act, tile)
            pT_high(NT - 1, STEPS - 1)
            act.wait_ge(job_filled, tail_number(("oT", 3)) + 1)
            nc.scalar.copy(oT_hi[:, 3, :], job_ps[:, len(LAST) % 2, 0:T]).then_inc(hi_done, 1)

        @block.vector
        def _(dve):
            def mask_scale_max(i, s):
                _, b, _ = where(s)
                w0, w1 = window(i, s)
                n, r = STEPS * i + s, s % 2
                cols = slice((w0 - b) * P, (w1 - b) * P)
                dve.wait_ge(scores_done, n + 1)
                wait(dve, probs_done, n - 1)
                settle(dve, ticks)
                nc.vector.tensor_tensor_reduce(out=neg_scores[:, r, cols], in0=score_ps[:, r, cols],
                                               in1=mask[:, cols], scale=-SCORE_SCALE, scalar=3e38, op0=ALU.add,
                                               op1=ALU.min, accum_out=neg_max[:, s % 4:s % 4 + 1]).then_inc(neg_done, 1)

            def pT_low(i, s):
                _, b, _ = where(s)
                w0, w1 = window(i, s)
                n, r = STEPS * i + s, s % 2
                cols = slice((w0 - b) * P, (w1 - b) * P)
                dve.wait_ge(pT_hi_done, n + 1)
                nc.vector.tensor_tensor(pT_lo[:, s % 4, cols], pT_ps[:, r, cols], pT_hi[:, s % 4, cols], ALU.subtract
                                        ).then_inc(pT_lo_done, 1)

            def fold(i, g):
                n, r = GROUPS * i + g, g % 2
                cols = o_ps[:, r, 0:HC * VW].rearrange("p (h w) -> p h w", h=HC)
                dve.wait_ge(pv_done, HC * (n + 1))
                wait(dve, o_done, n - 1)
                nc.vector.reciprocal(o_rcp[:, r, :].unsqueeze(2), cols[:, :, 0:1])
                nc.vector.tensor_reduce(o_sum[:, r, :].rearrange("p (h d) -> p h d", h=HC),
                                        cols[:, :, 1:VW].rearrange("p h (k d) -> p h d k", k=3),
                                        AX_X, ALU.add).then_inc(o_summed, 1)

            def qk_lo(c, hi_number, bank):
                r = c % 2
                dve.wait_ge(hi_done, hi_number + 1)
                nc.vector.scalar_tensor_tensor(qk_parts[:, r, 1, :], job_ps[:, bank, 0:T], qk_bias[:, c:c + 1],
                                               qk_parts[:, r, 0, :].bitcast(F32), ALU.add, ALU.subtract)
                nc.vector.scalar_tensor_tensor(qk_parts[:, r, 3, :], job_ps[:, bank, T:2 * T],
                                               qk_bias[:, DC + c:DC + c + 1], qk_parts[:, r, 2, :].bitcast(F32),
                                               ALU.add, ALU.subtract).then_inc(job_freed, 1)

            def v_remainder(parity, r, hi_number, bank, count):
                dve.wait_ge(hi_done, hi_number + 1)
                wait(dve, v_done, count - 1)
                nc.vector.tensor_tensor(v_rest[:, r, :].rearrange("p (h d) -> p h d", h=H),
                                        job_ps[:, bank, :].rearrange("p (h d) -> p h d", h=H),
                                        head_columns(values[:, parity, 2 + r, :, :], 1), ALU.subtract
                                        ).then_inc(job_freed, 1)

            def job(i, par, j):
                kind, a = j
                bank = bank_of(par, i, j)
                if kind == "qk":
                    qk_lo(a, split_number(i, j), bank)
                elif kind == "v":
                    v_remainder(1 - par, a, split_number(i, j), bank, 2 * i + 2 + a)
                elif kind == "oT":
                    dve.wait_ge(hi_done, split_number(i, j) + 1)
                    nc.vector.tensor_tensor(oT_lo[:, a, :], job_ps[:, bank, 0:T], oT_hi[:, a, :].bitcast(F32),
                                            ALU.subtract).then_inc(job_freed, 1)
                elif kind == "x":
                    dve.wait_ge(hi_done, split_number(i, j) + 1)
                    cols = slice((1 + a) * P, (2 + a) * P)
                    nc.vector.tensor_tensor(xT_lo[:, :, cols], four(bank), xT_hi[:, :, cols].bitcast(F32),
                                            ALU.subtract).then_inc(job_freed, 1)
                elif kind == "out":
                    dve.wait_ge(job_filled, job_number(i, j) + 1)
                    dve.wait_ge(y_stored[a], 16 * i)
                    nc.vector.tensor_tensor(y[:, a, :], job_ps[:, bank, :], out_bias[:, :], ALU.add
                                            ).then_inc(job_freed, 1)

            def layernorm(i, r, stage):
                if stage == 0:
                    dve.wait_ge(x_here[r], 16 * (i + 1))
                    nc.vector.bn_stats(bn[:, r, :], x_in[:, r, :]).then_inc(ln_step[r], 1)
                    return
                dve.wait_ge(ln_step[r], 5 * i + (stage if stage < 3 else 4))
                if stage == 1:
                    settle(dve, ticks)
                    nc.vector.bn_aggr(stats[:, r, 0:2], bn[:, r, :]).then_inc(ln_step[r], 1)
                elif stage == 2:
                    nc.vector.tensor_scalar(stats[:, r, 1:2], stats[:, r, 1:2], EPS, None, ALU.add
                                            ).then_inc(ln_step[r], 1)
                else:
                    nc.vector.scalar_tensor_tensor(stats[:, r, 3:4], stats[:, r, 0:1], -1.0, stats[:, r, 2:3],
                                                   ALU.mult, ALU.mult).then_inc(ln_step[r], 1)

            qk_lo(0, 0, 0)
            v_remainder(0, 0, 1, 1, 0)
            v_remainder(0, 1, 2, 0, 1)

            def tile(i, par):
                for s in range(STEPS):
                    mask_scale_max(i, s)
                    pi, ps = back(i, s, LOW)
                    if exists(pi):
                        pT_low(pi, ps)
                    gi, gs = back(i, s, FOLD)
                    if exists(gi) and gs % HC == HC - 1:
                        fold(gi, gs // HC)
                    if ("x", 0) in kind_of(i) and s in LN_STEPS:
                        for r in range(2):
                            layernorm(i, r, LN_STEPS.index(s))
                    if ("v", 0) in kind_of(i) and s == 7:
                        dve.wait_ge(v_done, 2 * i + 2)
                        wait(dve, pv_done, STEPS * i)
                        nc.vector.tensor_copy(values[:, 1 - par, 0:2, :, :], values[:, par, 2:4, :, :]
                                              ).then_inc(v_carried, 1)
                    for kind, a, part in PARTS.get(s, ()):
                        if part == LAST_PART[kind] and (kind, a) in kind_of(i):
                            job(i, par, (kind, a))

            tiles(dve, tile)
            for s in range(STEPS - LOW, STEPS):
                pT_low(NT - 1, s)
            fold(NT - 1, GROUPS - 1)
            dve.wait_ge(hi_done, tail_split_number(("oT", 3)) + 1)
            nc.vector.tensor_tensor(oT_lo[:, 3, :], job_ps[:, len(LAST) % 2, 0:T], oT_hi[:, 3, :].bitcast(F32),
                                    ALU.subtract).then_inc(job_freed, 1)
            for b in range(2):
                dve.wait_ge(job_filled, tail_number(("out", b)) + 1)
                dve.wait_ge(y_stored[b], 16 * NT)
                nc.vector.tensor_tensor(y[:, b, :], job_ps[:, (len(LAST) + 1 + b) % 2, :], out_bias[:, :], ALU.add
                                        ).then_inc(job_freed, 1)

        @block.tensor
        def _(pe):
            def scores(i, s):
                c, b, h = where(s)
                w0, w1 = window(i, s)
                n = STEPS * i + s
                if b == 0:
                    pe.wait_ge(stacked[h][c % 2], 48 * (2 * i + c // 2 + 1))
                wait(pe, neg_done, n - 1)
                nc.tensor.matmul(score_ps[:, s % 2, (w0 - b) * P:(w1 - b) * P], q_cols(c, h, b), k_cols(c, h, w0, w1),
                                 start=True, stop=True).then_inc(scores_done, 1)

            def transpose_probs(i, s):
                _, b, _ = where(s)
                w0, w1 = window(i, s)
                n, r = STEPS * i + s, s % 2
                pe.wait_ge(probs_done, n + 1)
                wait(pe, pT_lo_done, n - 1)
                for w in range(w0 - b, w1 - b):
                    last = nc.tensor.transpose(pT_ps[:, r, w * P:(w + 1) * P], probs[:, r, w * P:(w + 1) * P],
                                               ident[:, :])
                last.then_inc(pT_done, 1)

            def probs_times_values(i, par, s):
                c, b, h = where(s)
                w0, w1 = window(i, s)
                n, r, g = STEPS * i + s, s % 4, s // HC
                pe.wait_ge(pT_lo_done, n + 1)
                if h == 0:
                    wait(pe, o_summed, GROUPS * i + g - 1)
                if s == 0:
                    wait(pe, v_carried, i)
                    pe.wait_ge(v_done, 2 * i + 1)
                if s == HC:
                    pe.wait_ge(v_done, 2 * i + 2)
                col = h * VW
                for w in range(w0, w1):
                    t = slice((w - b) * P, (w - b + 1) * P)
                    v = values[:, par, w, c * HC + h, :]
                    nc.tensor.matmul(o_ps[:, g % 2, col:col + VW], pT_hi[:, r, t], v,
                                     start=(w == w0), stop=False)
                    last = nc.tensor.matmul(o_ps[:, g % 2, col:col + 1 + 2 * DH], pT_lo[:, r, t], v[:, 0:1 + 2 * DH],
                                            start=False, stop=(w == w1 - 1))
                last.then_inc(pv_done, 1)

            def transpose_heads(bank, c):
                for b in range(2):
                    last = nc.tensor.transpose(job_ps[:, bank, b * P:(b + 1) * P], o_heads[:, c % 2, b, :], ident[:, :])
                return last

            def project_out(bank, b, part):
                for n in range(part * 3, part * 3 + 3):
                    k, pass_ = divmod(n, 3)
                    w = wout_lo if pass_ == 2 else wout_hi
                    a = oT_lo if pass_ == 1 else oT_hi
                    last = nc.tensor.matmul(job_ps[:, bank, :], a[:, k, b * P:(b + 1) * P], w[:, k, :],
                                            start=(n == 0), stop=(n == 3 * DC - 1))
                return last

            def job_part(i, par, kind, a, part):
                j = (kind, a)
                number, bank = job_number(i, j), bank_of(par, i, j)
                if part == 0:
                    pe.wait_ge(job_freed, number - 1)
                if kind == "qk":
                    if a == 0 and part == 0:
                        pe.wait_ge(job_freed, job_number(i, ("x", 1)) + 1)
                        pe.wait_ge(xT_carried, 2 * i + 2)
                    last = pe_project_qk(bank, a, part)
                elif kind == "v":
                    last = pe_project_v(bank, 1 + a, part)
                elif kind == "x":
                    pe.wait_ge(xn_done, 2 * i + a + 1)
                    last = pe_transpose_x(bank, a)
                elif kind == "oT":
                    pe.wait_ge(o_done, 2 * DC * (i - 1) + 2 * DC if a == 3 else 2 * DC * i + 2 * a + 2)
                    last = transpose_heads(bank, a)
                else:
                    if part == 0:
                        pe.wait_ge(job_freed, job_number(i, ("oT", 3)) + 1)
                    last = project_out(bank, a, part)
                if part == LAST_PART[kind]:
                    last.then_inc(job_filled, 1)

            for part in range(4):
                last = pe_project_qk(0, 0, part)
            last.then_inc(job_filled, 1)
            for part in range(4):
                last = pe_project_v(1, 1, part)
            last.then_inc(job_filled, 1)
            pe.wait_ge(job_freed, 1)
            for part in range(4):
                last = pe_project_v(0, 2, part)
            last.then_inc(job_filled, 1)

            def tile(i, par):
                for s in range(STEPS):
                    scores(i, s)
                    for kind, a, part in PARTS.get(s, ()):
                        if (kind, a) in kind_of(i):
                            job_part(i, par, kind, a, part)
                    pi, ps = back(i, s, TURN)
                    if exists(pi):
                        transpose_probs(pi, ps)
                    vi, vs = back(i, s, PV)
                    if exists(vi):
                        probs_times_values(vi, parity_back(par, s, PV), vs)

            tiles(pe, tile)
            end, par = NT - 1, (NT - 1) % 2
            transpose_probs(end, STEPS - 1)
            for s in range(STEPS - PV, STEPS):
                probs_times_values(end, par, s)
            pe.wait_ge(job_freed, tail_number(("oT", 3)) - 1)
            pe.wait_ge(o_done, GROUPS * NT)
            transpose_heads(len(LAST) % 2, 3).then_inc(job_filled, 1)
            for b in range(2):
                pe.wait_ge(job_freed, tail_number(("oT", 3)) + 1)
                for part in range(4):
                    last = project_out((len(LAST) + 1 + b) % 2, b, part)
                last.then_inc(job_filled, 1)



def prepare_feed_forward(nc, fast_b, w_fc, w_proj, u, v, gate, ident, fc_T, proj_T, fc_scale2, proj_scale,
                         low_in_hi, low_in_lo, low_out):
    F = w_fc.shape[0]
    FB = F // P
    R = v.shape[0]
    COLS = F // D
    UNITS = FB + DC * COLS
    with ExitStack() as ctx:
        def sb(name, shape, dt=F32):
            return ctx.enter_context(nc.sbuf_tensor(name, shape, dt))

        def sem(name):
            return ctx.enter_context(nc.semaphore(name))

        fc_in = sb("fc_in", [P, 4, D])
        proj_in = sb("proj_in", [P, 2, F])
        abs_sum = sb("abs_sum", [P, FB + DC])
        scale = sb("scale", [P, FB + DC])
        inv_scale = sb("inv_scale", [P, FB + DC])
        neg_round = sb("neg_round", [P, 1])
        ones = sb("ones", [P, P])
        diagonal = sb("diagonal", [P, DC, P])
        gate_wide = sb("gate_wide", [P, 1])
        v_in = sb("v_in", [R, D])
        fast_T = sb("fast_T", [R, R])
        u_in = sb("u_in", [P, FB, R])
        u_wide = sb("u_wide", [P, FB, 3 * DH])
        turn_ps = ctx.enter_context(nc.psum_tensor("turn_ps", [P, 4, D], F32))
        scale_ps = ctx.enter_context(nc.psum_tensor("scale_ps", [P, D], F32))
        low_ps = ctx.enter_context(nc.psum_tensor("low_ps", [P, DC * R], F32))

        fc_here = [sem(f"fc_here{n}") for n in range(4)]
        proj_here = [sem(f"proj_here{n}") for n in range(2)]
        small_here = sem("small_here")
        zeroed, ident_done, consts_set = sem("f_ident_zeroed"), sem("f_ident_done"), sem("f_consts_set")
        quant_step = sem("quant_step")
        turned, copied = sem("turned"), sem("copied")
        diag_done, scale_summed, low_summed, low_hi_done, prep_done = (
            sem("diag_done"), sem("scale_summed"), sem("low_summed"), sem("low_hi_done"), sem("prep_done"))
        u_done, u_turned, u_copied = sem("u_done"), sem("u_turned"), sem("u_copied")
        block = ctx.enter_context(nc.Block())

        @block.sync
        def _(sp):
            for n in range(FB):
                if n >= 4:
                    sp.wait_ge(turned, n - 3)
                sp.dma_start(fc_in[:, n % 4, :], w_fc[n * P:(n + 1) * P, :]).then_inc(fc_here[n % 4], 16)
            for n in range(DC):
                if n >= 2:
                    sp.wait_ge(turned, FB + COLS * (n - 1))
                sp.dma_start(proj_in[:, n % 2, :], w_proj[n * P:(n + 1) * P, :]).then_inc(proj_here[n % 2], 16)

        @block.gpsimd
        def _(pool):
            pool.dma_start(v_in[:, :], v).then_inc(small_here, 16)
            pool.dma_start(u_in[:, :, :], u.rearrange("(n p) r -> p n r", p=P)).then_inc(small_here, 16)
            pool.dma_start(gate_wide[:, :], gate.partition_broadcast(P)).then_inc(small_here, 16)
            with nc.allow_non_contiguous_dma("a 16 x 16 matrix, once"):
                pool.dma_start(fast_T[:, :], fast_b.rearrange("a b -> b a")).then_inc(small_here, 16)
            identity_on_pool(pool, nc, ident, zeroed, ident_done)
            nc.gpsimd.memset(neg_round[:, :], -ROUND)
            nc.gpsimd.memset(ones[:, :], 1.0)
            nc.gpsimd.memset(u_wide[:, :, :], 0.0)
            nc.gpsimd.memset(low_in_hi.bitcast(F32), 0.0)
            nc.gpsimd.memset(low_in_lo.bitcast(F32), 0.0).then_inc(consts_set, 1)

        @block.vector
        def _(dve):
            step = 0
            dve.wait_ge(consts_set, 1)
            dve.wait_ge(ident_done, 1)
            for n in range(FB + DC):
                if n < FB:
                    w, width = fc_in[:, n % 4, :], D
                    dve.wait_ge(fc_here[n % 4], 16 * (n // 4 + 1))
                else:
                    w, width = proj_in[:, n % 2, :], F
                    dve.wait_ge(proj_here[n % 2], 16 * ((n - FB) // 2 + 1))
                nc.vector.tensor_reduce(abs_sum[:, n:n + 1], w, AX_X, ALU.add, apply_absolute_value=True
                                        ).then_inc(quant_step, 1)
                dve.wait_ge(quant_step, step + 1)
                nc.vector.tensor_scalar(scale[:, n:n + 1], abs_sum[:, n:n + 1], 1.0 / width, MIN_SCALE,
                                        ALU.mult, ALU.max).then_inc(quant_step, 1)
                dve.wait_ge(quant_step, step + 2)
                nc.vector.reciprocal(inv_scale[:, n:n + 1], scale[:, n:n + 1]).then_inc(quant_step, 1)
                dve.wait_ge(quant_step, step + 3)
                nc.vector.tensor_scalar(w, w, inv_scale[:, n:n + 1], 1.0, ALU.mult, ALU.min).then_inc(quant_step, 1)
                dve.wait_ge(quant_step, step + 4)
                nc.vector.tensor_scalar(w, w, -1.0, ROUND, ALU.max, ALU.add).then_inc(quant_step, 1)
                step += 5
            nc.vector.tensor_tensor(fc_scale2[:, :], scale[:, 0:FB], scale[:, 0:FB], ALU.mult)
            for c in range(DC):
                last = nc.vector.tensor_scalar(diagonal[:, c, :], ident[:, :], scale[:, FB + c:FB + c + 1], None,
                                               ALU.mult)
            last.then_inc(diag_done, 1)
            dve.wait_ge(small_here, 64)
            for rep in range(3):
                for n in range(FB):
                    last = nc.vector.tensor_scalar(u_wide[:, n, rep * DH:rep * DH + R], u_in[:, n, :],
                                                   gate_wide[:, 0:1], inv_scale[:, n:n + 1], ALU.mult, ALU.mult)
            last.then_inc(u_done, 1)
            dve.wait_ge(scale_summed, 1)
            nc.vector.tensor_copy(proj_scale[:, :], scale_ps[:, :])
            dve.wait_ge(low_hi_done, 3)
            for rep in range(3):
                nc.vector.tensor_tensor(low_in_lo[:, :, rep * DH:rep * DH + R],
                                        low_ps[:, :].rearrange("p (c r) -> p c r", c=DC),
                                        low_in_hi[:, :, rep * DH:rep * DH + R].bitcast(F32), ALU.subtract)
            lo = slice(2 * DH, 3 * DH)
            for n in range(FB // 4):
                dve.wait_ge(u_copied, n + 1)
                cols = slice(n * D, (n + 1) * D)
                nc.vector.tensor_tensor(low_out[lo, cols], turn_ps[lo, n, :], low_out[lo, cols].bitcast(F32),
                                        ALU.subtract).then_inc(prep_done, 1)

        @block.tensor
        def _(pe):
            pe.wait_ge(ident_done, 1)
            for n in range(UNITS):
                if n < FB:
                    blk, first, src = n, 0, fc_in[:, n % 4, :]
                else:
                    blk, first = FB + (n - FB) // COLS, (n - FB) % COLS * D
                    src = proj_in[:, blk % 2, :]
                pe.wait_ge(quant_step, 5 * (blk + 1))
                if n >= 4:
                    pe.wait_ge(copied, n - 3)
                for k in range(DC):
                    last = nc.tensor.transpose(turn_ps[:, n % 4, k * P:(k + 1) * P],
                                               src[:, first + k * P:first + (k + 1) * P], ident[:, :])
                last.then_inc(turned, 1)
            pe.wait_ge(diag_done, 1)
            for c in range(DC):
                last = nc.tensor.matmul(scale_ps[:, c * P:(c + 1) * P], ones[:, :], diagonal[:, c, :],
                                        start=True, stop=True)
            last.then_inc(scale_summed, 1)
            pe.wait_ge(u_done, 1)
            for c in range(DC):
                last = nc.tensor.matmul(low_ps[:, c * R:(c + 1) * R], v_in[:, c * P:(c + 1) * P], fast_T[:, :],
                                        start=True, stop=True)
            last.then_inc(low_summed, 1)
            pe.wait_ge(copied, UNITS)
            for n in range(FB):
                last = nc.tensor.transpose(turn_ps[0:3 * DH, n // 4, n % 4 * P:(n % 4 + 1) * P], u_wide[:, n, :],
                                           ident[:, :])
                if n % 4 == 3:
                    last.then_inc(u_turned, 1)

        @block.scalar
        def _(act):
            act.wait_ge(consts_set, 1)
            for n in range(UNITS):
                act.wait_ge(turned, n + 1)
                if n < FB:
                    dst = fc_T[:, :, n * P:(n + 1) * P]
                else:
                    c, g = divmod(n - FB, COLS)
                    dst = proj_T[:, g * 4:g * 4 + 4, c * P:(c + 1) * P]
                nc.scalar.activation(dst, turn_ps[:, n % 4, :].rearrange("p (k t) -> p k t", k=4), ACT.Identity,
                                     bias=neg_round[:, 0:1], scale=1.0).then_inc(copied, 1)
            act.wait_ge(low_summed, 1)
            for rep in range(3):
                nc.scalar.copy(low_in_hi[:, :, rep * DH:rep * DH + R],
                               low_ps[:, :].rearrange("p (c r) -> p c r", c=DC)).then_inc(low_hi_done, 1)
            for n in range(FB // 4):
                act.wait_ge(u_turned, n + 1)
                nc.scalar.copy(low_out[:, n * D:(n + 1) * D], turn_ps[0:3 * DH, n, :]).then_inc(u_copied, 1)


def feed_forward(nc, x, partial, fast_b, w_fc, w_proj, u, v, gate, out):
    F = w_fc.shape[0]
    FB = F // P
    NB = D // P
    T = NB * P
    NT = x.shape[0] // T
    LAG = 2
    assert FB % 2 == 0 and NT % 2 == 0
    with ExitStack() as ctx:
        def sb(name, shape, dt=F32):
            return ctx.enter_context(nc.sbuf_tensor(name, shape, dt))

        def sem(name):
            return ctx.enter_context(nc.semaphore(name))

        ident = sb("f_ident", [P, P])
        fc_T = sb("fc_T", [P, DC, F], F32R)
        proj_T = sb("proj_T", [P, FB, D], F32R)
        fc_scale2 = sb("fc_scale2", [P, FB])
        proj_scale = sb("proj_scale", [P, D])
        low_in_hi = sb("low_in_hi", [P, DC, 3 * DH], F32R)
        low_in_lo = sb("low_in_lo", [P, DC, 3 * DH], F32R)
        low_out = sb("low_out", [3 * DH, F], F32R)
        prepare_feed_forward(nc, fast_b, w_fc, w_proj, u, v, gate, ident, fc_T, proj_T, fc_scale2, proj_scale,
                             low_in_hi[:, :, :], low_in_lo[:, :, :], low_out)

        x_in = sb("f_x_in", [P, NB, D])
        xn = sb("f_xn", [P, 2, D])
        bn = sb("f_bn", [P, NB, 6])
        minus_half = sb("f_minus_half", [P, 1])
        stats = sb("f_stats", [P, NB, 4])
        xT_hi = sb("f_xT_hi", [P, 2, DC, T], F32R)
        xT_lo = sb("f_xT_lo", [P, 2, DC, T], F32R)
        low = sb("low", [3 * DH, 2, T], F32R)
        relu = sb("relu", [P, 2, T])
        sq = sb("sq", [P, 2, T])
        sq_hi = sb("sq_hi", [P, 2, T], F32R)
        sq_lo = sb("sq_lo", [P, 2, T], F32R)
        part_in = sb("part_in", [P, NB, D])
        y = sb("f_y", [P, NB, D])
        up_ps = ctx.enter_context(nc.psum_tensor("up_ps", [P, 2, T], F32))
        down_ps = ctx.enter_context(nc.psum_tensor("down_ps", [P, NB, D], F32))
        turn_ps = ctx.enter_context(nc.psum_tensor("x_turn_ps", [P, DC * P], F32))
        low_ps = ctx.enter_context(nc.psum_tensor("low_act_ps", [3 * DH, T], F32))

        x_here = [sem(f"f_x_here{b}") for b in range(NB)]
        part_here = [sem(f"part_here{b}") for b in range(NB)]
        ln_step, xn_done, x_turned, xT_hi_done, xT_done = (
            sem("f_ln_step"), sem("f_xn_done"), sem("x_turned"), sem("f_xT_hi_done"), sem("f_xT_done"))
        half_set = sem("half_set")
        ticks = {e: sem(f"f_ticks_{n}") for n, e in (("dve", nc.vector.engine), ("sp", nc.sync.engine))}
        low_filled, low_hi_done, low_done = sem("low_filled"), sem("low_act_hi_done"), sem("low_done")
        up_done, relu_done, sq_done, sq_hi_done, sq_lo_done, down_done = (
            sem("up_done"), sem("relu_done"), sem("sq_done"), sem("sq_hi_done"), sem("sq_lo_done"), sem("down_done"))
        down_taken, y_done = sem("down_taken"), sem("f_y_done")
        stored = [sem(f"stored{b}") for b in range(NB)]
        block = ctx.enter_context(nc.Block())

        TURN_STEP = [4, 6, 8, 10]
        LOW_STEP = 13

        def tiles(eng, tile):
            tile(0, 0)
            with eng.Fori(0, (NT - 2) // 2) as pair:
                for n in range(2):
                    tile(2 * pair + 1 + n, (1 + n) % 2)
            tile(NT - 1, (NT - 1) % 2)

        def is_last(i):
            return isinstance(i, int) and i == NT - 1

        def back(i, s, n):
            return (i, s - n) if s >= n else (i - 1, s - n + FB)

        def exists(i):
            return not (isinstance(i, int) and i < 0)

        @block.sync
        def _(sp):
            def load_x(i):
                for b in range(NB):
                    wait(sp, xn_done, NB * (i - 1) + b + 1)
                    settle(sp, ticks)
                    sp.dma_start(x_in[:, b, :], block_rows(x, NB * i + b)).then_inc(x_here[b], 16)

            for b in range(NB):
                sp.sem_inc(stored[b], 16)
            load_x(0)

            def tile(i, par):
                if not is_last(i):
                    load_x(i + 1)
                if not (isinstance(i, int) and i == 0):
                    for b in range(NB):
                        sp.wait_ge(y_done, NB * (i - 1) + b + 1)
                        settle(sp, ticks)
                        sp.dma_start(block_rows(out, NB * (i - 1) + b), y[:, b, :]).then_inc(stored[b], 16)
                for b in range(NB):
                    sp.dma_start(part_in[:, b, :], block_rows(partial, NB * i + b)).then_inc(part_here[b], 16)

            tiles(sp, tile)
            for b in range(NB):
                sp.wait_ge(y_done, NB * (NT - 1) + b + 1)
                sp.dma_start(block_rows(out, NB * (NT - 1) + b), y[:, b, :]).then_inc(stored[b], 16)
            for b in range(NB):
                sp.wait_ge(stored[b], 16 * (NT + 1))

        @block.gpsimd
        def _(pool):
            nc.gpsimd.memset(minus_half[:, :], -0.5).then_inc(half_set, 1)
            pool.wait_ge(half_set, 1)
            for b in range(NB):
                inverse_std(pool, nc, stats[:, b, :], minus_half, ln_step, 5 * b + 3)

            def tile(i, par):
                if not is_last(i):
                    for b in range(NB):
                        inverse_std(pool, nc, stats[:, b, :], minus_half, ln_step, 5 * (NB * (i + 1) + b) + 3)
                for b in range(NB):
                    pool.wait_ge(down_taken, NB * i + b + 1)
                    pool.wait_ge(part_here[b], 16 * (i + 1))
                    nc.gpsimd.tensor_tensor(y[:, b, :], y[:, b, :], part_in[:, b, :], ALU.add).then_inc(y_done, 1)

            tiles(pool, tile)

        @block.scalar
        def _(act):
            def normalise(i, b):
                act.wait_ge(ln_step, 5 * (NB * i + b) + 5)
                wait(act, x_turned, NB * i + b - 1)
                nc.scalar.activation(xn[:, b % 2, :], x_in[:, b, :], ACT.Identity, bias=stats[:, b, 3:4],
                                     scale=stats[:, b, 2:3]).then_inc(xn_done, 1)

            def xT_high(i, par, b):
                act.wait_ge(x_turned, NB * i + b + 1)
                nc.scalar.copy(xT_hi[:, par, :, b * P:(b + 1) * P], turn_ps[:, :].rearrange("p (c t) -> p c t", c=DC)
                               ).then_inc(xT_hi_done, 1)

            def low_high(i, par):
                act.wait_ge(low_filled, i + 1)
                nc.scalar.copy(low[:, par, :], low_ps[:, :]).then_inc(low_hi_done, 1)

            for b in range(NB):
                normalise(0, b)
                xT_high(0, 0, b)
            low_high(0, 0)

            def square_hi(i, s):
                n = FB * i + s
                act.wait_ge(sq_done, n + 1)
                wait(act, down_done, n - 1)
                nc.scalar.copy(sq_hi[:, s % 2, :], sq[:, s % 2, :]).then_inc(sq_hi_done, 1)

            def tile(i, par):
                for s in range(FB):
                    n = FB * i + s
                    act.wait_ge(up_done, n + 1)
                    wait(act, sq_done, n - 1)
                    nc.scalar.activation(relu[:, s % 2, :], up_ps[:, s % 2, :], ACT.Relu,
                                         scale=fc_scale2[:, s:s + 1]).then_inc(relu_done, 1)
                    pi, ps = back(i, s, 1)
                    if exists(pi):
                        square_hi(pi, ps)
                    if not is_last(i):
                        for b in range(NB):
                            if s == TURN_STEP[b] - 1:
                                normalise(i + 1, b)
                            if s == TURN_STEP[b]:
                                xT_high(i + 1, 1 - par, b)
                        if s == LOW_STEP:
                            low_high(i + 1, 1 - par)

            tiles(act, tile)
            square_hi(NT - 1, FB - 1)

        @block.vector
        def _(dve):
            def layernorm(i, b):
                n = 5 * (NB * i + b)
                dve.wait_ge(x_here[b], 16 * (i + 1))
                nc.vector.bn_stats(bn[:, b, :], x_in[:, b, :]).then_inc(ln_step, 1)
                dve.wait_ge(ln_step, n + 1)
                settle(dve, ticks)
                nc.vector.bn_aggr(stats[:, b, 0:2], bn[:, b, :]).then_inc(ln_step, 1)
                dve.wait_ge(ln_step, n + 2)
                nc.vector.tensor_scalar(stats[:, b, 1:2], stats[:, b, 1:2], EPS, None, ALU.add).then_inc(ln_step, 1)
                dve.wait_ge(ln_step, n + 4)
                nc.vector.scalar_tensor_tensor(stats[:, b, 3:4], stats[:, b, 0:1], -1.0, stats[:, b, 2:3],
                                               ALU.mult, ALU.mult).then_inc(ln_step, 1)

            def xT_low(i, par, b):
                dve.wait_ge(xT_hi_done, NB * i + b + 1)
                cols = slice(b * P, (b + 1) * P)
                nc.vector.tensor_tensor(xT_lo[:, par, :, cols], turn_ps[:, :].rearrange("p (c t) -> p c t", c=DC),
                                        xT_hi[:, par, :, cols].bitcast(F32), ALU.subtract).then_inc(xT_done, 1)

            def low_low(i, par):
                dve.wait_ge(low_hi_done, i + 1)
                rows = slice(DH, 2 * DH)
                nc.vector.tensor_tensor(low[rows, par, :], low_ps[rows, :], low[rows, par, :].bitcast(F32),
                                        ALU.subtract).then_inc(low_done, 1)

            for b in range(NB):
                layernorm(0, b)
                xT_low(0, 0, b)
            low_low(0, 0)

            def square_lo(i, s):
                dve.wait_ge(sq_hi_done, FB * i + s + 1)
                nc.vector.tensor_tensor(sq_lo[:, s % 2, :], sq[:, s % 2, :], sq_hi[:, s % 2, :].bitcast(F32),
                                        ALU.subtract).then_inc(sq_lo_done, 1)

            def take_down(i):
                for b in range(NB):
                    if b == 0:
                        dve.wait_ge(down_done, FB * (i + 1))
                    dve.wait_ge(stored[b], 16 * (i + 1))
                    nc.vector.tensor_tensor(y[:, b, :], down_ps[:, b, :], proj_scale[:, :], ALU.mult
                                            ).then_inc(down_taken, 1)

            def tile(i, par):
                for s in range(FB):
                    n = FB * i + s
                    dve.wait_ge(relu_done, n + 1)
                    wait(dve, sq_lo_done, n - 1)
                    nc.vector.scalar_tensor_tensor(sq[:, s % 2, :], up_ps[:, s % 2, :], 0.0, relu[:, s % 2, :],
                                                   ALU.max, ALU.mult).then_inc(sq_done, 1)
                    pi, ps = back(i, s, 1)
                    if exists(pi):
                        square_lo(pi, ps)
                    if s == LAG - 1 and not (isinstance(i, int) and i == 0):
                        take_down(i - 1)
                    if not is_last(i):
                        for b in range(NB):
                            if s == TURN_STEP[b] - 2:
                                layernorm(i + 1, b)
                            if s == TURN_STEP[b]:
                                xT_low(i + 1, 1 - par, b)
                        if s == LOW_STEP:
                            low_low(i + 1, 1 - par)

            tiles(dve, tile)
            square_lo(NT - 1, FB - 1)
            take_down(NT - 1)

        @block.tensor
        def _(pe):
            def turn_x(i, b):
                n = NB * i + b
                pe.wait_ge(xn_done, n + 1)
                wait(pe, xT_done, n)
                for k in range(DC):
                    last = nc.tensor.transpose(turn_ps[:, k * P:(k + 1) * P], xn[:, b % 2, k * P:(k + 1) * P],
                                               ident[:, :])
                last.then_inc(x_turned, 1)

            def low_rank(i, par):
                pe.wait_ge(xT_done, NB * (i + 1))
                wait(pe, low_done, i)
                for n in range(3 * DC):
                    k, pass_ = divmod(n, 3)
                    w = low_in_lo if pass_ == 2 else low_in_hi
                    a = xT_lo if pass_ == 1 else xT_hi
                    last = nc.tensor.matmul(low_ps[:, :], w[:, k, :], a[:, par, k, :],
                                            start=(n == 0), stop=(n == 3 * DC - 1))
                last.then_inc(low_filled, 1)

            def up(i, par, s):
                n = FB * i + s
                cols = slice(s * P, (s + 1) * P)
                if s == 0:
                    pe.wait_ge(low_done, i + 1)
                wait(pe, sq_done, n - 1)
                for k in range(DC):
                    nc.tensor.matmul(up_ps[:, s % 2, :], fc_T[:, k, cols], xT_hi[:, par, k, :],
                                     start=(k == 0), stop=False)
                    nc.tensor.matmul(up_ps[:, s % 2, :], fc_T[:, k, cols], xT_lo[:, par, k, :],
                                     start=False, stop=False)
                nc.tensor.matmul(up_ps[:, s % 2, :], low_out[:, cols], low[:, par, :],
                                 start=False, stop=True).then_inc(up_done, 1)

            def down(i, s):
                n = FB * i + s
                pe.wait_ge(sq_lo_done, n + 1)
                for b in range(NB):
                    if s == 0:
                        wait(pe, down_taken, NB * (i - 1) + b + 1)
                    t = slice(b * P, (b + 1) * P)
                    nc.tensor.matmul(down_ps[:, b, :], sq_hi[:, s % 2, t], proj_T[:, s, :],
                                     start=(s == 0), stop=False)
                    last = nc.tensor.matmul(down_ps[:, b, :], sq_lo[:, s % 2, t], proj_T[:, s, :],
                                            start=False, stop=(s == FB - 1))
                last.then_inc(down_done, 1)

            for b in range(NB):
                turn_x(0, b)
            low_rank(0, 0)

            def tile(i, par):
                for s in range(FB):
                    up(i, par, s)
                    if not is_last(i):
                        if s in TURN_STEP:
                            turn_x(i + 1, TURN_STEP.index(s))
                        if s == LOW_STEP:
                            low_rank(i + 1, 1 - par)
                    di, ds = back(i, s, LAG)
                    if exists(di):
                        down(di, ds)

            tiles(pe, tile)
            for s in range(FB - LAG, FB):
                down(NT - 1, s)


_INS = ["L0_attn_x", "L0_attn_Wqkv", "L0_attn_bqkv", "L0_attn_Wout", "L0_attn_bout", "L0_ffn_fast_b", "L0_ffn_w_fc",
        "L0_ffn_w_proj", "L0_ffn_u", "L0_ffn_v", "L0_ffn_gate"]


def build(nc, x, Wqkv, bqkv, Wout, bout, fast_b, w_fc, w_proj, u, v, gate, out):
    rows = x.rearrange("b s d -> (b s) d")
    partial = nc.dram_tensor("partial", rows.shape, F32, kind="Internal").ap()
    attention(nc, rows, Wqkv, bqkv, Wout, bout, partial)
    feed_forward(nc, rows, partial, fast_b, w_fc, w_proj, u, v, gate, out.rearrange("b s d -> (b s) d"))


def kernel(**inputs):
    import numpy as np
    import concourse.bacc as bacc
    from concourse import mybir as mb
    from concourse.bass_utils import run_bass_kernel_spmd

    nc = bacc.Bacc("TRN2", target_bir_lowering=False, num_devices=1)
    arrays, args = {}, []
    for name in _INS:
        a = np.ascontiguousarray(inputs[name])
        if name == "L0_ffn_gate":
            a = a.reshape(1)
        arrays[f"in_{name}"] = a
        args.append(nc.dram_tensor(f"in_{name}", a.shape, mb.dt.from_np(a.dtype), kind="ExternalInput").ap())
    shape = inputs["L0_attn_x"].shape
    args.append(nc.dram_tensor("out", shape, F32, kind="ExternalOutput").ap())
    build(nc, *args)
    r = run_bass_kernel_spmd(nc, [arrays], core_ids=[0])
    return r.results[0]["out"]
```

```python
from contextlib import ExitStack

import concourse.bass as bass
from concourse import mybir

F32 = mybir.dt.float32
F32R = mybir.dt.float32r
BF16 = mybir.dt.bfloat16
F16 = mybir.dt.float16
ALU = mybir.AluOpType
ACT = mybir.ActivationFunctionType
AX_X = mybir.AxisListType.X

P = 128
D = 512
DC = D // P
H = 16
DH = D // H
HC = P // DH
EPS = 1e-5
MIN_SCALE = 1e-5
NEG = -1e30
SCORE_SCALE = 1.0 / float(D) ** 0.5
ROUND = 1.5 * 2.0 ** 23
VW = 1 + 3 * DH


def wait(eng, sem, value):
    if isinstance(value, int) and value <= 0:
        return
    eng.wait_ge(sem, value)


def settle(eng, ticks):
    eng.sem_inc(ticks[eng.engine], 1)


def block_rows(dram, block):
    return dram[bass.ds(block * P, P), :]


def identity_on_pool(pool, nc, ident, zeroed, ready):
    nc.gpsimd.memset(ident[:, :], 0.0).then_inc(zeroed, 1)
    pool.wait_ge(zeroed, 1)
    nc.gpsimd.affine_select(out=ident[:, :], in_=ident[:, :], compare_op=ALU.not_equal, fill=1.0,
                            base=0, pattern=[[-1, P]], channel_multiplier=1).then_inc(ready, 1)


def inverse_std(pool, nc, stats, minus_half, ln_step, value):
    pool.wait_ge(ln_step, value)
    nc.gpsimd.tensor_tensor(stats[:, 2:3], stats[:, 1:2], minus_half[:, :], ALU.pow).then_inc(ln_step, 1)



def split_attention_weights(nc, Wqkv, bqkv, Wout, bout, wqkv_hi, wqkv_lo, wout_hi, wout_lo, qk_bias, out_bias):
    with ExitStack() as ctx:
        stage = ctx.enter_context(nc.sbuf_tensor("w_stage", [P, 2, 3 * D], F32))
        wout_raw = ctx.enter_context(nc.sbuf_tensor("wout_raw", [P, DC, D], F32))
        v_bias = ctx.enter_context(nc.sbuf_tensor("v_bias", [P, DC], F32))
        v_bias_wide = ctx.enter_context(nc.sbuf_tensor("v_bias_wide", [P, DC, P], F32))
        bout_wide = ctx.enter_context(nc.sbuf_tensor("bout_wide", [P, D], F32))
        bias_ps = ctx.enter_context(nc.psum_tensor("bias_ps", [P, D], F32))
        chunk_in = [ctx.enter_context(nc.semaphore(f"wqkv_chunk_in{b}")) for b in range(2)]
        wout_in = ctx.enter_context(nc.semaphore("wout_in"))
        biases_in = ctx.enter_context(nc.semaphore("biases_in"))
        hi_done = ctx.enter_context(nc.semaphore("w_hi_done"))
        lo_done = ctx.enter_context(nc.semaphore("w_lo_done"))
        wide_done = ctx.enter_context(nc.semaphore("v_bias_wide_done"))
        bias_summed = ctx.enter_context(nc.semaphore("bias_summed"))
        block = ctx.enter_context(nc.Block())

        @block.sync
        def _(sp):
            sp.dma_start(wout_raw[:, :, :], Wout.rearrange("(c p) n -> p c n", p=P)).then_inc(wout_in, 16)
            for k in range(DC):
                if k >= 2:
                    sp.wait_ge(lo_done, k - 1)
                sp.dma_start(stage[:, k % 2, :], Wqkv[k * P:(k + 1) * P, :]).then_inc(chunk_in[k % 2], 16)

        @block.gpsimd
        def _(pool):
            with nc.allow_non_contiguous_dma("a bias vector, once"):
                pool.dma_start(v_bias[:, :], bqkv[2 * D:3 * D].rearrange("(c p) -> p c", p=P)).then_inc(biases_in, 16)
                pool.dma_start(qk_bias[:, :], bqkv[0:2 * D].rearrange("(c p) -> p c", p=P)).then_inc(biases_in, 16)
            pool.dma_start(bout_wide[:, :], bout.partition_broadcast(P)).then_inc(biases_in, 16)

        @block.scalar
        def _(act):
            for k in range(DC):
                act.wait_ge(chunk_in[k % 2], 16 * (k // 2 + 1))
                nc.scalar.copy(wqkv_hi[:, k, :], stage[:, k % 2, :]).then_inc(hi_done, 1)
            act.wait_ge(wout_in, 16)
            nc.scalar.copy(wout_hi[:, :, :], wout_raw[:, :, :]).then_inc(hi_done, 1)

        @block.vector
        def _(dve):
            dve.wait_ge(biases_in, 48)
            nc.vector.tensor_copy(v_bias_wide[:, :, :], v_bias[:, :].unsqueeze(2).to_broadcast([P, DC, P])
                                  ).then_inc(wide_done, 1)
            for k in range(DC):
                dve.wait_ge(hi_done, k + 1)
                nc.vector.tensor_tensor(wqkv_lo[:, k, :], stage[:, k % 2, :], wqkv_hi[:, k, :].bitcast(F32),
                                        ALU.subtract).then_inc(lo_done, 1)
            dve.wait_ge(hi_done, DC + 1)
            nc.vector.tensor_tensor(wout_lo[:, :, :], wout_raw[:, :, :], wout_hi[:, :, :].bitcast(F32),
                                    ALU.subtract).then_inc(lo_done, 1)
            dve.wait_ge(bias_summed, 1)
            nc.vector.tensor_tensor(out_bias[:, :], bias_ps[:, :], bout_wide[:, :], ALU.add).then_inc(lo_done, 1)

        @block.tensor
        def _(pe):
            pe.wait_ge(wide_done, 1)
            pe.wait_ge(wout_in, 16)
            for k in range(DC):
                last = nc.tensor.matmul(bias_ps[:, :], v_bias_wide[:, k, :], wout_raw[:, k, :],
                                        start=(k == 0), stop=(k == DC - 1))
            last.then_inc(bias_summed, 1)


def attention(nc, x, Wqkv, bqkv, Wout, bout, partial):
    NBLK = x.shape[0] // P
    NT = NBLK // 2
    T = 2 * P
    UNIT = 2 * HC
    STEPS = DC * UNIT
    GROUPS = STEPS // HC

    ctx = ExitStack()
    with ctx:
        def sb(name, shape, dt):
            return ctx.enter_context(nc.sbuf_tensor(name, shape, dt))

        def sem(name):
            return ctx.enter_context(nc.semaphore(name))

        wqkv_hi = sb("wqkv_hi", [P, DC, 3 * D], F32R)
        wqkv_lo = sb("wqkv_lo", [P, DC, 3 * D], F32R)
        wout_hi = sb("wout_hi", [P, DC, D], F32R)
        wout_lo = sb("wout_lo", [P, DC, D], F32R)
        qk_bias = sb("qk_bias", [P, 2 * DC], F32)
        out_bias = sb("out_bias", [P, D], F32)
        split_attention_weights(nc, Wqkv, bqkv, Wout, bout, wqkv_hi, wqkv_lo, wout_hi, wout_lo, qk_bias, out_bias)

        ident = sb("ident", [P, P], F32)
        mask = sb("mask", [P, 3 * P], F32)
        x_in = sb("x_in", [P, 2, D], F32)
        bn = sb("bn", [P, 2, 6], F32)
        minus_half = sb("minus_half", [P, 1], F32)
        stats = sb("stats", [P, 2, 4], F32)
        xT_hi = sb("xT_hi", [P, DC, 2, T], F32R)
        xT_lo = sb("xT_lo", [P, DC, 2, T], F32R)
        qk_parts = sb("qk_parts", [P, 2, 4, T], F32R)
        stack = [sb(f"stack{c}", [3 * DH, HC, 3, T], F32R) for c in range(DC)]
        values = sb("values", [P, 2, 4, H, VW], BF16)
        v_rest = sb("v_rest", [P, 2, D], F32)
        neg_scores = sb("neg_scores", [P, 2, 3 * P], F32)
        neg_max = sb("neg_max", [P, 4], F32)
        probs = sb("probs", [P, 2, 3 * P], F32)
        pT_hi = sb("pT_hi", [P, 4, 3 * P], F16)
        pT_lo = sb("pT_lo", [P, 4, 3 * P], F16)
        o_sum = sb("o_sum", [P, 2, P], F32)
        o_rcp = sb("o_rcp", [P, 2, HC], F32)
        o_heads = sb("o_heads", [P, 2, 2, P], F32)
        oT_hi = sb("oT_hi", [P, DC, T], F32R)
        oT_lo = sb("oT_lo", [P, DC, T], F32R)
        y = sb("y", [P, 2, D], F32)

        job_ps = ctx.enter_context(nc.psum_tensor("job_ps", [P, 2, D], F32))
        score_ps = ctx.enter_context(nc.psum_tensor("score_ps", [P, 2, D], F32))
        pT_ps = ctx.enter_context(nc.psum_tensor("pT_ps", [P, 2, D], F32))
        o_ps = ctx.enter_context(nc.psum_tensor("o_ps", [P, 2, D], F32))

        def q_cols(par, c, h, b):
            at = b if par else 1 - b
            return stack[c][:, h, 0, at * P:(at + 1) * P]

        def key_runs(par, b, w0, w1):
            if par:
                return [(w0, w0 // 2, w0 % 2, w1 - w0)]
            return [(w, 1 - w // 2, w % 2, n) for w, n in ((w0, min(w1, 2) - w0), (2, w1 - 2)) if n > 0]

        def own_tokens(xT, par, k):
            blocks = xT[:, k, :, :].rearrange("p a (b t) -> p (a b) t", b=2)
            return blocks[:, 1:3, :] if par else blocks[:, 0:4:3, :]

        def pe_project_qk(bank, par, c, part):
            is_k, half = divmod(part, 2)
            col = is_k * D + c * P
            out = job_ps[:, bank, is_k * T:(is_k + 1) * T]
            for n in range(half * 6, half * 6 + 6):
                k, pass_ = divmod(n, 3)
                w = wqkv_lo if pass_ == 2 else wqkv_hi
                a = xT_lo if pass_ == 1 else xT_hi
                last = nc.tensor.matmul(out, w[:, k, col:col + P], a[:, k, par, :] if is_k else own_tokens(a, par, k),
                                        start=(n == 0), stop=(n == 3 * DC - 1))
            return last

        def pe_project_v(bank, half, b, part):
            for n in range(part * 3, part * 3 + 3):
                k, pass_ = divmod(n, 3)
                w = wqkv_lo if pass_ == 2 else wqkv_hi
                a = xT_lo if pass_ == 1 else xT_hi
                last = nc.tensor.matmul(job_ps[:, bank, :], a[:, k, half, b * P:(b + 1) * P], w[:, k, 2 * D:3 * D],
                                        start=(n == 0), stop=(n == 3 * DC - 1))
            return last

        def pe_transpose_x(bank, r):
            for k in range(DC):
                last = nc.tensor.transpose(job_ps[:, bank, k * P:(k + 1) * P], x_in[:, r, k * P:(k + 1) * P], ident[:, :])
            return last

        def four(bank):
            return job_ps[:, bank, :].rearrange("p (c t) -> p c t", c=DC)

        def rider_cells(par, rider):
            kind, c, b = rider
            if kind == "oT":
                return [oT[:, c, b * P:(b + 1) * P] for oT in (oT_hi, oT_lo)]
            return [xT[:, c, 1 - par, b * P:(b + 1) * P] for xT in (xT_hi, xT_lo)]

        RIDER_COLS = slice(3 * P, 4 * P)

        def head_columns(ap, first):
            return ap[:, :, first:first + DH]

        with ExitStack() as pro:
            def psem(name):
                return pro.enter_context(nc.semaphore(name))

            zeroed, ident_done = psem("ident_zeroed"), psem("ident_done")
            mask_set, ones_set = psem("mask_set"), psem("ones_set")
            x_here = [psem(f"pro_x_here{r}") for r in range(2)]
            ln_step, xn_done, job_filled = psem("pro_ln_step"), psem("pro_xn_done"), psem("pro_job_filled")
            hi_done, job_freed, v2_done, v_done = psem("pro_hi"), psem("pro_job_freed"), psem("pro_v2"), psem("pro_v_done")
            k0_stacked = psem("k0_stacked")
            block = pro.enter_context(nc.Block())
            place = [(1, P), (0, 0), (0, P)]
            K0 = [(qk_parts[:, 0, c // 2, (c % 2) * P:(c % 2 + 1) * P],
                   qk_parts[:, 0, 2 + c // 2, (c % 2) * P:(c % 2 + 1) * P]) for c in range(DC)]

            @block.sync
            def _(sp):
                for b in range(3):
                    if b == 2:
                        sp.wait_ge(job_filled, 1)
                    sp.dma_start(x_in[:, b % 2, :], block_rows(x, b)).then_inc(x_here[b % 2], 16)
                sp.wait_ge(job_freed, 4)
                for c in range(DC):
                    for h in range(HC):
                        rows = slice(h * DH, (h + 1) * DH)
                        for r, part in enumerate((0, 0, 1)):
                            sp.dma_start(stack[c][r * DH:(r + 1) * DH, h, 2, P:2 * P].bitcast(F32),
                                         K0[c][part][rows, :].bitcast(F32)).then_inc(k0_stacked, 16)
                sp.wait_ge(k0_stacked, 16 * 3 * H)

            @block.gpsimd
            def _(pool):
                identity_on_pool(pool, nc, ident, zeroed, ident_done)
                nc.gpsimd.memset(minus_half[:, :], -0.5).then_inc(mask_set, 1)
                nc.gpsimd.memset(mask[:, :], 0.0).then_inc(mask_set, 1)
                nc.gpsimd.memset(values[:, :, :, :, 0:1], 1.0).then_inc(ones_set, 1)
                pool.wait_ge(mask_set, 2)
                nc.gpsimd.affine_select(out=mask[:, 0:P], in_=mask[:, 0:P], compare_op=ALU.is_ge, fill=NEG,
                                        base=0, pattern=[[1, P]], channel_multiplier=-1).then_inc(mask_set, 1)
                nc.gpsimd.affine_select(out=mask[:, 2 * P:3 * P], in_=mask[:, 2 * P:3 * P], compare_op=ALU.is_ge,
                                        fill=NEG, base=0, pattern=[[-1, P]], channel_multiplier=1).then_inc(mask_set, 1)
                for b in range(3):
                    inverse_std(pool, nc, stats[:, b % 2, :], minus_half, ln_step, 5 * b + 3)
                pool.wait_ge(job_freed, 5)
                slot = values[:, 0, 1, :, :]
                rest = v_rest[:, 0, :].rearrange("p (h d) -> p h d", h=H)
                nc.gpsimd.tensor_copy(head_columns(slot, 1 + DH), rest).then_inc(v2_done, 1)
                pool.wait_ge(v2_done, 1)
                nc.gpsimd.tensor_tensor(head_columns(slot, 1 + 2 * DH), rest, head_columns(slot, 1 + DH),
                                        ALU.subtract).then_inc(v_done, 1)

            @block.scalar
            def _(act):
                for b in range(3):
                    act.wait_ge(ln_step, 5 * b + 5)
                    nc.scalar.activation(x_in[:, b % 2, :], x_in[:, b % 2, :], ACT.Identity,
                                         bias=stats[:, b % 2, 3:4], scale=stats[:, b % 2, 2:3]).then_inc(xn_done, 1)
                    act.wait_ge(job_filled, b + 1)
                    half, col = place[b]
                    nc.scalar.copy(xT_hi[:, :, half, col:col + P], four(b % 2)).then_inc(hi_done, 1)
                act.wait_ge(job_filled, 4)
                for c in range(DC):
                    nc.scalar.activation(K0[c][0], job_ps[:, 1, c * P:(c + 1) * P], ACT.Identity,
                                         bias=qk_bias[:, DC + c:DC + c + 1], scale=1.0).then_inc(hi_done, 1)
                act.wait_ge(job_filled, 5)
                act.wait_ge(ones_set, 1)
                nc.scalar.copy(head_columns(values[:, 0, 1, :, :], 1),
                               job_ps[:, 0, :].rearrange("p (h d) -> p h d", h=H)).then_inc(hi_done, 1)

            @block.vector
            def _(dve):
                for b in range(3):
                    r = b % 2
                    dve.wait_ge(x_here[r], 16 * (b // 2 + 1))
                    nc.vector.bn_stats(bn[:, r, :], x_in[:, r, :]).then_inc(ln_step, 1)
                    dve.wait_ge(ln_step, 5 * b + 1)
                    nc.vector.bn_aggr(stats[:, r, 0:2], bn[:, r, :]).then_inc(ln_step, 1)
                    dve.wait_ge(ln_step, 5 * b + 2)
                    nc.vector.tensor_scalar(stats[:, r, 1:2], stats[:, r, 1:2], EPS, None, ALU.add
                                            ).then_inc(ln_step, 1)
                    dve.wait_ge(ln_step, 5 * b + 4)
                    nc.vector.scalar_tensor_tensor(stats[:, r, 3:4], stats[:, r, 0:1], -1.0, stats[:, r, 2:3],
                                                   ALU.mult, ALU.mult).then_inc(ln_step, 1)
                    dve.wait_ge(hi_done, b + 1)
                    half, col = place[b]
                    nc.vector.tensor_tensor(xT_lo[:, :, half, col:col + P], four(r),
                                            xT_hi[:, :, half, col:col + P].bitcast(F32), ALU.subtract
                                            ).then_inc(job_freed, 1)
                dve.wait_ge(hi_done, 3 + DC)
                for c in range(DC):
                    last = nc.vector.scalar_tensor_tensor(K0[c][1], job_ps[:, 1, c * P:(c + 1) * P],
                                                          qk_bias[:, DC + c:DC + c + 1], K0[c][0].bitcast(F32),
                                                          ALU.add, ALU.subtract)
                last.then_inc(job_freed, 1)
                dve.wait_ge(hi_done, 4 + DC)
                nc.vector.tensor_tensor(v_rest[:, 0, :].rearrange("p (h d) -> p h d", h=H),
                                        job_ps[:, 0, :].rearrange("p (h d) -> p h d", h=H),
                                        head_columns(values[:, 0, 1, :, :], 1), ALU.subtract).then_inc(job_freed, 1)

            @block.tensor
            def _(pe):
                pe.wait_ge(ident_done, 1)
                for b in range(3):
                    pe.wait_ge(xn_done, b + 1)
                    if b == 2:
                        pe.wait_ge(job_freed, 1)
                    pe_transpose_x(b % 2, b % 2).then_inc(job_filled, 1)
                pe.wait_ge(job_freed, 2)
                for c in range(DC):
                    for n in range(3 * DC):
                        k, pass_ = divmod(n, 3)
                        w = wqkv_lo if pass_ == 2 else wqkv_hi
                        a = xT_lo if pass_ == 1 else xT_hi
                        last = nc.tensor.matmul(job_ps[:, 1, c * P:(c + 1) * P], w[:, k, D + c * P:D + (c + 1) * P],
                                                a[:, k, 1, P:2 * P], start=(n == 0), stop=(n == 3 * DC - 1))
                last.then_inc(job_filled, 1)
                pe.wait_ge(job_freed, 3)
                for part in range(4):
                    last = pe_project_v(0, 1, 1, part)
                last.then_inc(job_filled, 1)

        FULL = [("qk", 2), ("qk", 3), ("out", 0), ("out", 1), ("qk", 0), ("qk", 1), ("v", 0), ("v", 1)]
        HEAD = [("qk", 0), ("qk", 1), ("v", 0), ("v", 1)]
        FIRST = [j for j in FULL if j[0] != "out"]
        LAST = FULL[:4]
        TAIL = [("out", 0), ("out", 1)]
        PARTS = STEPS // len(FULL)
        RIDERS = {6: ("oT", 3, 0), 7: ("oT", 3, 1), 16: ("oT", 0, 0), 17: ("oT", 0, 1), 22: ("oT", 1, 0),
                  23: ("oT", 1, 1), 30: ("oT", 2, 0), 31: ("oT", 2, 1)}
        RIDERS.update({8 + 2 * k + r: ("x", k, r) for k in range(DC) for r in range(2)})
        RIDER_STEP = {rider: step for step, rider in RIDERS.items()}
        TURN, LOW, PV, FOLD = 1, 2, 3, 4
        LN_STEPS = {0: [(0, 0)], 1: [(0, 1)], 2: [(1, 0), (0, 2)], 3: [(1, 1)], 4: [(1, 2), (0, 3)], 6: [(1, 3)]}
        XN_STEPS = [6, 7]
        CARRY_STEP = 18
        JOB_LAG = 2

        def jobs_of(i):
            if isinstance(i, int):
                return FIRST if i == 0 else LAST if i == NT - 1 else FULL
            return FULL

        def job_at(i, s):
            n, part = divmod(s, PARTS)
            return FULL[n] if FULL[n] in jobs_of(i) else None, part

        def rider_at(i, s):
            rider = RIDERS.get(s)
            if rider and isinstance(i, int):
                if (i == 0 and rider[0:2] == ("oT", 3)) or (i == NT - 1 and rider[0] == "x"):
                    return None
            return rider

        def job_number(i, job):
            if isinstance(i, int) and i == 0:
                return len(HEAD) + FIRST.index(job)
            return (i - 1) * len(FULL) + len(HEAD) + len(FIRST) + FULL.index(job)

        def split_number(i, job):
            if isinstance(i, int) and i == 0:
                return len(HEAD) + FIRST.index(job)
            return i * len(FIRST) + len(HEAD) + FIRST.index(job)

        def bank_of(i, job):
            return FULL.index(job) % 2

        def tail_number(job):
            return job_number(NT - 1, LAST[-1]) + 1 + TAIL.index(job)

        def rider_count(i, rider):
            return STEPS * i + RIDER_STEP[rider] + 1 - TURN

        ticks = {e: sem(f"ticks_{n}") for n, e in (("dve", nc.vector.engine), ("pool", nc.gpsimd.engine),
                                                   ("sp", nc.sync.engine))}
        x_here = [sem(f"x_here{r}") for r in range(2)]
        ln_step = [sem(f"ln_step{r}") for r in range(2)]
        xn_done = sem("xn_done")
        job_filled = sem("job_filled")
        hi_done = sem("job_hi_done")
        job_freed = sem("job_freed")
        stacked = [[sem(f"stacked{h}_{r}") for r in range(2)] for h in range(HC)]
        v2_done = sem("v2_done")
        v_done = sem("v_done")
        v_carried = sem("v_carried")
        scores_done = sem("scores_done")
        neg_done = sem("neg_scores_done")
        probs_done = sem("probs_done")
        pT_done = sem("probs_transposed")
        pT_hi_done = sem("pT_hi_done")
        pT_lo_done = sem("pT_lo_done")
        pv_done = sem("pv_done")
        o_summed = sem("o_summed")
        o_done = sem("o_heads_done")
        y_here = [sem(f"y_here{b}") for b in range(2)]
        y_biased = sem("y_biased")
        y_stored = [sem(f"y_stored{b}") for b in range(2)]
        block = ctx.enter_context(nc.Block())

        def window(i, s):
            b = (s % UNIT) // HC
            first = 1 if isinstance(i, int) and i == 0 and b == 0 else b
            last = 3 if isinstance(i, int) and i == NT - 1 and b == 1 else b + 3
            return first, last

        def where(s):
            return s // UNIT, (s % UNIT) // HC, s % HC

        def back(i, s, n):
            return (i, s - n) if s >= n else (i - 1, s - n + STEPS)

        def exists(i):
            return not (isinstance(i, int) and i < 0)

        def parity_back(par, s, n):
            return par if s >= n else 1 - par

        def tiles(eng, tile):
            tile(0, 0)
            with eng.Fori(0, (NT - 2) // 2) as pair:
                for u in range(2):
                    tile(2 * pair + 1 + u, (1 + u) % 2)
            tile(NT - 1, (NT - 1) % 2)

        assert NT % 2 == 0 and len(FULL) % 2 == 0 and len(FIRST) % 2 == 0 and len(HEAD) % 2 == 0

        @block.sync
        def _(sp):
            def stack_qk(i, par, c):
                r = c % 2
                settle(sp, ticks)
                wait(sp, scores_done, STEPS * (i - 1) + UNIT * (c + 1))
                settle(sp, ticks)
                for h in range(HC):
                    rows = slice(h * DH, (h + 1) * DH)
                    ready = stacked[h][r]
                    q_k = stack[c][:, h, slice(0, 3, 2) if par else slice(0, 2), :].bitcast(F32)
                    parts = qk_parts[rows, r, :, :].bitcast(F32)
                    for row, pair in enumerate((slice(0, 3, 2), slice(1, 3), slice(0, 4, 3))):
                        sp.dma_start(q_k[row * DH:(row + 1) * DH, :, :], parts[:, pair, :]).then_inc(ready, 16)

            def load_x(i, r):
                sp.dma_start(x_in[:, r, :], block_rows(x, (2 * i + 3 + r) % NBLK)).then_inc(x_here[r], 16)

            def load_y(i, b):
                sp.wait_ge(y_stored[b], 16 * (i + 1))
                settle(sp, ticks)
                sp.dma_start(y[:, b, :], block_rows(x, 2 * i + b)).then_inc(y_here[b], 16)

            for b in range(2):
                sp.sem_inc(y_stored[b], 16)
                load_x(0, b)
            for c in range(2):
                sp.wait_ge(job_freed, c + 1)
                stack_qk(0, 0, c)

            def tile(i, par):
                first = isinstance(i, int) and i == 0
                last = isinstance(i, int) and i == NT - 1
                if not first:
                    for b in range(2):
                        load_y(i - 1, b)
                for c in range(2, DC):
                    sp.wait_ge(job_freed, job_number(i, ("qk", c)) + 1)
                    stack_qk(i, par, c)
                if not last:
                    for r in range(2):
                        sp.wait_ge(pT_done, rider_count(i, ("x", DC - 1, r)))
                        settle(sp, ticks)
                        load_x(i + 1, r)
                if not first:
                    for b in range(2):
                        sp.wait_ge(job_freed, job_number(i, ("out", b)) + 1)
                        settle(sp, ticks)
                        sp.dma_start(block_rows(partial, 2 * (i - 1) + b), y[:, b, :]).then_inc(y_stored[b], 16)
                if not last:
                    for c in range(2):
                        sp.wait_ge(job_freed, job_number(i, ("qk", c)) + 1)
                        stack_qk(i + 1, 1 - par, c)

            tiles(sp, tile)
            for b in range(2):
                load_y(NT - 1, b)
            for b in range(2):
                sp.wait_ge(job_freed, tail_number(("out", b)) + 1)
                sp.dma_start(block_rows(partial, 2 * (NT - 1) + b), y[:, b, :]).then_inc(y_stored[b], 16)
            for b in range(2):
                sp.wait_ge(x_here[b], 16 * NT)
                sp.wait_ge(y_stored[b], 16 * (NT + 1))

        @block.gpsimd
        def _(pool):
            def finish_values(parity, r, number, count):
                slot = values[:, parity, 2 + r, :, :]
                rest = v_rest[:, r, :].rearrange("p (h d) -> p h d", h=H)
                pool.wait_ge(job_freed, number + 1)
                settle(pool, ticks)
                nc.gpsimd.tensor_copy(head_columns(slot, 1 + DH), rest).then_inc(v2_done, 1)
                pool.wait_ge(v2_done, count + 1)
                nc.gpsimd.tensor_tensor(head_columns(slot, 1 + 2 * DH), rest, head_columns(slot, 1 + DH),
                                        ALU.subtract).then_inc(v_done, 1)

            def normalise(i, g):
                c, b = g // 2, g % 2
                pool.wait_ge(o_summed, GROUPS * i + g + 1)
                if c != 1:
                    wait(pool, pT_done, rider_count(i - 1 if c == 0 else i, ("oT", (c - 2) % DC, 1)))
                elif not (isinstance(i, int) and i == 0):
                    pool.wait_ge(pT_done, rider_count(i, ("oT", 3, 1)))
                nc.gpsimd.tensor_tensor(o_heads[:, c % 2, b, :].rearrange("p (h d) -> p h d", h=HC),
                                        o_sum[:, g % 2, :].rearrange("p (h d) -> p h d", h=HC),
                                        o_rcp[:, g % 2, :].unsqueeze(2).to_broadcast([P, HC, DH]), ALU.mult
                                        ).then_inc(o_done, 1)

            def add_bias(i, b):
                pool.wait_ge(y_here[b], 16 * (i + 1))
                nc.gpsimd.tensor_tensor(y[:, b, :], y[:, b, :], out_bias[:, :], ALU.add).then_inc(y_biased, 1)

            finish_values(0, 0, HEAD.index(("v", 0)), 0)
            finish_values(0, 1, HEAD.index(("v", 1)), 1)

            def tile(i, par):
                first = isinstance(i, int) and i == 0
                last = isinstance(i, int) and i == NT - 1

                if not first:
                    normalise(i - 1, GROUPS - 1)
                if not last:
                    for r in range(2):
                        inverse_std(pool, nc, stats[:, r, :], minus_half, ln_step[r], 5 * i + 3)
                normalise(i, 0)
                if not first:
                    for b in range(2):
                        add_bias(i - 1, b)
                for g in range(1, 6):
                    normalise(i, g)
                if not last:
                    for r in range(2):
                        finish_values(1 - par, r, job_number(i, ("v", r)), 2 * i + 2 + r)
                normalise(i, 6)

            tiles(pool, tile)
            normalise(NT - 1, GROUPS - 1)
            for b in range(2):
                add_bias(NT - 1, b)

        @block.scalar
        def _(act):
            def qk_hi(i, c, number, bank):
                r = c % 2
                act.wait_ge(job_filled, number + 1)
                for h in range(HC):
                    wait(act, stacked[h][r], 48 * (2 * i + c // 2))
                nc.scalar.activation(qk_parts[:, r, 0, :], job_ps[:, bank, 0:T], ACT.Identity,
                                     bias=qk_bias[:, c:c + 1], scale=1.0)
                nc.scalar.activation(qk_parts[:, r, 2, :], job_ps[:, bank, T:2 * T], ACT.Identity,
                                     bias=qk_bias[:, DC + c:DC + c + 1], scale=1.0).then_inc(hi_done, 1)

            def v1(i, parity, r, number, bank):
                act.wait_ge(job_filled, number + 1)
                wait(act, pv_done, STEPS * (i - 1))
                nc.scalar.copy(head_columns(values[:, parity, 2 + r, :, :], 1),
                               job_ps[:, bank, :].rearrange("p (h d) -> p h d", h=H)).then_inc(hi_done, 1)

            def exp(i, s):
                _, b, _ = where(s)
                w0, w1 = window(i, s)
                n, r = STEPS * i + s, s % 2
                cols = slice((w0 - b) * P, (w1 - b) * P)
                act.wait_ge(neg_done, n + 1)
                wait(act, pT_done, n - 1)
                nc.scalar.activation(probs[:, r, cols], neg_scores[:, r, cols], ACT.Exp,
                                     bias=neg_max[:, s % 4:s % 4 + 1], scale=-1.0).then_inc(probs_done, 1)

            def pT_high(i, s, par=0, rider=None):
                _, b, _ = where(s)
                w0, w1 = window(i, s)
                n, r = STEPS * i + s, s % 2
                cols = slice((w0 - b) * P, (w1 - b) * P)
                act.wait_ge(pT_done, n + 1)
                wait(act, pv_done, n - 3)
                last = nc.scalar.copy(pT_hi[:, s % 4, cols], pT_ps[:, r, cols])
                if rider:
                    last = nc.scalar.copy(rider_cells(par, rider)[0], pT_ps[:, r, RIDER_COLS])
                last.then_inc(pT_hi_done, 1)

            def job(i, par, j):
                kind, a = j
                number, bank = job_number(i, j), bank_of(i, j)
                if kind == "qk":
                    qk_hi(i + 1 if a < 2 else i, a, number, bank)
                elif kind == "v":
                    v1(i + 1, 1 - par, a, number, bank)

            def normalise_x(i, r):
                act.wait_ge(ln_step[r], 5 * i + 5)
                nc.scalar.activation(x_in[:, r, :], x_in[:, r, :], ACT.Identity,
                                     bias=stats[:, r, 3:4], scale=stats[:, r, 2:3]).then_inc(xn_done, 1)

            for c in range(2):
                qk_hi(0, c, c, c)
            for b in range(2):
                v1(0, 0, b, 2 + b, b)

            def tile(i, par):
                for s in range(STEPS):
                    exp(i, s)
                    pi, ps = back(i, s, TURN)
                    if exists(pi):
                        pT_high(pi, ps, par, rider_at(i, s))
                    j, part = job_at(i, s)
                    if j and part == PARTS - 1:
                        job(i, par, j)
                    if s in XN_STEPS and ("v", 0) in jobs_of(i):
                        normalise_x(i, XN_STEPS.index(s))

            tiles(act, tile)
            pT_high(NT - 1, STEPS - 1)
            act.wait_ge(pT_done, STEPS * NT + 1)
            nc.scalar.copy(oT_hi[:, DC - 1, :], pT_ps[:, 0, 0:T]).then_inc(pT_hi_done, 1)

        @block.vector
        def _(dve):
            def mask_scale_max(i, s):
                _, b, _ = where(s)
                w0, w1 = window(i, s)
                n, r = STEPS * i + s, s % 2
                cols = slice((w0 - b) * P, (w1 - b) * P)
                dve.wait_ge(scores_done, n + 1)
                wait(dve, probs_done, n - 1)
                settle(dve, ticks)
                nc.vector.tensor_tensor_reduce(out=neg_scores[:, r, cols], in0=score_ps[:, r, cols],
                                               in1=mask[:, cols], scale=-SCORE_SCALE, scalar=3e38, op0=ALU.add,
                                               op1=ALU.min, accum_out=neg_max[:, s % 4:s % 4 + 1]).then_inc(neg_done, 1)

            def pT_low(i, s, par=0, rider=None):
                _, b, _ = where(s)
                w0, w1 = window(i, s)
                n, r = STEPS * i + s, s % 2
                cols = slice((w0 - b) * P, (w1 - b) * P)
                dve.wait_ge(pT_hi_done, n + 1)
                last = nc.vector.tensor_tensor(pT_lo[:, s % 4, cols], pT_ps[:, r, cols], pT_hi[:, s % 4, cols],
                                               ALU.subtract)
                if rider:
                    hi, lo = rider_cells(par, rider)
                    last = nc.vector.tensor_tensor(lo, pT_ps[:, r, RIDER_COLS], hi.bitcast(F32), ALU.subtract)
                last.then_inc(pT_lo_done, 1)

            def fold(i, g):
                n, r = GROUPS * i + g, g % 2
                cols = o_ps[:, r, 0:HC * VW].rearrange("p (h w) -> p h w", h=HC)
                dve.wait_ge(pv_done, HC * (n + 1))
                wait(dve, o_done, n - 1)
                nc.vector.reciprocal(o_rcp[:, r, :].unsqueeze(2), cols[:, :, 0:1])
                nc.vector.tensor_reduce(o_sum[:, r, :].rearrange("p (h d) -> p h d", h=HC),
                                        cols[:, :, 1:VW].rearrange("p h (k d) -> p h d k", k=3),
                                        AX_X, ALU.add).then_inc(o_summed, 1)

            def qk_lo(c, hi_number, bank):
                r = c % 2
                dve.wait_ge(hi_done, hi_number + 1)
                nc.vector.scalar_tensor_tensor(qk_parts[:, r, 1, :], job_ps[:, bank, 0:T], qk_bias[:, c:c + 1],
                                               qk_parts[:, r, 0, :].bitcast(F32), ALU.add, ALU.subtract)
                nc.vector.scalar_tensor_tensor(qk_parts[:, r, 3, :], job_ps[:, bank, T:2 * T],
                                               qk_bias[:, DC + c:DC + c + 1], qk_parts[:, r, 2, :].bitcast(F32),
                                               ALU.add, ALU.subtract).then_inc(job_freed, 1)

            def v_remainder(parity, r, hi_number, bank, count):
                dve.wait_ge(hi_done, hi_number + 1)
                wait(dve, v_done, count - 1)
                nc.vector.tensor_tensor(v_rest[:, r, :].rearrange("p (h d) -> p h d", h=H),
                                        job_ps[:, bank, :].rearrange("p (h d) -> p h d", h=H),
                                        head_columns(values[:, parity, 2 + r, :, :], 1), ALU.subtract
                                        ).then_inc(job_freed, 1)

            def job(i, par, j):
                kind, a = j
                bank = bank_of(i, j)
                if kind == "qk":
                    qk_lo(a, split_number(i, j), bank)
                elif kind == "v":
                    v_remainder(1 - par, a, split_number(i, j), bank, 2 * i + 2 + a)
                else:
                    add_out(i - 1, a, job_number(i, j), bank)

            def add_out(i, b, number, bank):
                dve.wait_ge(job_filled, number + 1)
                dve.wait_ge(y_biased, 2 * i + b + 1)
                nc.vector.tensor_tensor(y[:, b, :], job_ps[:, bank, :], y[:, b, :], ALU.add).then_inc(job_freed, 1)

            def layernorm(i, r, stage):
                if stage == 0:
                    dve.wait_ge(x_here[r], 16 * (i + 1))
                    nc.vector.bn_stats(bn[:, r, :], x_in[:, r, :]).then_inc(ln_step[r], 1)
                    return
                dve.wait_ge(ln_step[r], 5 * i + (stage if stage < 3 else 4))
                if stage == 1:
                    settle(dve, ticks)
                    nc.vector.bn_aggr(stats[:, r, 0:2], bn[:, r, :]).then_inc(ln_step[r], 1)
                elif stage == 2:
                    nc.vector.tensor_scalar(stats[:, r, 1:2], stats[:, r, 1:2], EPS, None, ALU.add
                                            ).then_inc(ln_step[r], 1)
                else:
                    nc.vector.scalar_tensor_tensor(stats[:, r, 3:4], stats[:, r, 0:1], -1.0, stats[:, r, 2:3],
                                                   ALU.mult, ALU.mult).then_inc(ln_step[r], 1)

            for c in range(2):
                qk_lo(c, c, c)
            for b in range(2):
                v_remainder(0, b, 2 + b, b, b)

            def tile(i, par):
                for s in range(STEPS):
                    mask_scale_max(i, s)
                    pi, ps = back(i, s, LOW)
                    if exists(pi):
                        ri, rs = back(i, s, LOW - TURN)
                        pT_low(pi, ps, parity_back(par, s, LOW - TURN), rider_at(ri, rs))
                    gi, gs = back(i, s, FOLD)
                    if exists(gi) and gs % HC == HC - 1:
                        fold(gi, gs // HC)
                    if ("v", 0) in jobs_of(i):
                        for r, stage in LN_STEPS.get(s, ()):
                            layernorm(i, r, stage)
                    if s == CARRY_STEP and ("v", 0) in jobs_of(i):
                        dve.wait_ge(v_done, 2 * i + 2)
                        wait(dve, pv_done, STEPS * i)
                        nc.vector.tensor_copy(values[:, 1 - par, 0:2, :, :], values[:, par, 2:4, :, :]
                                              ).then_inc(v_carried, 1)
                    ji, js = back(i, s, JOB_LAG)
                    j, part = job_at(ji, js) if exists(ji) else (None, 0)
                    if j and part == PARTS - 1:
                        job(ji, parity_back(par, s, JOB_LAG), j)

            tiles(dve, tile)
            end, par = NT - 1, (NT - 1) % 2
            pT_low(end, STEPS - 2, par, rider_at(end, STEPS - 1))
            pT_low(end, STEPS - 1)
            fold(end, GROUPS - 1)
            dve.wait_ge(pT_hi_done, STEPS * NT + 1)
            nc.vector.tensor_tensor(oT_lo[:, DC - 1, :], pT_ps[:, 0, 0:T], oT_hi[:, DC - 1, :].bitcast(F32),
                                    ALU.subtract).then_inc(pT_lo_done, 1)
            for b in range(2):
                add_out(end, b, tail_number(("out", b)), b)

        @block.tensor
        def _(pe):
            def scores(i, par, s):
                c, b, h = where(s)
                w0, w1 = window(i, s)
                n = STEPS * i + s
                if b == 0:
                    pe.wait_ge(stacked[h][c % 2], 48 * (2 * i + c // 2 + 1))
                wait(pe, neg_done, n - 1)
                keys = stack[c][:, h, 1:3, :].rearrange("p a t -> p (a t)")
                for w, half, blk, count in key_runs(par, b, w0, w1):
                    at = half * T + blk * P
                    last = nc.tensor.matmul(score_ps[:, s % 2, (w - b) * P:(w - b + count) * P], q_cols(par, c, h, b),
                                            keys[:, at:at + count * P], start=True, stop=True)
                last.then_inc(scores_done, 1)

            def transpose_probs(i, s, ti=0, rider=None):
                _, b, _ = where(s)
                w0, w1 = window(i, s)
                n, r = STEPS * i + s, s % 2
                wait(pe, pT_lo_done, n - 1)
                if rider:
                    kind, c, rb = rider
                    if kind == "oT":
                        pe.wait_ge(o_done, GROUPS * (ti - 1 if c == DC - 1 else ti) + 2 * c + rb + 1)
                        in_ = o_heads[:, c % 2, rb, :]
                    else:
                        pe.wait_ge(xn_done, 2 * ti + rb + 1)
                        in_ = x_in[:, rb, c * P:(c + 1) * P]
                    nc.tensor.transpose(pT_ps[:, r, RIDER_COLS], in_, ident[:, :])
                pe.wait_ge(probs_done, n + 1)
                for w in range(w0 - b, w1 - b):
                    last = nc.tensor.transpose(pT_ps[:, r, w * P:(w + 1) * P], probs[:, r, w * P:(w + 1) * P],
                                               ident[:, :])
                last.then_inc(pT_done, 1)

            def probs_times_values(i, par, s):
                c, b, h = where(s)
                w0, w1 = window(i, s)
                n, r, g = STEPS * i + s, s % 4, s // HC
                pe.wait_ge(pT_lo_done, n + 1)
                if h == 0:
                    wait(pe, o_summed, GROUPS * i + g - 1)
                if s == 0:
                    wait(pe, v_carried, i)
                    pe.wait_ge(v_done, 2 * i + 1)
                if s == HC:
                    pe.wait_ge(v_done, 2 * i + 2)
                col = h * VW
                for w in range(w0, w1):
                    t = slice((w - b) * P, (w - b + 1) * P)
                    v = values[:, par, w, c * HC + h, :]
                    nc.tensor.matmul(o_ps[:, g % 2, col:col + VW], pT_hi[:, r, t], v,
                                     start=(w == w0), stop=False)
                    last = nc.tensor.matmul(o_ps[:, g % 2, col:col + 1 + 2 * DH], pT_lo[:, r, t], v[:, 0:1 + 2 * DH],
                                            start=False, stop=(w == w1 - 1))
                last.then_inc(pv_done, 1)

            def project_out(bank, b, part):
                for n in range(part * 3, part * 3 + 3):
                    k, pass_ = divmod(n, 3)
                    w = wout_lo if pass_ == 2 else wout_hi
                    a = oT_lo if pass_ == 1 else oT_hi
                    last = nc.tensor.matmul(job_ps[:, bank, :], a[:, k, b * P:(b + 1) * P], w[:, k, :],
                                            start=(n == 0), stop=(n == 3 * DC - 1))
                return last

            def job_part(i, par, j, part):
                kind, a = j
                number, bank = job_number(i, j), bank_of(i, j)
                if part == 0:
                    pe.wait_ge(job_freed, number - 1)
                if kind == "qk":
                    if a == 0 and part < 2:
                        pe.wait_ge(pT_lo_done, rider_count(i, ("x", 2 * part + 1, 1)))
                    last = pe_project_qk(bank, 1 - par if a < 2 else par, a, part)
                elif kind == "v":
                    last = pe_project_v(bank, 1 - par, a, part)
                else:
                    if a == 0 and part == 0:
                        pe.wait_ge(pT_lo_done, rider_count(i - 1, ("oT", 2, 1)))
                    if a == 0 and part == PARTS - 1:
                        pe.wait_ge(pT_lo_done, rider_count(i, ("oT", 3, 1)))
                    last = project_out(bank, a, part)
                if part == PARTS - 1:
                    last.then_inc(job_filled, 1)

            for c in range(2):
                for part in range(PARTS):
                    last = pe_project_qk(c, 0, c, part)
                last.then_inc(job_filled, 1)
            for b in range(2):
                pe.wait_ge(job_freed, b + 1)
                for part in range(PARTS):
                    last = pe_project_v(b, 0, b, part)
                last.then_inc(job_filled, 1)

            def tile(i, par):
                for s in range(STEPS):
                    scores(i, par, s)
                    j, part = job_at(i, s)
                    if j:
                        job_part(i, par, j, part)
                    pi, ps = back(i, s, TURN)
                    if exists(pi):
                        transpose_probs(pi, ps, i, rider_at(i, s))
                    vi, vs = back(i, s, PV)
                    if exists(vi):
                        probs_times_values(vi, parity_back(par, s, PV), vs)

            tiles(pe, tile)
            end, par = NT - 1, (NT - 1) % 2
            transpose_probs(end, STEPS - 1)
            for s in range(STEPS - PV, STEPS):
                probs_times_values(end, par, s)
            pe.wait_ge(pT_lo_done, STEPS * NT)
            pe.wait_ge(o_done, GROUPS * NT)
            for b in range(2):
                last = nc.tensor.transpose(pT_ps[:, 0, b * P:(b + 1) * P], o_heads[:, (DC - 1) % 2, b, :], ident[:, :])
            last.then_inc(pT_done, 1)
            for b in range(2):
                pe.wait_ge(job_freed, tail_number(("out", b)) - 1)
                for part in range(PARTS):
                    if b == 0 and part == PARTS - 1:
                        pe.wait_ge(pT_lo_done, STEPS * NT + 1)
                    last = project_out(b, b, part)
                last.then_inc(job_filled, 1)



def prepare_feed_forward(nc, fast_b, w_fc, w_proj, u, v, gate, ident, fc_T, proj_T, fc_scale2, proj_scale,
                         low_in_hi, low_in_lo, low_out):
    F = w_fc.shape[0]
    FB = F // P
    R = v.shape[0]
    COLS = F // D
    UNITS = FB + DC * COLS
    with ExitStack() as ctx:
        def sb(name, shape, dt=F32):
            return ctx.enter_context(nc.sbuf_tensor(name, shape, dt))

        def sem(name):
            return ctx.enter_context(nc.semaphore(name))

        fc_in = sb("fc_in", [P, 4, D])
        proj_in = sb("proj_in", [P, 2, F])
        abs_sum = sb("abs_sum", [P, FB + DC])
        scale = sb("scale", [P, FB + DC])
        inv_scale = sb("inv_scale", [P, FB + DC])
        neg_round = sb("neg_round", [P, 1])
        ones = sb("ones", [P, P])
        diagonal = sb("diagonal", [P, DC, P])
        gate_wide = sb("gate_wide", [P, 1])
        v_in = sb("v_in", [R, D])
        fast_T = sb("fast_T", [R, R])
        u_in = sb("u_in", [P, FB, R])
        u_wide = sb("u_wide", [P, FB, 3 * DH])
        turn_ps = ctx.enter_context(nc.psum_tensor("turn_ps", [P, 4, D], F32))
        scale_ps = ctx.enter_context(nc.psum_tensor("scale_ps", [P, D], F32))
        low_ps = ctx.enter_context(nc.psum_tensor("low_ps", [P, DC * R], F32))

        fc_here = [sem(f"fc_here{n}") for n in range(4)]
        proj_here = [sem(f"proj_here{n}") for n in range(2)]
        small_here = sem("small_here")
        zeroed, ident_done, consts_set = sem("f_ident_zeroed"), sem("f_ident_done"), sem("f_consts_set")
        quant_step = sem("quant_step")
        turned, copied = sem("turned"), sem("copied")
        diag_done, scale_summed, low_summed, low_hi_done, prep_done = (
            sem("diag_done"), sem("scale_summed"), sem("low_summed"), sem("low_hi_done"), sem("prep_done"))
        u_done, u_turned, u_copied = sem("u_done"), sem("u_turned"), sem("u_copied")
        block = ctx.enter_context(nc.Block())

        @block.sync
        def _(sp):
            for n in range(FB):
                if n >= 4:
                    sp.wait_ge(turned, n - 3)
                sp.dma_start(fc_in[:, n % 4, :], w_fc[n * P:(n + 1) * P, :]).then_inc(fc_here[n % 4], 16)
            for n in range(DC):
                if n >= 2:
                    sp.wait_ge(turned, FB + COLS * (n - 1))
                sp.dma_start(proj_in[:, n % 2, :], w_proj[n * P:(n + 1) * P, :]).then_inc(proj_here[n % 2], 16)

        @block.gpsimd
        def _(pool):
            pool.dma_start(v_in[:, :], v).then_inc(small_here, 16)
            pool.dma_start(u_in[:, :, :], u.rearrange("(n p) r -> p n r", p=P)).then_inc(small_here, 16)
            pool.dma_start(gate_wide[:, :], gate.partition_broadcast(P)).then_inc(small_here, 16)
            with nc.allow_non_contiguous_dma("a 16 x 16 matrix, once"):
                pool.dma_start(fast_T[:, :], fast_b.rearrange("a b -> b a")).then_inc(small_here, 16)
            identity_on_pool(pool, nc, ident, zeroed, ident_done)
            nc.gpsimd.memset(neg_round[:, :], -ROUND)
            nc.gpsimd.memset(ones[:, :], 1.0)
            nc.gpsimd.memset(u_wide[:, :, :], 0.0)
            nc.gpsimd.memset(low_in_hi.bitcast(F32), 0.0)
            nc.gpsimd.memset(low_in_lo.bitcast(F32), 0.0).then_inc(consts_set, 1)

        @block.vector
        def _(dve):
            step = 0
            dve.wait_ge(consts_set, 1)
            dve.wait_ge(ident_done, 1)
            for n in range(FB + DC):
                if n < FB:
                    w, width = fc_in[:, n % 4, :], D
                    dve.wait_ge(fc_here[n % 4], 16 * (n // 4 + 1))
                else:
                    w, width = proj_in[:, n % 2, :], F
                    dve.wait_ge(proj_here[n % 2], 16 * ((n - FB) // 2 + 1))
                nc.vector.tensor_reduce(abs_sum[:, n:n + 1], w, AX_X, ALU.add, apply_absolute_value=True
                                        ).then_inc(quant_step, 1)
                dve.wait_ge(quant_step, step + 1)
                nc.vector.tensor_scalar(scale[:, n:n + 1], abs_sum[:, n:n + 1], 1.0 / width, MIN_SCALE,
                                        ALU.mult, ALU.max).then_inc(quant_step, 1)
                dve.wait_ge(quant_step, step + 2)
                nc.vector.reciprocal(inv_scale[:, n:n + 1], scale[:, n:n + 1]).then_inc(quant_step, 1)
                dve.wait_ge(quant_step, step + 3)
                nc.vector.tensor_scalar(w, w, inv_scale[:, n:n + 1], 1.0, ALU.mult, ALU.min).then_inc(quant_step, 1)
                dve.wait_ge(quant_step, step + 4)
                nc.vector.tensor_scalar(w, w, -1.0, ROUND, ALU.max, ALU.add).then_inc(quant_step, 1)
                step += 5
            nc.vector.tensor_tensor(fc_scale2[:, :], scale[:, 0:FB], scale[:, 0:FB], ALU.mult)
            for c in range(DC):
                last = nc.vector.tensor_scalar(diagonal[:, c, :], ident[:, :], scale[:, FB + c:FB + c + 1], None,
                                               ALU.mult)
            last.then_inc(diag_done, 1)
            dve.wait_ge(small_here, 64)
            for rep in range(3):
                for n in range(FB):
                    last = nc.vector.tensor_scalar(u_wide[:, n, rep * DH:rep * DH + R], u_in[:, n, :],
                                                   gate_wide[:, 0:1], inv_scale[:, n:n + 1], ALU.mult, ALU.mult)
            last.then_inc(u_done, 1)
            dve.wait_ge(scale_summed, 1)
            nc.vector.tensor_copy(proj_scale[:, :], scale_ps[:, :])
            dve.wait_ge(low_hi_done, 3)
            for rep in range(3):
                nc.vector.tensor_tensor(low_in_lo[:, :, rep * DH:rep * DH + R],
                                        low_ps[:, :].rearrange("p (c r) -> p c r", c=DC),
                                        low_in_hi[:, :, rep * DH:rep * DH + R].bitcast(F32), ALU.subtract)
            lo = slice(2 * DH, 3 * DH)
            for n in range(FB // 4):
                dve.wait_ge(u_copied, n + 1)
                cols = slice(n * D, (n + 1) * D)
                nc.vector.tensor_tensor(low_out[lo, cols], turn_ps[lo, n, :], low_out[lo, cols].bitcast(F32),
                                        ALU.subtract).then_inc(prep_done, 1)

        @block.tensor
        def _(pe):
            pe.wait_ge(ident_done, 1)
            for n in range(UNITS):
                if n < FB:
                    blk, first, src = n, 0, fc_in[:, n % 4, :]
                else:
                    blk, first = FB + (n - FB) // COLS, (n - FB) % COLS * D
                    src = proj_in[:, blk % 2, :]
                pe.wait_ge(quant_step, 5 * (blk + 1))
                if n >= 4:
                    pe.wait_ge(copied, n - 3)
                for k in range(DC):
                    last = nc.tensor.transpose(turn_ps[:, n % 4, k * P:(k + 1) * P],
                                               src[:, first + k * P:first + (k + 1) * P], ident[:, :])
                last.then_inc(turned, 1)
            pe.wait_ge(diag_done, 1)
            for c in range(DC):
                last = nc.tensor.matmul(scale_ps[:, c * P:(c + 1) * P], ones[:, :], diagonal[:, c, :],
                                        start=True, stop=True)
            last.then_inc(scale_summed, 1)
            pe.wait_ge(u_done, 1)
            for c in range(DC):
                last = nc.tensor.matmul(low_ps[:, c * R:(c + 1) * R], v_in[:, c * P:(c + 1) * P], fast_T[:, :],
                                        start=True, stop=True)
            last.then_inc(low_summed, 1)
            pe.wait_ge(copied, UNITS)
            for n in range(FB):
                last = nc.tensor.transpose(turn_ps[0:3 * DH, n // 4, n % 4 * P:(n % 4 + 1) * P], u_wide[:, n, :],
                                           ident[:, :])
                if n % 4 == 3:
                    last.then_inc(u_turned, 1)

        @block.scalar
        def _(act):
            act.wait_ge(consts_set, 1)
            for n in range(UNITS):
                act.wait_ge(turned, n + 1)
                if n < FB:
                    dst = fc_T[:, :, n * P:(n + 1) * P]
                else:
                    c, g = divmod(n - FB, COLS)
                    dst = proj_T[:, g * 4:g * 4 + 4, c * P:(c + 1) * P]
                nc.scalar.activation(dst, turn_ps[:, n % 4, :].rearrange("p (k t) -> p k t", k=4), ACT.Identity,
                                     bias=neg_round[:, 0:1], scale=1.0).then_inc(copied, 1)
            act.wait_ge(low_summed, 1)
            for rep in range(3):
                nc.scalar.copy(low_in_hi[:, :, rep * DH:rep * DH + R],
                               low_ps[:, :].rearrange("p (c r) -> p c r", c=DC)).then_inc(low_hi_done, 1)
            for n in range(FB // 4):
                act.wait_ge(u_turned, n + 1)
                nc.scalar.copy(low_out[:, n * D:(n + 1) * D], turn_ps[0:3 * DH, n, :]).then_inc(u_copied, 1)


def feed_forward(nc, x, partial, fast_b, w_fc, w_proj, u, v, gate, out):
    F = w_fc.shape[0]
    FB = F // P
    NB = D // P
    T = NB * P
    NT = x.shape[0] // T
    LAG = 2
    assert FB % 2 == 0 and NT % 2 == 0
    with ExitStack() as ctx:
        def sb(name, shape, dt=F32):
            return ctx.enter_context(nc.sbuf_tensor(name, shape, dt))

        def sem(name):
            return ctx.enter_context(nc.semaphore(name))

        ident = sb("f_ident", [P, P])
        fc_T = sb("fc_T", [P, DC, F], F32R)
        proj_T = sb("proj_T", [P, FB, D], F32R)
        fc_scale2 = sb("fc_scale2", [P, FB])
        proj_scale = sb("proj_scale", [P, D])
        low_in_hi = sb("low_in_hi", [P, DC, 3 * DH], F32R)
        low_in_lo = sb("low_in_lo", [P, DC, 3 * DH], F32R)
        low_out = sb("low_out", [3 * DH, F], F32R)
        prepare_feed_forward(nc, fast_b, w_fc, w_proj, u, v, gate, ident, fc_T, proj_T, fc_scale2, proj_scale,
                             low_in_hi[:, :, :], low_in_lo[:, :, :], low_out)

        x_in = sb("f_x_in", [P, NB, D])
        xn = sb("f_xn", [P, 2, D])
        bn = sb("f_bn", [P, NB, 6])
        minus_half = sb("f_minus_half", [P, 1])
        stats = sb("f_stats", [P, NB, 4])
        xT_hi = sb("f_xT_hi", [P, 2, DC, T], F32R)
        xT_lo = sb("f_xT_lo", [P, 2, DC, T], F32R)
        low = sb("low", [3 * DH, 2, T], F32R)
        relu = sb("relu", [P, 2, T])
        sq = sb("sq", [P, 2, T])
        sq_hi = sb("sq_hi", [P, 2, T], F32R)
        sq_lo = sb("sq_lo", [P, 2, T], F32R)
        part_in = sb("part_in", [P, NB, D])
        y = sb("f_y", [P, NB, D])
        up_ps = ctx.enter_context(nc.psum_tensor("up_ps", [P, 2, T], F32))
        down_ps = ctx.enter_context(nc.psum_tensor("down_ps", [P, NB, D], F32))
        turn_ps = ctx.enter_context(nc.psum_tensor("x_turn_ps", [P, DC * P], F32))
        low_ps = ctx.enter_context(nc.psum_tensor("low_act_ps", [3 * DH, T], F32))

        x_here = [sem(f"f_x_here{b}") for b in range(NB)]
        part_here = [sem(f"part_here{b}") for b in range(NB)]
        ln_step, xn_done, x_turned, xT_hi_done, xT_done = (
            sem("f_ln_step"), sem("f_xn_done"), sem("x_turned"), sem("f_xT_hi_done"), sem("f_xT_done"))
        half_set = sem("half_set")
        ticks = {e: sem(f"f_ticks_{n}") for n, e in (("dve", nc.vector.engine), ("sp", nc.sync.engine))}
        low_filled, low_hi_done, low_done = sem("low_filled"), sem("low_act_hi_done"), sem("low_done")
        up_done, relu_done, sq_done, sq_hi_done, sq_lo_done, down_done = (
            sem("up_done"), sem("relu_done"), sem("sq_done"), sem("sq_hi_done"), sem("sq_lo_done"), sem("down_done"))
        down_taken, y_done = sem("down_taken"), sem("f_y_done")
        stored = [sem(f"stored{b}") for b in range(NB)]
        block = ctx.enter_context(nc.Block())

        TURN_STEP = [4, 6, 8, 10]
        LOW_STEP = 13

        def tiles(eng, tile):
            tile(0, 0)
            with eng.Fori(0, (NT - 2) // 2) as pair:
                for n in range(2):
                    tile(2 * pair + 1 + n, (1 + n) % 2)
            tile(NT - 1, (NT - 1) % 2)

        def is_last(i):
            return isinstance(i, int) and i == NT - 1

        def back(i, s, n):
            return (i, s - n) if s >= n else (i - 1, s - n + FB)

        def exists(i):
            return not (isinstance(i, int) and i < 0)

        @block.sync
        def _(sp):
            def load_x(i):
                for b in range(NB):
                    wait(sp, xn_done, NB * (i - 1) + b + 1)
                    settle(sp, ticks)
                    sp.dma_start(x_in[:, b, :], block_rows(x, NB * i + b)).then_inc(x_here[b], 16)

            for b in range(NB):
                sp.sem_inc(stored[b], 16)
            load_x(0)

            def tile(i, par):
                if not is_last(i):
                    load_x(i + 1)
                if not (isinstance(i, int) and i == 0):
                    for b in range(NB):
                        sp.wait_ge(y_done, NB * (i - 1) + b + 1)
                        settle(sp, ticks)
                        sp.dma_start(block_rows(out, NB * (i - 1) + b), y[:, b, :]).then_inc(stored[b], 16)
                for b in range(NB):
                    sp.dma_start(part_in[:, b, :], block_rows(partial, NB * i + b)).then_inc(part_here[b], 16)

            tiles(sp, tile)
            for b in range(NB):
                sp.wait_ge(y_done, NB * (NT - 1) + b + 1)
                sp.dma_start(block_rows(out, NB * (NT - 1) + b), y[:, b, :]).then_inc(stored[b], 16)
            for b in range(NB):
                sp.wait_ge(stored[b], 16 * (NT + 1))

        @block.gpsimd
        def _(pool):
            nc.gpsimd.memset(minus_half[:, :], -0.5).then_inc(half_set, 1)
            pool.wait_ge(half_set, 1)
            for b in range(NB):
                inverse_std(pool, nc, stats[:, b, :], minus_half, ln_step, 5 * b + 3)

            def tile(i, par):
                if not is_last(i):
                    for b in range(NB):
                        inverse_std(pool, nc, stats[:, b, :], minus_half, ln_step, 5 * (NB * (i + 1) + b) + 3)
                for b in range(NB):
                    pool.wait_ge(down_taken, NB * i + b + 1)
                    pool.wait_ge(part_here[b], 16 * (i + 1))
                    nc.gpsimd.tensor_tensor(y[:, b, :], y[:, b, :], part_in[:, b, :], ALU.add).then_inc(y_done, 1)

            tiles(pool, tile)

        @block.scalar
        def _(act):
            def normalise(i, b):
                act.wait_ge(ln_step, 5 * (NB * i + b) + 5)
                wait(act, x_turned, NB * i + b - 1)
                nc.scalar.activation(xn[:, b % 2, :], x_in[:, b, :], ACT.Identity, bias=stats[:, b, 3:4],
                                     scale=stats[:, b, 2:3]).then_inc(xn_done, 1)

            def xT_high(i, par, b):
                act.wait_ge(x_turned, NB * i + b + 1)
                nc.scalar.copy(xT_hi[:, par, :, b * P:(b + 1) * P], turn_ps[:, :].rearrange("p (c t) -> p c t", c=DC)
                               ).then_inc(xT_hi_done, 1)

            def low_high(i, par):
                act.wait_ge(low_filled, i + 1)
                nc.scalar.copy(low[:, par, :], low_ps[:, :]).then_inc(low_hi_done, 1)

            for b in range(NB):
                normalise(0, b)
                xT_high(0, 0, b)
            low_high(0, 0)

            def square_hi(i, s):
                n = FB * i + s
                act.wait_ge(sq_done, n + 1)
                wait(act, down_done, n - 1)
                nc.scalar.copy(sq_hi[:, s % 2, :], sq[:, s % 2, :]).then_inc(sq_hi_done, 1)

            def tile(i, par):
                for s in range(FB):
                    n = FB * i + s
                    act.wait_ge(up_done, n + 1)
                    wait(act, sq_done, n - 1)
                    nc.scalar.activation(relu[:, s % 2, :], up_ps[:, s % 2, :], ACT.Relu,
                                         scale=fc_scale2[:, s:s + 1]).then_inc(relu_done, 1)
                    pi, ps = back(i, s, 1)
                    if exists(pi):
                        square_hi(pi, ps)
                    if not is_last(i):
                        for b in range(NB):
                            if s == TURN_STEP[b] - 1:
                                normalise(i + 1, b)
                            if s == TURN_STEP[b]:
                                xT_high(i + 1, 1 - par, b)
                        if s == LOW_STEP:
                            low_high(i + 1, 1 - par)

            tiles(act, tile)
            square_hi(NT - 1, FB - 1)

        @block.vector
        def _(dve):
            def layernorm(i, b):
                n = 5 * (NB * i + b)
                dve.wait_ge(x_here[b], 16 * (i + 1))
                nc.vector.bn_stats(bn[:, b, :], x_in[:, b, :]).then_inc(ln_step, 1)
                dve.wait_ge(ln_step, n + 1)
                settle(dve, ticks)
                nc.vector.bn_aggr(stats[:, b, 0:2], bn[:, b, :]).then_inc(ln_step, 1)
                dve.wait_ge(ln_step, n + 2)
                nc.vector.tensor_scalar(stats[:, b, 1:2], stats[:, b, 1:2], EPS, None, ALU.add).then_inc(ln_step, 1)
                dve.wait_ge(ln_step, n + 4)
                nc.vector.scalar_tensor_tensor(stats[:, b, 3:4], stats[:, b, 0:1], -1.0, stats[:, b, 2:3],
                                               ALU.mult, ALU.mult).then_inc(ln_step, 1)

            def xT_low(i, par, b):
                dve.wait_ge(xT_hi_done, NB * i + b + 1)
                cols = slice(b * P, (b + 1) * P)
                nc.vector.tensor_tensor(xT_lo[:, par, :, cols], turn_ps[:, :].rearrange("p (c t) -> p c t", c=DC),
                                        xT_hi[:, par, :, cols].bitcast(F32), ALU.subtract).then_inc(xT_done, 1)

            def low_low(i, par):
                dve.wait_ge(low_hi_done, i + 1)
                rows = slice(DH, 2 * DH)
                nc.vector.tensor_tensor(low[rows, par, :], low_ps[rows, :], low[rows, par, :].bitcast(F32),
                                        ALU.subtract).then_inc(low_done, 1)

            for b in range(NB):
                layernorm(0, b)
                xT_low(0, 0, b)
            low_low(0, 0)

            def square_lo(i, s):
                dve.wait_ge(sq_hi_done, FB * i + s + 1)
                nc.vector.tensor_tensor(sq_lo[:, s % 2, :], sq[:, s % 2, :], sq_hi[:, s % 2, :].bitcast(F32),
                                        ALU.subtract).then_inc(sq_lo_done, 1)

            def take_down(i):
                for b in range(NB):
                    if b == 0:
                        dve.wait_ge(down_done, FB * (i + 1))
                    dve.wait_ge(stored[b], 16 * (i + 1))
                    nc.vector.tensor_tensor(y[:, b, :], down_ps[:, b, :], proj_scale[:, :], ALU.mult
                                            ).then_inc(down_taken, 1)

            def tile(i, par):
                for s in range(FB):
                    n = FB * i + s
                    dve.wait_ge(relu_done, n + 1)
                    wait(dve, sq_lo_done, n - 1)
                    nc.vector.scalar_tensor_tensor(sq[:, s % 2, :], up_ps[:, s % 2, :], 0.0, relu[:, s % 2, :],
                                                   ALU.max, ALU.mult).then_inc(sq_done, 1)
                    pi, ps = back(i, s, 1)
                    if exists(pi):
                        square_lo(pi, ps)
                    if s == LAG - 1 and not (isinstance(i, int) and i == 0):
                        take_down(i - 1)
                    if not is_last(i):
                        for b in range(NB):
                            if s == TURN_STEP[b] - 2:
                                layernorm(i + 1, b)
                            if s == TURN_STEP[b]:
                                xT_low(i + 1, 1 - par, b)
                        if s == LOW_STEP:
                            low_low(i + 1, 1 - par)

            tiles(dve, tile)
            square_lo(NT - 1, FB - 1)
            take_down(NT - 1)

        @block.tensor
        def _(pe):
            def turn_x(i, b):
                n = NB * i + b
                pe.wait_ge(xn_done, n + 1)
                wait(pe, xT_done, n)
                for k in range(DC):
                    last = nc.tensor.transpose(turn_ps[:, k * P:(k + 1) * P], xn[:, b % 2, k * P:(k + 1) * P],
                                               ident[:, :])
                last.then_inc(x_turned, 1)

            def low_rank(i, par):
                pe.wait_ge(xT_done, NB * (i + 1))
                wait(pe, low_done, i)
                for n in range(3 * DC):
                    k, pass_ = divmod(n, 3)
                    w = low_in_lo if pass_ == 2 else low_in_hi
                    a = xT_lo if pass_ == 1 else xT_hi
                    last = nc.tensor.matmul(low_ps[:, :], w[:, k, :], a[:, par, k, :],
                                            start=(n == 0), stop=(n == 3 * DC - 1))
                last.then_inc(low_filled, 1)

            def up(i, par, s):
                n = FB * i + s
                cols = slice(s * P, (s + 1) * P)
                if s == 0:
                    pe.wait_ge(low_done, i + 1)
                wait(pe, sq_done, n - 1)
                for k in range(DC):
                    nc.tensor.matmul(up_ps[:, s % 2, :], fc_T[:, k, cols], xT_hi[:, par, k, :],
                                     start=(k == 0), stop=False)
                    nc.tensor.matmul(up_ps[:, s % 2, :], fc_T[:, k, cols], xT_lo[:, par, k, :],
                                     start=False, stop=False)
                nc.tensor.matmul(up_ps[:, s % 2, :], low_out[:, cols], low[:, par, :],
                                 start=False, stop=True).then_inc(up_done, 1)

            def down(i, s):
                n = FB * i + s
                pe.wait_ge(sq_lo_done, n + 1)
                for b in range(NB):
                    if s == 0:
                        wait(pe, down_taken, NB * (i - 1) + b + 1)
                    t = slice(b * P, (b + 1) * P)
                    nc.tensor.matmul(down_ps[:, b, :], sq_hi[:, s % 2, t], proj_T[:, s, :],
                                     start=(s == 0), stop=False)
                    last = nc.tensor.matmul(down_ps[:, b, :], sq_lo[:, s % 2, t], proj_T[:, s, :],
                                            start=False, stop=(s == FB - 1))
                last.then_inc(down_done, 1)

            for b in range(NB):
                turn_x(0, b)
            low_rank(0, 0)

            def tile(i, par):
                for s in range(FB):
                    up(i, par, s)
                    if not is_last(i):
                        if s in TURN_STEP:
                            turn_x(i + 1, TURN_STEP.index(s))
                        if s == LOW_STEP:
                            low_rank(i + 1, 1 - par)
                    di, ds = back(i, s, LAG)
                    if exists(di):
                        down(di, ds)

            tiles(pe, tile)
            for s in range(FB - LAG, FB):
                down(NT - 1, s)


_INS = ["L0_attn_x", "L0_attn_Wqkv", "L0_attn_bqkv", "L0_attn_Wout", "L0_attn_bout", "L0_ffn_fast_b", "L0_ffn_w_fc",
        "L0_ffn_w_proj", "L0_ffn_u", "L0_ffn_v", "L0_ffn_gate"]


def build(nc, x, Wqkv, bqkv, Wout, bout, fast_b, w_fc, w_proj, u, v, gate, out):
    rows = x.rearrange("b s d -> (b s) d")
    partial = nc.dram_tensor("partial", rows.shape, F32, kind="Internal").ap()
    attention(nc, rows, Wqkv, bqkv, Wout, bout, partial)
    feed_forward(nc, rows, partial, fast_b, w_fc, w_proj, u, v, gate, out.rearrange("b s d -> (b s) d"))


def kernel(**inputs):
    import numpy as np
    import concourse.bacc as bacc
    from concourse import mybir as mb
    from concourse.bass_utils import run_bass_kernel_spmd

    nc = bacc.Bacc("TRN2", target_bir_lowering=False, num_devices=1)
    arrays, args = {}, []
    for name in _INS:
        a = np.ascontiguousarray(inputs[name])
        if name == "L0_ffn_gate":
            a = a.reshape(1)
        arrays[f"in_{name}"] = a
        args.append(nc.dram_tensor(f"in_{name}", a.shape, mb.dt.from_np(a.dtype), kind="ExternalInput").ap())
    shape = inputs["L0_attn_x"].shape
    args.append(nc.dram_tensor("out", shape, F32, kind="ExternalOutput").ap())
    build(nc, *args)
    r = run_bass_kernel_spmd(nc, [arrays], core_ids=[0])
    return r.results[0]["out"]
```

```python
from contextlib import ExitStack

import concourse.bass as bass
from concourse import mybir

F32 = mybir.dt.float32
F32R = mybir.dt.float32r
BF16 = mybir.dt.bfloat16
F16 = mybir.dt.float16
ALU = mybir.AluOpType
ACT = mybir.ActivationFunctionType
AX_X = mybir.AxisListType.X

P = 128
D = 512
DC = D // P
H = 16
DH = D // H
HC = P // DH
EPS = 1e-5
MIN_SCALE = 1e-5
NEG = -1e30
SCORE_SCALE = 1.0 / float(D) ** 0.5
ROUND = 1.5 * 2.0 ** 23
VW = 1 + 3 * DH


def wait(eng, sem, value):
    if isinstance(value, int) and value <= 0:
        return
    eng.wait_ge(sem, value)


def settle(eng, ticks):
    eng.sem_inc(ticks[eng.engine], 1)


def block_rows(dram, block):
    return dram[bass.ds(block * P, P), :]


def identity_on_pool(pool, nc, ident, zeroed, ready):
    nc.gpsimd.memset(ident[:, :], 0.0).then_inc(zeroed, 1)
    pool.wait_ge(zeroed, 1)
    nc.gpsimd.affine_select(out=ident[:, :], in_=ident[:, :], compare_op=ALU.not_equal, fill=1.0,
                            base=0, pattern=[[-1, P]], channel_multiplier=1).then_inc(ready, 1)


def inverse_std(pool, nc, stats, minus_half, ln_step, value):
    pool.wait_ge(ln_step, value)
    nc.gpsimd.tensor_tensor(stats[:, 2:3], stats[:, 1:2], minus_half[:, :], ALU.pow).then_inc(ln_step, 1)



def prepare_attention(nc, x, Wqkv, bqkv, Wout, bout, wqkv_hi, wqkv_lo, wout_hi, wout_lo, qk_bias, out_bias, ident,
                      minus_half, job_ps, xT_places):
    NX = len(xT_places)
    with ExitStack() as ctx:
        def sb(name, shape):
            return ctx.enter_context(nc.sbuf_tensor(name, shape, F32))

        def sem(name):
            return ctx.enter_context(nc.semaphore(name))

        stage = sb("w_stage", [P, DC, 3 * D])
        wout_raw = sb("wout_raw", [P, DC, D])
        v_bias = sb("v_bias", [P, DC])
        v_bias_wide = sb("v_bias_wide", [P, DC, P])
        bout_wide = sb("bout_wide", [P, D])
        x_in = sb("pro_x", [P, NX, D])
        bn = sb("pro_bn", [P, NX, 6])
        stats = sb("pro_stats", [P, NX, 4])
        bias_ps = ctx.enter_context(nc.psum_tensor("bias_ps", [P, D], F32))
        chunk_in = [sem(f"wqkv_chunk_in{k}") for k in range(DC)]
        wout_in, biases_in = sem("wout_in"), sem("biases_in")
        hi_done, lo_done = sem("w_hi_done"), sem("w_lo_done")
        wide_done, bias_summed = sem("v_bias_wide_done"), sem("bias_summed")
        zeroed, ident_done, half_set = sem("ident_zeroed"), sem("ident_done"), sem("pro_half_set")
        x_here = [sem(f"pro_x_here{b}") for b in range(NX)]
        ln_step = [sem(f"pro_ln_step{b}") for b in range(NX)]
        xn_done, x_turned, xT_hi_done, xT_done = (
            sem("pro_xn_done"), sem("pro_x_turned"), sem("pro_xT_hi_done"), sem("pro_xT_done"))
        block = ctx.enter_context(nc.Block())

        def four(ps):
            return ps.rearrange("p (c t) -> p c t", c=DC)

        @block.sync
        def _(sp):
            for b in range(NX):
                sp.dma_start(x_in[:, b, :], block_rows(x, b)).then_inc(x_here[b], 16)
            for k in range(DC):
                sp.dma_start(stage[:, k, :], Wqkv[k * P:(k + 1) * P, :]).then_inc(chunk_in[k], 16)
            sp.dma_start(wout_raw[:, :, :], Wout.rearrange("(c p) n -> p c n", p=P)).then_inc(wout_in, 16)

        @block.gpsimd
        def _(pool):
            identity_on_pool(pool, nc, ident, zeroed, ident_done)
            nc.gpsimd.memset(minus_half[:, :], -0.5).then_inc(half_set, 1)
            pool.wait_ge(half_set, 1)
            for b in range(NX):
                inverse_std(pool, nc, stats[:, b, :], minus_half, ln_step[b], 3)
            with nc.allow_non_contiguous_dma("a bias vector, once"):
                pool.dma_start(v_bias[:, :], bqkv[2 * D:3 * D].rearrange("(c p) -> p c", p=P)).then_inc(biases_in, 16)
                pool.dma_start(qk_bias[:, :], bqkv[0:2 * D].rearrange("(c p) -> p c", p=P)).then_inc(biases_in, 16)
            pool.dma_start(bout_wide[:, :], bout.partition_broadcast(P)).then_inc(biases_in, 16)

        @block.scalar
        def _(act):
            for b in range(NX + 1):
                if b < NX:
                    act.wait_ge(ln_step[b], 5)
                    nc.scalar.activation(x_in[:, b, :], x_in[:, b, :], ACT.Identity,
                                         bias=stats[:, b, 3:4], scale=stats[:, b, 2:3]).then_inc(xn_done, 1)
                if b > 0:
                    act.wait_ge(x_turned, b)
                    nc.scalar.copy(xT_places[b - 1][0], four(job_ps[:, (b - 1) % 2, :])).then_inc(xT_hi_done, 1)
            for k in range(DC):
                act.wait_ge(chunk_in[k], 16)
                nc.scalar.copy(wqkv_hi[:, k, :], stage[:, k, :]).then_inc(hi_done, 1)
            act.wait_ge(wout_in, 16)
            nc.scalar.copy(wout_hi[:, :, :], wout_raw[:, :, :]).then_inc(hi_done, 1)

        @block.vector
        def _(dve):
            for b in range(NX):
                dve.wait_ge(x_here[b], 16)
                nc.vector.bn_stats(bn[:, b, :], x_in[:, b, :]).then_inc(ln_step[b], 1)
                dve.wait_ge(ln_step[b], 1)
                nc.vector.bn_aggr(stats[:, b, 0:2], bn[:, b, :]).then_inc(ln_step[b], 1)
                dve.wait_ge(ln_step[b], 2)
                nc.vector.tensor_scalar(stats[:, b, 1:2], stats[:, b, 1:2], EPS, None, ALU.add).then_inc(ln_step[b], 1)
            for b in range(NX):
                dve.wait_ge(ln_step[b], 4)
                nc.vector.scalar_tensor_tensor(stats[:, b, 3:4], stats[:, b, 0:1], -1.0, stats[:, b, 2:3],
                                               ALU.mult, ALU.mult).then_inc(ln_step[b], 1)
            for b, (hi, lo) in enumerate(xT_places):
                dve.wait_ge(xT_hi_done, b + 1)
                nc.vector.tensor_tensor(lo, four(job_ps[:, b % 2, :]), hi.bitcast(F32), ALU.subtract
                                        ).then_inc(xT_done, 1)
            for k in range(DC):
                dve.wait_ge(hi_done, k + 1)
                nc.vector.tensor_tensor(wqkv_lo[:, k, :], stage[:, k, :], wqkv_hi[:, k, :].bitcast(F32),
                                        ALU.subtract).then_inc(lo_done, 1)
            dve.wait_ge(biases_in, 48)
            nc.vector.tensor_copy(v_bias_wide[:, :, :], v_bias[:, :].unsqueeze(2).to_broadcast([P, DC, P])
                                  ).then_inc(wide_done, 1)
            dve.wait_ge(hi_done, DC + 1)
            nc.vector.tensor_tensor(wout_lo[:, :, :], wout_raw[:, :, :], wout_hi[:, :, :].bitcast(F32),
                                    ALU.subtract).then_inc(lo_done, 1)
            dve.wait_ge(bias_summed, 1)
            nc.vector.tensor_tensor(out_bias[:, :], bias_ps[:, :], bout_wide[:, :], ALU.add).then_inc(lo_done, 1)

        @block.tensor
        def _(pe):
            pe.wait_ge(ident_done, 1)
            for b in range(NX):
                pe.wait_ge(xn_done, b + 1)
                wait(pe, xT_done, b - 1)
                for k in range(DC):
                    last = nc.tensor.transpose(job_ps[:, b % 2, k * P:(k + 1) * P], x_in[:, b, k * P:(k + 1) * P],
                                               ident[:, :])
                last.then_inc(x_turned, 1)
            pe.wait_ge(wide_done, 1)
            pe.wait_ge(wout_in, 16)
            for k in range(DC):
                last = nc.tensor.matmul(bias_ps[:, :], v_bias_wide[:, k, :], wout_raw[:, k, :],
                                        start=(k == 0), stop=(k == DC - 1))
            last.then_inc(bias_summed, 1)


def attention(nc, x, Wqkv, bqkv, Wout, bout, partial):
    NBLK = x.shape[0] // P
    NT = NBLK // 2
    T = 2 * P
    UNIT = 2 * HC
    STEPS = DC * UNIT
    GROUPS = STEPS // HC

    ctx = ExitStack()
    with ctx:
        def sb(name, shape, dt):
            return ctx.enter_context(nc.sbuf_tensor(name, shape, dt))

        def sem(name):
            return ctx.enter_context(nc.semaphore(name))

        wqkv_hi = sb("wqkv_hi", [P, DC, 3 * D], F32R)
        wqkv_lo = sb("wqkv_lo", [P, DC, 3 * D], F32R)
        wout_hi = sb("wout_hi", [P, DC, D], F32R)
        wout_lo = sb("wout_lo", [P, DC, D], F32R)
        qk_bias = sb("qk_bias", [P, 2 * DC], F32)
        out_bias = sb("out_bias", [P, D], F32)
        ident = sb("ident", [P, P], F32)
        minus_half = sb("minus_half", [P, 1], F32)
        xT_hi = sb("xT_hi", [P, DC, 2, T], F32R)
        xT_lo = sb("xT_lo", [P, DC, 2, T], F32R)
        job_ps = ctx.enter_context(nc.psum_tensor("job_ps", [P, 2, D], F32))
        places = [(1, P), (0, 0), (0, P)]
        prepare_attention(nc, x, Wqkv, bqkv, Wout, bout, wqkv_hi, wqkv_lo, wout_hi, wout_lo, qk_bias, out_bias, ident,
                          minus_half, job_ps, [tuple(xT[:, :, half, col:col + P] for xT in (xT_hi, xT_lo))
                                               for half, col in places])

        mask = sb("mask", [P, 3 * P], F32)
        x_in = sb("x_in", [P, 2, D], F32)
        bn = sb("bn", [P, 2, 6], F32)
        stats = sb("stats", [P, 2, 4], F32)
        qk_parts = sb("qk_parts", [P, 2, 4, T], F32R)
        k0_parts = sb("k0_parts", [P, DC, 2, P], F32R)
        stack = [sb(f"stack{c}", [3 * DH, HC, 3, T], F32R) for c in range(DC)]
        values = sb("values", [P, 2, 4, H, VW], BF16)
        v_rest = sb("v_rest", [P, 2, D], F32)
        neg_scores = sb("neg_scores", [P, 2, 3 * P], F32)
        neg_max = sb("neg_max", [P, 4], F32)
        probs = sb("probs", [P, 2, 3 * P], F32)
        pT_hi = sb("pT_hi", [P, 4, 3 * P], F16)
        pT_lo = sb("pT_lo", [P, 4, 3 * P], F16)
        o_sum = sb("o_sum", [P, 2, P], F32)
        o_rcp = sb("o_rcp", [P, 2, HC], F32)
        o_heads = sb("o_heads", [P, 2, 2, P], F32)
        oT_hi = sb("oT_hi", [P, DC, T], F32R)
        oT_lo = sb("oT_lo", [P, DC, T], F32R)
        y = sb("y", [P, 2, D], F32)
        projected = sb("projected", [P, 2, D], F32)

        score_ps = ctx.enter_context(nc.psum_tensor("score_ps", [P, 2, D], F32))
        pT_ps = ctx.enter_context(nc.psum_tensor("pT_ps", [P, 2, D], F32))
        o_ps = ctx.enter_context(nc.psum_tensor("o_ps", [P, 2, D], F32))

        def q_cols(par, c, h, b):
            at = b if par else 1 - b
            return stack[c][:, h, 0, at * P:(at + 1) * P]

        def key_runs(par, b, w0, w1):
            if par:
                return [(w0, w0 // 2, w0 % 2, w1 - w0)]
            return [(w, 1 - w // 2, w % 2, n) for w, n in ((w0, min(w1, 2) - w0), (2, w1 - 2)) if n > 0]

        def own_tokens(xT, par, k):
            blocks = xT[:, k, :, :].rearrange("p a (b t) -> p (a b) t", b=2)
            return blocks[:, 1:3, :] if par else blocks[:, 0:4:3, :]

        def pe_project_qk(bank, par, c, part):
            is_k, half = divmod(part, 2)
            col = is_k * D + c * P
            out = job_ps[:, bank, is_k * T:(is_k + 1) * T]
            for n in range(half * 6, half * 6 + 6):
                k, pass_ = divmod(n, 3)
                w = wqkv_lo if pass_ == 2 else wqkv_hi
                a = xT_lo if pass_ == 1 else xT_hi
                last = nc.tensor.matmul(out, w[:, k, col:col + P], a[:, k, par, :] if is_k else own_tokens(a, par, k),
                                        start=(n == 0), stop=(n == 3 * DC - 1))
            return last

        def pe_project_v(bank, half, b, part):
            for n in range(part * 3, part * 3 + 3):
                k, pass_ = divmod(n, 3)
                w = wqkv_lo if pass_ == 2 else wqkv_hi
                a = xT_lo if pass_ == 1 else xT_hi
                last = nc.tensor.matmul(job_ps[:, bank, :], a[:, k, half, b * P:(b + 1) * P], w[:, k, 2 * D:3 * D],
                                        start=(n == 0), stop=(n == 3 * DC - 1))
            return last

        def rider_cells(par, rider):
            kind, c, b = rider
            if kind == "oT":
                return [oT[:, c, b * P:(b + 1) * P] for oT in (oT_hi, oT_lo)]
            return [xT[:, c, 1 - par, b * P:(b + 1) * P] for xT in (xT_hi, xT_lo)]

        RIDER_COLS = slice(3 * P, 4 * P)

        def head_columns(ap, first):
            return ap[:, :, first:first + DH]

        with ExitStack() as pro:
            def psem(name):
                return pro.enter_context(nc.semaphore(name))

            mask_set, ones_set = psem("mask_set"), psem("ones_set")
            job_filled, hi_done, job_freed = psem("pro_job_filled"), psem("pro_hi"), psem("pro_job_freed")
            v2_done, v_done = psem("pro_v2"), psem("pro_v_done")
            block = pro.enter_context(nc.Block())

            @block.gpsimd
            def _(pool):
                nc.gpsimd.memset(mask[:, :], 0.0).then_inc(mask_set, 1)
                nc.gpsimd.memset(values[:, :, :, :, 0:1], 1.0).then_inc(ones_set, 1)
                pool.wait_ge(mask_set, 1)
                nc.gpsimd.affine_select(out=mask[:, 0:P], in_=mask[:, 0:P], compare_op=ALU.is_ge, fill=NEG,
                                        base=0, pattern=[[1, P]], channel_multiplier=-1).then_inc(mask_set, 1)
                nc.gpsimd.affine_select(out=mask[:, 2 * P:3 * P], in_=mask[:, 2 * P:3 * P], compare_op=ALU.is_ge,
                                        fill=NEG, base=0, pattern=[[-1, P]], channel_multiplier=1).then_inc(mask_set, 1)
                pool.wait_ge(job_freed, 1)
                slot = values[:, 0, 1, :, :]
                rest = v_rest[:, 0, :].rearrange("p (h d) -> p h d", h=H)
                nc.gpsimd.tensor_copy(head_columns(slot, 1 + DH), rest).then_inc(v2_done, 1)
                pool.wait_ge(v2_done, 1)
                nc.gpsimd.tensor_tensor(head_columns(slot, 1 + 2 * DH), rest, head_columns(slot, 1 + DH),
                                        ALU.subtract).then_inc(v_done, 1)

            @block.scalar
            def _(act):
                act.wait_ge(job_filled, 1)
                act.wait_ge(ones_set, 1)
                nc.scalar.copy(head_columns(values[:, 0, 1, :, :], 1),
                               job_ps[:, 0, :].rearrange("p (h d) -> p h d", h=H)).then_inc(hi_done, 1)
                act.wait_ge(job_filled, 2)
                for c in range(DC):
                    last = nc.scalar.activation(k0_parts[:, c, 0, :], job_ps[:, 1, c * P:(c + 1) * P], ACT.Identity,
                                                bias=qk_bias[:, DC + c:DC + c + 1], scale=1.0)
                last.then_inc(hi_done, 1)

            @block.vector
            def _(dve):
                dve.wait_ge(hi_done, 1)
                nc.vector.tensor_tensor(v_rest[:, 0, :].rearrange("p (h d) -> p h d", h=H),
                                        job_ps[:, 0, :].rearrange("p (h d) -> p h d", h=H),
                                        head_columns(values[:, 0, 1, :, :], 1), ALU.subtract).then_inc(job_freed, 1)
                dve.wait_ge(hi_done, 2)
                for c in range(DC):
                    nc.vector.scalar_tensor_tensor(k0_parts[:, c, 1, :], job_ps[:, 1, c * P:(c + 1) * P],
                                                   qk_bias[:, DC + c:DC + c + 1], k0_parts[:, c, 0, :].bitcast(F32),
                                                   ALU.add, ALU.subtract)

            @block.tensor
            def _(pe):
                for part in range(4):
                    last = pe_project_v(0, 1, 1, part)
                last.then_inc(job_filled, 1)
                for c in range(DC):
                    for n in range(3 * DC):
                        k, pass_ = divmod(n, 3)
                        w = wqkv_lo if pass_ == 2 else wqkv_hi
                        a = xT_lo if pass_ == 1 else xT_hi
                        last = nc.tensor.matmul(job_ps[:, 1, c * P:(c + 1) * P], w[:, k, D + c * P:D + (c + 1) * P],
                                                a[:, k, 1, P:2 * P], start=(n == 0), stop=(n == 3 * DC - 1))
                last.then_inc(job_filled, 1)

        FULL = [("qk", 2), ("qk", 3), ("out", 0), ("out", 1), ("qk", 0), ("qk", 1), ("v", 0), ("v", 1)]
        HEAD = [("qk", 0), ("qk", 1), ("v", 0), ("v", 1)]
        FIRST = [j for j in FULL if j[0] != "out"]
        LAST = FULL[:4]
        TAIL = [("out", 0), ("out", 1)]
        PARTS = STEPS // len(FULL)
        RIDERS = {5: ("oT", 3, 0), 6: ("oT", 3, 1), 16: ("oT", 0, 0), 17: ("oT", 0, 1), 22: ("oT", 1, 0),
                  23: ("oT", 1, 1), 30: ("oT", 2, 0), 31: ("oT", 2, 1)}
        RIDERS.update({7 + 2 * k + r: ("x", k, r) for k in range(DC) for r in range(2)})
        RIDER_STEP = {rider: step for step, rider in RIDERS.items()}
        TURN, LOW, PV, FOLD = 1, 2, (4, 3), 4
        LN_STEPS = {18: [(0, 0)], 19: [(0, 1)], 20: [(0, 2)], 22: [(1, 0)], 23: [(1, 1)], 24: [(1, 2)],
                    30: [(0, 3), (1, 3)]}
        FIRST_LN_STEP = 4
        XN_STEPS = [5, 6]
        JOB_LAG = 2

        def jobs_of(i):
            if isinstance(i, int):
                return FIRST if i == 0 else LAST if i == NT - 1 else FULL
            return FULL

        def job_at(i, s):
            n, part = divmod(s, PARTS)
            return FULL[n] if FULL[n] in jobs_of(i) else None, part

        def rider_at(i, s):
            rider = RIDERS.get(s)
            if rider and isinstance(i, int):
                if (i == 0 and rider[0:2] == ("oT", 3)) or (i == NT - 1 and rider[0] == "x"):
                    return None
            return rider

        def job_number(i, job):
            if isinstance(i, int) and i == 0:
                return len(HEAD) + FIRST.index(job)
            return (i - 1) * len(FULL) + len(HEAD) + len(FIRST) + FULL.index(job)

        def split_number(i, job):
            if isinstance(i, int) and i == 0:
                return len(HEAD) + FIRST.index(job)
            return i * len(FIRST) + len(HEAD) + FIRST.index(job)

        def bank_of(i, job):
            return FULL.index(job) % 2

        def wait_bank(eng, i, job):
            n = FULL.index(job) - 2
            if isinstance(i, int) and i == 0:
                eng.wait_ge(job_freed, len(HEAD) + FIRST.index(job) - 1)
            elif n < 0:
                eng.wait_ge(job_freed, split_number(i - 1, FULL[n]) + 1)
            elif FULL[n][0] == "out":
                eng.wait_ge(out_taken, 2 * (i - 1) + FULL[n][1] + 1)
            else:
                eng.wait_ge(job_freed, split_number(i, FULL[n]) + 1)

        def tail_number(job):
            return job_number(NT - 1, LAST[-1]) + 1 + TAIL.index(job)

        def rider_count(i, rider):
            return STEPS * i + RIDER_STEP[rider] + 1 - TURN

        ticks = {e: sem(f"ticks_{n}") for n, e in (("dve", nc.vector.engine), ("pool", nc.gpsimd.engine),
                                                   ("sp", nc.sync.engine))}
        x_here = [sem(f"x_here{r}") for r in range(2)]
        ln_step = [sem(f"ln_step{r}") for r in range(2)]
        xn_done = sem("xn_done")
        job_filled = sem("job_filled")
        hi_done = sem("job_hi_done")
        job_freed = sem("job_freed")
        out_taken = sem("out_taken")
        stacked = [[sem(f"stacked{h}_{r}") for r in range(2)] for h in range(HC)]
        k0_stacked = [[sem(f"k0_stacked{c}_{h}") for h in range(HC)] for c in range(DC)]
        v2_done = sem("v2_done")
        v_done = sem("v_done")
        v_carried = sem("v_carried")
        scores_done = sem("scores_done")
        neg_done = sem("neg_scores_done")
        probs_done = sem("probs_done")
        pT_done = sem("probs_transposed")
        pT_hi_done = sem("pT_hi_done")
        pT_lo_done = sem("pT_lo_done")
        pv_done = sem("pv_done")
        o_summed = sem("o_summed")
        o_done = sem("o_heads_done")
        y_here = [sem(f"y_here{b}") for b in range(2)]
        y_biased = sem("y_biased")
        y_done = sem("y_done")
        y_stored = [sem(f"y_stored{b}") for b in range(2)]
        block = ctx.enter_context(nc.Block())

        def window(i, s):
            b = (s % UNIT) // HC
            first = 1 if isinstance(i, int) and i == 0 and b == 0 else b
            last = 3 if isinstance(i, int) and i == NT - 1 and b == 1 else b + 3
            return first, last

        def stack_k0(queue, c, heads):
            for h in heads:
                for row, part in enumerate((0, 0, 1)):
                    queue.dma_start(stack[c][row * DH:(row + 1) * DH, h, 2, P:2 * P].bitcast(F32),
                                    k0_parts[h * DH:(h + 1) * DH, c, part, :].bitcast(F32)
                                    ).then_inc(k0_stacked[c][h], 16)

        def where(s):
            return s // UNIT, (s % UNIT) // HC, s % HC

        def back(i, s, n):
            return (i, s - n) if s >= n else (i - 1, s - n + STEPS)

        def exists(i):
            return not (isinstance(i, int) and i < 0)

        def parity_back(par, s, n):
            return par if s >= n else 1 - par

        def tiles(eng, tile):
            tile(0, 0)
            with eng.Fori(0, (NT - 2) // 2) as pair:
                for u in range(2):
                    tile(2 * pair + 1 + u, (1 + u) % 2)
            tile(NT - 1, (NT - 1) % 2)

        assert NT % 2 == 0 and len(FULL) % 2 == 0 and len(FIRST) % 2 == 0 and len(HEAD) % 2 == 0

        @block.sync
        def _(sp):
            def stack_qk(i, par, c):
                r = c % 2
                settle(sp, ticks)
                wait(sp, scores_done, STEPS * (i - 1) + UNIT * (c + 1))
                settle(sp, ticks)
                for h in range(HC):
                    rows = slice(h * DH, (h + 1) * DH)
                    ready = stacked[h][r]
                    q_k = stack[c][:, h, slice(0, 3, 2) if par else slice(0, 2), :].bitcast(F32)
                    parts = qk_parts[rows, r, :, :].bitcast(F32)
                    for row, pair in enumerate((slice(0, 3, 2), slice(1, 3), slice(0, 4, 3))):
                        sp.dma_start(q_k[row * DH:(row + 1) * DH, :, :], parts[:, pair, :]).then_inc(ready, 16)

            def load_x(i, r):
                sp.dma_start(x_in[:, r, :], block_rows(x, (2 * i + 3 + r) % NBLK)).then_inc(x_here[r], 16)

            def load_y(i, b):
                sp.wait_ge(y_stored[b], 16 * (i + 1))
                settle(sp, ticks)
                sp.dma_start(y[:, b, :], block_rows(x, 2 * i + b)).then_inc(y_here[b], 16)

            for b in range(2):
                sp.sem_inc(y_stored[b], 16)
                load_x(0, b)
            stack_k0(sp, 0, range(2))
            for c in range(2):
                sp.wait_ge(job_freed, c + 1)
                stack_qk(0, 0, c)

            def tile(i, par):
                first = isinstance(i, int) and i == 0
                last = isinstance(i, int) and i == NT - 1
                if not first:
                    for b in range(2):
                        load_y(i - 1, b)
                def load_next():
                    for r in range(2):
                        sp.wait_ge(pT_done, rider_count(i, ("x", DC - 1, r)))
                        settle(sp, ticks)
                        load_x(i + 1, r)

                for c in range(2, DC):
                    if first:
                        stack_k0(sp, c, range(HC))
                    if first and c == DC - 1:
                        load_next()
                    sp.wait_ge(job_freed, split_number(i, ("qk", c)) + 1)
                    stack_qk(i, par, c)
                if not first and not last:
                    load_next()
                if not first:
                    for b in range(2):
                        sp.wait_ge(y_done, 2 * (i - 1) + b + 1)
                        settle(sp, ticks)
                        sp.dma_start(block_rows(partial, 2 * (i - 1) + b), y[:, b, :]).then_inc(y_stored[b], 16)
                if not last:
                    for c in range(2):
                        sp.wait_ge(job_freed, split_number(i, ("qk", c)) + 1)
                        stack_qk(i + 1, 1 - par, c)

            tiles(sp, tile)
            for b in range(2):
                load_y(NT - 1, b)
            for b in range(2):
                sp.wait_ge(y_done, 2 * (NT - 1) + b + 1)
                sp.dma_start(block_rows(partial, 2 * (NT - 1) + b), y[:, b, :]).then_inc(y_stored[b], 16)
            for b in range(2):
                sp.wait_ge(x_here[b], 16 * NT)
                sp.wait_ge(y_stored[b], 16 * (NT + 1))

        @block.gpsimd
        def _(pool):
            def finish_values(parity, r, number, count):
                slot = values[:, parity, 2 + r, :, :]
                rest = v_rest[:, r, :].rearrange("p (h d) -> p h d", h=H)
                pool.wait_ge(job_freed, number + 1)
                settle(pool, ticks)
                nc.gpsimd.tensor_copy(head_columns(slot, 1 + DH), rest).then_inc(v2_done, 1)
                pool.wait_ge(v2_done, count + 1)
                nc.gpsimd.tensor_tensor(head_columns(slot, 1 + 2 * DH), rest, head_columns(slot, 1 + DH),
                                        ALU.subtract).then_inc(v_done, 1)

            def normalise(i, g):
                c, b = g // 2, g % 2
                pool.wait_ge(o_summed, GROUPS * i + g + 1)
                if c != 1:
                    wait(pool, pT_done, rider_count(i - 1 if c == 0 else i, ("oT", (c - 2) % DC, 1)))
                elif not (isinstance(i, int) and i == 0):
                    pool.wait_ge(pT_done, rider_count(i, ("oT", 3, 1)))
                nc.gpsimd.tensor_tensor(o_heads[:, c % 2, b, :].rearrange("p (h d) -> p h d", h=HC),
                                        o_sum[:, g % 2, :].rearrange("p (h d) -> p h d", h=HC),
                                        o_rcp[:, g % 2, :].unsqueeze(2).to_broadcast([P, HC, DH]), ALU.mult
                                        ).then_inc(o_done, 1)

            def add_bias(i, b):
                pool.wait_ge(y_here[b], 16 * (i + 1))
                nc.gpsimd.tensor_tensor(y[:, b, :], y[:, b, :], out_bias[:, :], ALU.add).then_inc(y_biased, 1)

            def add_out(i, b):
                pool.wait_ge(out_taken, 2 * i + b + 1)
                pool.wait_ge(y_biased, 2 * i + b + 1)
                nc.gpsimd.tensor_tensor(y[:, b, :], y[:, b, :], projected[:, b, :], ALU.add).then_inc(y_done, 1)

            def carry_values(i, par, b):
                pool.wait_ge(v_done, 2 * i + b + 1)
                wait(pool, pv_done, STEPS * i)
                settle(pool, ticks)
                nc.gpsimd.tensor_copy(values[:, 1 - par, b, :, :], values[:, par, 2 + b, :, :]).then_inc(v_carried, 1)

            stack_k0(pool, 0, range(2, HC))
            stack_k0(pool, 1, range(HC))
            finish_values(0, 0, HEAD.index(("v", 0)), 0)
            finish_values(0, 1, HEAD.index(("v", 1)), 1)
            for r in range(2):
                inverse_std(pool, nc, stats[:, r, :], minus_half, ln_step[r], 3)

            def tile(i, par):
                first = isinstance(i, int) and i == 0
                last = isinstance(i, int) and i == NT - 1

                if not first:
                    finish_values(par, 1, split_number(i - 1, ("v", 1)), 2 * i + 1)
                    normalise(i - 1, GROUPS - 1)
                normalise(i, 0)
                if not first:
                    for b in range(2):
                        add_bias(i - 1, b)
                for g in range(1, 6):
                    normalise(i, g)
                    if g < 3 and not first:
                        add_out(i - 1, g - 1)
                    if g in (1, 3) and not last:
                        carry_values(i, par, g // 2)
                    if g == 4 and not last:
                        for r in range(2):
                            inverse_std(pool, nc, stats[:, r, :], minus_half, ln_step[r], 5 * (i + 1) + 3)
                if not last:
                    finish_values(1 - par, 0, split_number(i, ("v", 0)), 2 * i + 2)
                normalise(i, 6)

            tiles(pool, tile)
            normalise(NT - 1, GROUPS - 1)
            for b in range(2):
                add_bias(NT - 1, b)
            for b in range(2):
                add_out(NT - 1, b)

        @block.scalar
        def _(act):
            def qk_hi(i, c, number, bank):
                r = c % 2
                act.wait_ge(job_filled, number + 1)
                for h in range(HC):
                    wait(act, stacked[h][r], 48 * (2 * i + c // 2))
                nc.scalar.activation(qk_parts[:, r, 0, :], job_ps[:, bank, 0:T], ACT.Identity,
                                     bias=qk_bias[:, c:c + 1], scale=1.0)
                nc.scalar.activation(qk_parts[:, r, 2, :], job_ps[:, bank, T:2 * T], ACT.Identity,
                                     bias=qk_bias[:, DC + c:DC + c + 1], scale=1.0).then_inc(hi_done, 1)

            def v1(i, parity, r, number, bank):
                act.wait_ge(job_filled, number + 1)
                wait(act, pv_done, STEPS * (i - 1))
                nc.scalar.copy(head_columns(values[:, parity, 2 + r, :, :], 1),
                               job_ps[:, bank, :].rearrange("p (h d) -> p h d", h=H)).then_inc(hi_done, 1)

            def exp(i, s):
                _, b, _ = where(s)
                w0, w1 = window(i, s)
                n, r = STEPS * i + s, s % 2
                cols = slice((w0 - b) * P, (w1 - b) * P)
                act.wait_ge(neg_done, n + 1)
                wait(act, pT_done, n - 1)
                nc.scalar.activation(probs[:, r, cols], neg_scores[:, r, cols], ACT.Exp,
                                     bias=neg_max[:, s % 4:s % 4 + 1], scale=-1.0).then_inc(probs_done, 1)

            def pT_high(i, s, par=0, rider=None):
                _, b, _ = where(s)
                w0, w1 = window(i, s)
                n, r = STEPS * i + s, s % 2
                cols = slice((w0 - b) * P, (w1 - b) * P)
                act.wait_ge(pT_done, n + 1)
                wait(act, pv_done, n - 3)
                last = nc.scalar.copy(pT_hi[:, s % 4, cols], pT_ps[:, r, cols])
                if rider:
                    last = nc.scalar.copy(rider_cells(par, rider)[0], pT_ps[:, r, RIDER_COLS])
                last.then_inc(pT_hi_done, 1)

            def job(i, par, j):
                kind, a = j
                number, bank = job_number(i, j), bank_of(i, j)
                if kind == "qk":
                    qk_hi(i + 1 if a < 2 else i, a, number, bank)
                elif kind == "v":
                    v1(i + 1, 1 - par, a, number, bank)
                else:
                    take_out(i - 1, a, number, bank)

            def take_out(i, b, number, bank):
                act.wait_ge(job_filled, number + 1)
                act.wait_ge(y_stored[b], 16 * (i + 1))
                nc.scalar.copy(projected[:, b, :], job_ps[:, bank, :]).then_inc(out_taken, 1)

            def normalise_x(i, r):
                act.wait_ge(ln_step[r], 5 * i + 5)
                nc.scalar.activation(x_in[:, r, :], x_in[:, r, :], ACT.Identity,
                                     bias=stats[:, r, 3:4], scale=stats[:, r, 2:3]).then_inc(xn_done, 1)

            for c in range(2):
                qk_hi(0, c, c, c)
            for b in range(2):
                v1(0, 0, b, 2 + b, b)

            def tile(i, par):
                for s in range(STEPS):
                    exp(i, s)
                    pi, ps = back(i, s, TURN)
                    if exists(pi):
                        pT_high(pi, ps, par, rider_at(i, s))
                    j, part = job_at(i, s)
                    if j and part == PARTS - 1:
                        job(i, par, j)
                    if s in XN_STEPS and ("v", 0) in jobs_of(i):
                        normalise_x(i, XN_STEPS.index(s))

            tiles(act, tile)
            pT_high(NT - 1, STEPS - 1)
            act.wait_ge(pT_done, STEPS * NT + 1)
            nc.scalar.copy(oT_hi[:, DC - 1, :], pT_ps[:, 0, 0:T]).then_inc(pT_hi_done, 1)
            for b in range(2):
                take_out(NT - 1, b, tail_number(("out", b)), b)

        @block.vector
        def _(dve):
            def mask_scale_max(i, s):
                _, b, _ = where(s)
                w0, w1 = window(i, s)
                n, r = STEPS * i + s, s % 2
                cols = slice((w0 - b) * P, (w1 - b) * P)
                dve.wait_ge(scores_done, n + 1)
                wait(dve, probs_done, n - 1)
                settle(dve, ticks)
                nc.vector.tensor_tensor_reduce(out=neg_scores[:, r, cols], in0=score_ps[:, r, cols],
                                               in1=mask[:, cols], scale=-SCORE_SCALE, scalar=3e38, op0=ALU.add,
                                               op1=ALU.min, accum_out=neg_max[:, s % 4:s % 4 + 1]).then_inc(neg_done, 1)

            def pT_low(i, s, par=0, rider=None):
                _, b, _ = where(s)
                w0, w1 = window(i, s)
                n, r = STEPS * i + s, s % 2
                cols = slice((w0 - b) * P, (w1 - b) * P)
                dve.wait_ge(pT_hi_done, n + 1)
                last = nc.vector.tensor_tensor(pT_lo[:, s % 4, cols], pT_ps[:, r, cols], pT_hi[:, s % 4, cols],
                                               ALU.subtract)
                if rider:
                    hi, lo = rider_cells(par, rider)
                    last = nc.vector.tensor_tensor(lo, pT_ps[:, r, RIDER_COLS], hi.bitcast(F32), ALU.subtract)
                last.then_inc(pT_lo_done, 1)

            def fold(i, g):
                n, r = GROUPS * i + g, g % 2
                cols = o_ps[:, r, 0:HC * VW].rearrange("p (h w) -> p h w", h=HC)
                dve.wait_ge(pv_done, HC * (n + 1))
                wait(dve, o_done, n - 1)
                nc.vector.reciprocal(o_rcp[:, r, :].unsqueeze(2), cols[:, :, 0:1])
                nc.vector.tensor_reduce(o_sum[:, r, :].rearrange("p (h d) -> p h d", h=HC),
                                        cols[:, :, 1:VW].rearrange("p h (k d) -> p h d k", k=3),
                                        AX_X, ALU.add).then_inc(o_summed, 1)

            def qk_lo(c, hi_number, bank):
                r = c % 2
                dve.wait_ge(hi_done, hi_number + 1)
                nc.vector.scalar_tensor_tensor(qk_parts[:, r, 1, :], job_ps[:, bank, 0:T], qk_bias[:, c:c + 1],
                                               qk_parts[:, r, 0, :].bitcast(F32), ALU.add, ALU.subtract)
                nc.vector.scalar_tensor_tensor(qk_parts[:, r, 3, :], job_ps[:, bank, T:2 * T],
                                               qk_bias[:, DC + c:DC + c + 1], qk_parts[:, r, 2, :].bitcast(F32),
                                               ALU.add, ALU.subtract).then_inc(job_freed, 1)

            def v_remainder(parity, r, hi_number, bank, count):
                dve.wait_ge(hi_done, hi_number + 1)
                wait(dve, v_done, count - 1)
                nc.vector.tensor_tensor(v_rest[:, r, :].rearrange("p (h d) -> p h d", h=H),
                                        job_ps[:, bank, :].rearrange("p (h d) -> p h d", h=H),
                                        head_columns(values[:, parity, 2 + r, :, :], 1), ALU.subtract
                                        ).then_inc(job_freed, 1)

            def job(i, par, j):
                kind, a = j
                bank = bank_of(i, j)
                if kind == "qk":
                    qk_lo(a, split_number(i, j), bank)
                elif kind == "v":
                    v_remainder(1 - par, a, split_number(i, j), bank, 2 * i + 2 + a)

            def layernorm(i, r, stage):
                if stage == 0:
                    dve.wait_ge(x_here[r], 16 * (i + 1))
                    nc.vector.bn_stats(bn[:, r, :], x_in[:, r, :]).then_inc(ln_step[r], 1)
                    return
                dve.wait_ge(ln_step[r], 5 * i + (stage if stage < 3 else 4))
                if stage == 1:
                    settle(dve, ticks)
                    nc.vector.bn_aggr(stats[:, r, 0:2], bn[:, r, :]).then_inc(ln_step[r], 1)
                elif stage == 2:
                    nc.vector.tensor_scalar(stats[:, r, 1:2], stats[:, r, 1:2], EPS, None, ALU.add
                                            ).then_inc(ln_step[r], 1)
                else:
                    nc.vector.scalar_tensor_tensor(stats[:, r, 3:4], stats[:, r, 0:1], -1.0, stats[:, r, 2:3],
                                                   ALU.mult, ALU.mult).then_inc(ln_step[r], 1)

            for c in range(2):
                qk_lo(c, c, c)
            for b in range(2):
                v_remainder(0, b, 2 + b, b, b)
            for stage in range(3):
                for r in range(2):
                    layernorm(0, r, stage)

            def tile(i, par):
                for s in range(STEPS):
                    mask_scale_max(i, s)
                    pi, ps = back(i, s, LOW)
                    if exists(pi):
                        ri, rs = back(i, s, LOW - TURN)
                        pT_low(pi, ps, parity_back(par, s, LOW - TURN), rider_at(ri, rs))
                    gi, gs = back(i, s, FOLD)
                    if exists(gi) and gs % HC == HC - 1:
                        fold(gi, gs // HC)
                    if ("v", 0) in jobs_of(i):
                        for r, stage in LN_STEPS.get(s, ()):
                            layernorm(i + 1, r, stage)
                    if isinstance(i, int) and i == 0 and s == FIRST_LN_STEP:
                        for r in range(2):
                            layernorm(0, r, 3)
                    ji, js = back(i, s, JOB_LAG)
                    j, part = job_at(ji, js) if exists(ji) else (None, 0)
                    if j and part == PARTS - 1 and j[0] != "out":
                        job(ji, parity_back(par, s, JOB_LAG), j)

            tiles(dve, tile)
            end, par = NT - 1, (NT - 1) % 2
            pT_low(end, STEPS - 2, par, rider_at(end, STEPS - 1))
            pT_low(end, STEPS - 1)
            fold(end, GROUPS - 1)
            dve.wait_ge(pT_hi_done, STEPS * NT + 1)
            nc.vector.tensor_tensor(oT_lo[:, DC - 1, :], pT_ps[:, 0, 0:T], oT_hi[:, DC - 1, :].bitcast(F32),
                                    ALU.subtract).then_inc(pT_lo_done, 1)

        @block.tensor
        def _(pe):
            def scores(i, par, s):
                c, b, h = where(s)
                w0, w1 = window(i, s)
                n = STEPS * i + s
                if b == 0:
                    pe.wait_ge(stacked[h][c % 2], 48 * (2 * i + c // 2 + 1))
                if isinstance(i, int) and i == 0 and b == 0:
                    pe.wait_ge(k0_stacked[c][h], 48)
                wait(pe, neg_done, n - 1)
                keys = stack[c][:, h, 1:3, :].rearrange("p a t -> p (a t)")
                for w, half, blk, count in key_runs(par, b, w0, w1):
                    at = half * T + blk * P
                    last = nc.tensor.matmul(score_ps[:, s % 2, (w - b) * P:(w - b + count) * P], q_cols(par, c, h, b),
                                            keys[:, at:at + count * P], start=True, stop=True)
                last.then_inc(scores_done, 1)

            def transpose_probs(i, s, ti=0, rider=None):
                _, b, _ = where(s)
                w0, w1 = window(i, s)
                n, r = STEPS * i + s, s % 2
                wait(pe, pT_lo_done, n - 1)
                if rider:
                    kind, c, rb = rider
                    if kind == "oT":
                        pe.wait_ge(o_done, GROUPS * (ti - 1 if c == DC - 1 else ti) + 2 * c + rb + 1)
                        in_ = o_heads[:, c % 2, rb, :]
                    else:
                        pe.wait_ge(xn_done, 2 * ti + rb + 1)
                        in_ = x_in[:, rb, c * P:(c + 1) * P]
                    nc.tensor.transpose(pT_ps[:, r, RIDER_COLS], in_, ident[:, :])
                pe.wait_ge(probs_done, n + 1)
                for w in range(w0 - b, w1 - b):
                    last = nc.tensor.transpose(pT_ps[:, r, w * P:(w + 1) * P], probs[:, r, w * P:(w + 1) * P],
                                               ident[:, :])
                last.then_inc(pT_done, 1)

            def probs_times_values(i, par, s):
                c, b, h = where(s)
                w0, w1 = window(i, s)
                n, r, g = STEPS * i + s, s % 4, s // HC
                pe.wait_ge(pT_lo_done, n + 1)
                if h == 0:
                    wait(pe, o_summed, GROUPS * i + g - 1)
                if s == 0:
                    wait(pe, v_carried, 2 * i)
                    pe.wait_ge(v_done, 2 * i + 1)
                if s == HC:
                    pe.wait_ge(v_done, 2 * i + 2)
                col = h * VW
                for w in range(w0, w1):
                    t = slice((w - b) * P, (w - b + 1) * P)
                    v = values[:, par, w, c * HC + h, :]
                    nc.tensor.matmul(o_ps[:, g % 2, col:col + VW], pT_hi[:, r, t], v,
                                     start=(w == w0), stop=False)
                    last = nc.tensor.matmul(o_ps[:, g % 2, col:col + 1 + 2 * DH], pT_lo[:, r, t], v[:, 0:1 + 2 * DH],
                                            start=False, stop=(w == w1 - 1))
                last.then_inc(pv_done, 1)

            def project_out(bank, b, part):
                for n in range(part * 3, part * 3 + 3):
                    k, pass_ = divmod(n, 3)
                    w = wout_lo if pass_ == 2 else wout_hi
                    a = oT_lo if pass_ == 1 else oT_hi
                    last = nc.tensor.matmul(job_ps[:, bank, :], a[:, k, b * P:(b + 1) * P], w[:, k, :],
                                            start=(n == 0), stop=(n == 3 * DC - 1))
                return last

            def job_part(i, par, j, part):
                kind, a = j
                bank = bank_of(i, j)
                if part == 0:
                    wait_bank(pe, i, j)
                if kind == "qk":
                    if a == 0 and part < 2:
                        pe.wait_ge(pT_lo_done, rider_count(i, ("x", 2 * part + 1, 1)))
                    last = pe_project_qk(bank, 1 - par if a < 2 else par, a, part)
                elif kind == "v":
                    last = pe_project_v(bank, 1 - par, a, part)
                else:
                    if a == 0 and part == 0:
                        pe.wait_ge(pT_lo_done, rider_count(i - 1, ("oT", 2, 1)))
                    if a == 0 and part == PARTS - 1:
                        pe.wait_ge(pT_lo_done, rider_count(i, ("oT", 3, 1)))
                    last = project_out(bank, a, part)
                if part == PARTS - 1:
                    last.then_inc(job_filled, 1)

            for c in range(2):
                for part in range(PARTS):
                    last = pe_project_qk(c, 0, c, part)
                last.then_inc(job_filled, 1)
            for b in range(2):
                pe.wait_ge(job_freed, b + 1)
                for part in range(PARTS):
                    last = pe_project_v(b, 0, b, part)
                last.then_inc(job_filled, 1)

            def tile(i, par):
                for s in range(STEPS):
                    scores(i, par, s)
                    j, part = job_at(i, s)
                    if j:
                        job_part(i, par, j, part)
                    pi, ps = back(i, s, TURN)
                    if exists(pi):
                        transpose_probs(pi, ps, i, rider_at(i, s))
                    for lag in PV if s % 2 else ():
                        vi, vs = back(i, s, lag)
                        if exists(vi):
                            probs_times_values(vi, parity_back(par, s, lag), vs)

            tiles(pe, tile)
            end, par = NT - 1, (NT - 1) % 2
            transpose_probs(end, STEPS - 1)
            for s in range(STEPS - PV[1], STEPS):
                probs_times_values(end, par, s)
            pe.wait_ge(pT_lo_done, STEPS * NT)
            pe.wait_ge(o_done, GROUPS * NT)
            for b in range(2):
                last = nc.tensor.transpose(pT_ps[:, 0, b * P:(b + 1) * P], o_heads[:, (DC - 1) % 2, b, :], ident[:, :])
            last.then_inc(pT_done, 1)
            for b in range(2):
                pe.wait_ge(out_taken, 2 * (NT - 2) + b + 1)
                for part in range(PARTS):
                    if b == 0 and part == PARTS - 1:
                        pe.wait_ge(pT_lo_done, STEPS * NT + 1)
                    last = project_out(b, b, part)
                last.then_inc(job_filled, 1)



def prepare_feed_forward(nc, x, x_in, x_here, fast_b, w_fc, w_proj, u, v, gate, ident, fc_T, proj_T, fc_scale2, proj_scale,
                         low_in_hi, low_in_lo, low_out):
    F = w_fc.shape[0]
    FB = F // P
    R = v.shape[0]
    COLS = F // D
    UNITS = FB + DC * COLS
    BUFS = 8
    with ExitStack() as ctx:
        def sb(name, shape, dt=F32):
            return ctx.enter_context(nc.sbuf_tensor(name, shape, dt))

        def sem(name):
            return ctx.enter_context(nc.semaphore(name))

        fc_in = sb("fc_in", [P, BUFS, D])
        proj_in = sb("proj_in", [P, DC, F])
        absolute = sb("absolute", [P, F])
        abs_sum = sb("abs_sum", [P, FB + DC])
        scale = sb("scale", [P, FB + DC])
        inv_scale = sb("inv_scale", [P, FB + DC])
        neg_round = sb("neg_round", [P, 1])
        ones = sb("ones", [P, P])
        diagonal = sb("diagonal", [P, DC, P])
        gate_wide = sb("gate_wide", [P, 1])
        v_in = sb("v_in", [R, D])
        fast_T = sb("fast_T", [R, R])
        u_in = sb("u_in", [P, FB, R])
        gated_u = sb("gated_u", [P, FB, R])
        u_wide = sb("u_wide", [P, FB, 3 * DH])
        turn_ps = ctx.enter_context(nc.psum_tensor("turn_ps", [P, 4, D], F32))
        scale_ps = ctx.enter_context(nc.psum_tensor("scale_ps", [P, D], F32))
        low_ps = ctx.enter_context(nc.psum_tensor("low_ps", [P, DC * R], F32))

        fc_here = [sem(f"fc_here{n}") for n in range(BUFS)]
        proj_here = [sem(f"proj_here{n}") for n in range(DC)]
        small_here = sem("small_here")
        zeroed, ident_done, round_set, consts_set = (
            sem("f_ident_zeroed"), sem("f_ident_done"), sem("round_set"), sem("f_consts_set"))
        act_summed, proj_summed = sem("abs_summed_by_act"), sem("abs_summed_by_dve")
        scale_done, inv_done, clipped, quantised = sem("scale_done"), sem("inv_done"), sem("clipped"), sem("quantised")
        turned, copied = sem("turned"), sem("copied")
        diag_done, scale_summed, low_summed, low_hi_done, prep_done = (
            sem("diag_done"), sem("scale_summed"), sem("low_summed"), sem("low_hi_done"), sem("prep_done"))
        gated, u_done, u_turned, u_copied = sem("gated"), sem("u_done"), sem("u_turned"), sem("u_copied")
        block = ctx.enter_context(nc.Block())

        @block.sync
        def _(sp):
            for n in range(FB):
                if n >= BUFS:
                    sp.wait_ge(turned, n - BUFS + 1)
                sp.dma_start(fc_in[:, n % BUFS, :], w_fc[n * P:(n + 1) * P, :]).then_inc(fc_here[n % BUFS], 16)
                if n % 2 and n >= FB - 2 * DC:
                    k = (n - FB + 2 * DC) // 2
                    sp.dma_start(proj_in[:, k, :], w_proj[k * P:(k + 1) * P, :]).then_inc(proj_here[k], 16)
            for b, here in enumerate(x_here):
                sp.dma_start(x_in[:, b, :], block_rows(x, b)).then_inc(here, 16)

        @block.gpsimd
        def _(pool):
            nc.gpsimd.memset(neg_round[:, :], -ROUND).then_inc(round_set, 1)
            identity_on_pool(pool, nc, ident, zeroed, ident_done)
            pool.dma_start(v_in[:, :], v).then_inc(small_here, 16)
            pool.dma_start(u_in[:, :, :], u.rearrange("(n p) r -> p n r", p=P)).then_inc(small_here, 16)
            pool.dma_start(gate_wide[:, :], gate.partition_broadcast(P)).then_inc(small_here, 16)
            with nc.allow_non_contiguous_dma("a 16 x 16 matrix, once"):
                pool.dma_start(fast_T[:, :], fast_b.rearrange("a b -> b a")).then_inc(small_here, 16)
            nc.gpsimd.memset(ones[:, :], 1.0)
            nc.gpsimd.memset(u_wide[:, :, :], 0.0)
            nc.gpsimd.memset(low_in_hi.bitcast(F32), 0.0)
            nc.gpsimd.memset(low_in_lo.bitcast(F32), 0.0).then_inc(consts_set, 1)

        @block.vector
        def _(dve):
            def rows(n):
                return fc_in[:, n % BUFS, :] if n < FB else proj_in[:, n - FB, :]

            def sum_proj(n):
                dve.wait_ge(proj_here[n], 16)
                nc.vector.tensor_reduce(abs_sum[:, FB + n:FB + n + 1], rows(FB + n), AX_X, ALU.add,
                                        apply_absolute_value=True).then_inc(proj_summed, 1)

            def to_scale(n):
                if n < FB:
                    dve.wait_ge(act_summed, n + 1)
                elif (n - FB) % 2:
                    dve.wait_ge(act_summed, FB + (n - FB) // 2 + 1)
                else:
                    dve.wait_ge(proj_summed, (n - FB) // 2 + 1)
                nc.vector.tensor_scalar(scale[:, n:n + 1], abs_sum[:, n:n + 1], 1.0 / (D if n < FB else F), MIN_SCALE,
                                        ALU.mult, ALU.max).then_inc(scale_done, 1)

            def invert(n):
                dve.wait_ge(scale_done, n + 1)
                nc.vector.reciprocal(inv_scale[:, n:n + 1], scale[:, n:n + 1]).then_inc(inv_done, 1)

            def clip_above(n):
                dve.wait_ge(inv_done, n + 1)
                nc.vector.tensor_scalar(rows(n), rows(n), inv_scale[:, n:n + 1], 1.0, ALU.mult, ALU.min
                                        ).then_inc(clipped, 1)

            def round_(n):
                dve.wait_ge(clipped, n + 1)
                nc.vector.tensor_scalar(rows(n), rows(n), -1.0, ROUND, ALU.max, ALU.add).then_inc(quantised, 1)

            to_scale(0)
            invert(0)
            for n in range(FB + DC):
                clip_above(n)
                if 0 <= n + 1 - FB < DC and (n + 1 - FB) % 2 == 0:
                    sum_proj(n + 1 - FB)
                if n + 1 < FB + DC:
                    to_scale(n + 1)
                round_(n)
                if n + 1 < FB + DC:
                    invert(n + 1)
                if n == FB:
                    dve.wait_ge(small_here, 64)
                    dve.wait_ge(consts_set, 1)
                    nc.vector.tensor_scalar(gated_u[:, :, :], u_in[:, :, :], gate_wide[:, 0:1], None, ALU.mult
                                            ).then_inc(gated, 1)
                    nc.vector.tensor_tensor(fc_scale2[:, :], scale[:, 0:FB], scale[:, 0:FB], ALU.mult)
                    dve.wait_ge(gated, 1)
                    for rep in range(3):
                        last = nc.vector.tensor_tensor(u_wide[:, :, rep * DH:rep * DH + R], gated_u[:, :, :],
                                                       inv_scale[:, 0:FB].unsqueeze(2).to_broadcast([P, FB, R]),
                                                       ALU.mult)
                    last.then_inc(u_done, 1)
            for c in range(DC):
                last = nc.vector.tensor_scalar(diagonal[:, c, :], ident[:, :], scale[:, FB + c:FB + c + 1], None,
                                               ALU.mult)
            last.then_inc(diag_done, 1)
            dve.wait_ge(low_hi_done, 3)
            for rep in range(3):
                nc.vector.tensor_tensor(low_in_lo[:, :, rep * DH:rep * DH + R],
                                        low_ps[:, :].rearrange("p (c r) -> p c r", c=DC),
                                        low_in_hi[:, :, rep * DH:rep * DH + R].bitcast(F32), ALU.subtract)
            lo = slice(2 * DH, 3 * DH)
            for n in range(FB // 4):
                dve.wait_ge(u_copied, n + 1)
                cols = slice(n * D, (n + 1) * D)
                nc.vector.tensor_tensor(low_out[lo, cols], turn_ps[lo, n, :], low_out[lo, cols].bitcast(F32),
                                        ALU.subtract).then_inc(prep_done, 1)
            dve.wait_ge(scale_summed, 1)
            nc.vector.tensor_copy(proj_scale[:, :], scale_ps[:, :])

        @block.tensor
        def _(pe):
            pe.wait_ge(ident_done, 1)
            for n in range(UNITS):
                if n < FB:
                    blk, first, src = n, 0, fc_in[:, n % BUFS, :]
                else:
                    blk, first = FB + (n - FB) // COLS, (n - FB) % COLS * D
                    src = proj_in[:, blk - FB, :]
                pe.wait_ge(quantised, blk + 1)
                if n >= 4:
                    pe.wait_ge(copied, n - 3)
                for k in range(DC):
                    last = nc.tensor.transpose(turn_ps[:, n % 4, k * P:(k + 1) * P],
                                               src[:, first + k * P:first + (k + 1) * P], ident[:, :])
                last.then_inc(turned, 1)
                if n == FB:
                    pe.wait_ge(small_here, 64)
                    for c in range(DC):
                        last = nc.tensor.matmul(low_ps[:, c * R:(c + 1) * R], v_in[:, c * P:(c + 1) * P],
                                                fast_T[:, :], start=True, stop=True)
                    last.then_inc(low_summed, 1)
            pe.wait_ge(u_done, 1)
            for n in range(FB):
                if n % 4 == 0:
                    pe.wait_ge(copied, UNITS - 3 + n // 4)
                last = nc.tensor.transpose(turn_ps[0:3 * DH, n // 4, n % 4 * P:(n % 4 + 1) * P], u_wide[:, n, :],
                                           ident[:, :])
                if n % 4 == 3:
                    last.then_inc(u_turned, 1)
            pe.wait_ge(diag_done, 1)
            for c in range(DC):
                last = nc.tensor.matmul(scale_ps[:, c * P:(c + 1) * P], ones[:, :], diagonal[:, c, :],
                                        start=True, stop=True)
            last.then_inc(scale_summed, 1)

        @block.scalar
        def _(act):
            sums = list(range(FB)) + [FB + n for n in range(1, DC, 2)]

            def sum_abs(m):
                n = sums[m]
                if n < FB:
                    act.wait_ge(fc_here[n % BUFS], 16 * (n // BUFS + 1))
                    w = fc_in[:, n % BUFS, :]
                else:
                    act.wait_ge(proj_here[n - FB], 16)
                    w = proj_in[:, n - FB, :]
                wait(act, act_summed, m)
                nc.scalar.activation(absolute[:, 0:D if n < FB else F], w, ACT.Abs, accum_out=abs_sum[:, n:n + 1]
                                     ).then_inc(act_summed, 1)

            AHEAD = 3
            for n in range(AHEAD):
                sum_abs(n)
            act.wait_ge(round_set, 1)
            for n in range(UNITS):
                if n + AHEAD < FB:
                    sum_abs(n + AHEAD)
                elif n in (FB - AHEAD + 2, FB + COLS):
                    sum_abs(FB if n < FB + COLS else FB + 1)
                act.wait_ge(turned, n + 1)
                if n < FB:
                    dst = fc_T[:, :, n * P:(n + 1) * P]
                else:
                    c, g = divmod(n - FB, COLS)
                    dst = proj_T[:, g * 4:g * 4 + 4, c * P:(c + 1) * P]
                nc.scalar.activation(dst, turn_ps[:, n % 4, :].rearrange("p (k t) -> p k t", k=4), ACT.Identity,
                                     bias=neg_round[:, 0:1], scale=1.0).then_inc(copied, 1)
                if n == FB:
                    act.wait_ge(consts_set, 1)
                    act.wait_ge(low_summed, 1)
                    for rep in range(3):
                        nc.scalar.copy(low_in_hi[:, :, rep * DH:rep * DH + R],
                                       low_ps[:, :].rearrange("p (c r) -> p c r", c=DC)).then_inc(low_hi_done, 1)
            for n in range(FB // 4):
                act.wait_ge(u_turned, n + 1)
                nc.scalar.copy(low_out[:, n * D:(n + 1) * D], turn_ps[0:3 * DH, n, :]).then_inc(u_copied, 1)


def feed_forward(nc, x, partial, fast_b, w_fc, w_proj, u, v, gate, out):
    F = w_fc.shape[0]
    FB = F // P
    NB = D // P
    T = NB * P
    NT = x.shape[0] // T
    LAG = 2
    assert FB % 2 == 0 and NT % 2 == 0
    with ExitStack() as ctx:
        def sb(name, shape, dt=F32):
            return ctx.enter_context(nc.sbuf_tensor(name, shape, dt))

        def sem(name):
            return ctx.enter_context(nc.semaphore(name))

        ident = sb("f_ident", [P, P])
        fc_T = sb("fc_T", [P, DC, F], F32R)
        proj_T = sb("proj_T", [P, FB, D], F32R)
        fc_scale2 = sb("fc_scale2", [P, FB])
        proj_scale = sb("proj_scale", [P, D])
        low_in_hi = sb("low_in_hi", [P, DC, 3 * DH], F32R)
        low_in_lo = sb("low_in_lo", [P, DC, 3 * DH], F32R)
        low_out = sb("low_out", [3 * DH, F], F32R)
        x_in = sb("f_x_in", [P, NB, D])
        x_here = [sem(f"f_x_here{b}") for b in range(NB)]
        prepare_feed_forward(nc, x, x_in, x_here, fast_b, w_fc, w_proj, u, v, gate, ident, fc_T, proj_T, fc_scale2, proj_scale,
                             low_in_hi[:, :, :], low_in_lo[:, :, :], low_out)

        xn = sb("f_xn", [P, 2, D])
        bn = sb("f_bn", [P, NB, 6])
        minus_half = sb("f_minus_half", [P, 1])
        stats = sb("f_stats", [P, NB, 4])
        xT_hi = sb("f_xT_hi", [P, 2, DC, T], F32R)
        xT_lo = sb("f_xT_lo", [P, 2, DC, T], F32R)
        low = sb("low", [3 * DH, 2, T], F32R)
        relu = sb("relu", [P, 2, T])
        sq = sb("sq", [P, 2, T])
        sq_hi = sb("sq_hi", [P, 2, T], F32R)
        sq_lo = sb("sq_lo", [P, 2, T], F32R)
        part_in = sb("part_in", [P, NB, D])
        y = sb("f_y", [P, NB, D])
        up_ps = ctx.enter_context(nc.psum_tensor("up_ps", [P, 2, T], F32))
        down_ps = ctx.enter_context(nc.psum_tensor("down_ps", [P, NB, D], F32))
        turn_ps = ctx.enter_context(nc.psum_tensor("x_turn_ps", [P, DC * P], F32))
        low_ps = ctx.enter_context(nc.psum_tensor("low_act_ps", [3 * DH, T], F32))

        part_here = [sem(f"part_here{b}") for b in range(NB)]
        ln_step = [sem(f"f_ln_step{b}") for b in range(NB)]
        xn_done, x_turned, xT_hi_done, xT_done = (
            sem("f_xn_done"), sem("x_turned"), sem("f_xT_hi_done"), sem("f_xT_done"))
        half_set = sem("half_set")
        ticks = {e: sem(f"f_ticks_{n}") for n, e in (("dve", nc.vector.engine), ("sp", nc.sync.engine))}
        low_filled, low_hi_done, low_done = sem("low_filled"), sem("low_act_hi_done"), sem("low_done")
        up_done, relu_done, sq_done, sq_hi_done, sq_lo_done, down_done = (
            sem("up_done"), sem("relu_done"), sem("sq_done"), sem("sq_hi_done"), sem("sq_lo_done"), sem("down_done"))
        down_taken, y_done = sem("down_taken"), sem("f_y_done")
        stored = [sem(f"stored{b}") for b in range(NB)]
        block = ctx.enter_context(nc.Block())

        TURN_STEP = [4, 6, 8, 10]
        LOW_STEP = 13

        def tiles(eng, tile):
            tile(0, 0)
            with eng.Fori(0, (NT - 2) // 2) as pair:
                for n in range(2):
                    tile(2 * pair + 1 + n, (1 + n) % 2)
            tile(NT - 1, (NT - 1) % 2)

        def is_last(i):
            return isinstance(i, int) and i == NT - 1

        def turn_bank(i, b):
            return down_ps[:, b, :] if isinstance(i, int) and i == 0 else turn_ps[:, :]

        def back(i, s, n):
            return (i, s - n) if s >= n else (i - 1, s - n + FB)

        def exists(i):
            return not (isinstance(i, int) and i < 0)

        @block.sync
        def _(sp):
            def load_x(i):
                for b in range(NB):
                    wait(sp, xn_done, NB * (i - 1) + b + 1)
                    settle(sp, ticks)
                    sp.dma_start(x_in[:, b, :], block_rows(x, NB * i + b)).then_inc(x_here[b], 16)

            for b in range(NB):
                sp.sem_inc(stored[b], 16)

            def tile(i, par):
                if not is_last(i):
                    load_x(i + 1)
                if not (isinstance(i, int) and i == 0):
                    for b in range(NB):
                        sp.wait_ge(y_done, NB * (i - 1) + b + 1)
                        settle(sp, ticks)
                        sp.dma_start(block_rows(out, NB * (i - 1) + b), y[:, b, :]).then_inc(stored[b], 16)
                for b in range(NB):
                    sp.dma_start(part_in[:, b, :], block_rows(partial, NB * i + b)).then_inc(part_here[b], 16)

            tiles(sp, tile)
            for b in range(NB):
                sp.wait_ge(y_done, NB * (NT - 1) + b + 1)
                sp.dma_start(block_rows(out, NB * (NT - 1) + b), y[:, b, :]).then_inc(stored[b], 16)
            for b in range(NB):
                sp.wait_ge(stored[b], 16 * (NT + 1))

        @block.gpsimd
        def _(pool):
            nc.gpsimd.memset(minus_half[:, :], -0.5).then_inc(half_set, 1)
            pool.wait_ge(half_set, 1)
            for b in range(NB):
                inverse_std(pool, nc, stats[:, b, :], minus_half, ln_step[b], 3)

            def tile(i, par):
                if not is_last(i):
                    for b in range(NB):
                        inverse_std(pool, nc, stats[:, b, :], minus_half, ln_step[b], 5 * (i + 1) + 3)
                for b in range(NB):
                    pool.wait_ge(down_taken, NB * i + b + 1)
                    pool.wait_ge(part_here[b], 16 * (i + 1))
                    nc.gpsimd.tensor_tensor(y[:, b, :], y[:, b, :], part_in[:, b, :], ALU.add).then_inc(y_done, 1)

            tiles(pool, tile)

        @block.scalar
        def _(act):
            def normalise(i, b):
                act.wait_ge(ln_step[b], 5 * i + 5)
                wait(act, x_turned, NB * i + b - 1)
                nc.scalar.activation(xn[:, b % 2, :], x_in[:, b, :], ACT.Identity, bias=stats[:, b, 3:4],
                                     scale=stats[:, b, 2:3]).then_inc(xn_done, 1)

            def xT_high(i, par, b):
                act.wait_ge(x_turned, NB * i + b + 1)
                nc.scalar.copy(xT_hi[:, par, :, b * P:(b + 1) * P],
                               turn_bank(i, b).rearrange("p (c t) -> p c t", c=DC)).then_inc(xT_hi_done, 1)

            def low_high(i, par):
                act.wait_ge(low_filled, i + 1)
                nc.scalar.copy(low[:, par, :], low_ps[:, :]).then_inc(low_hi_done, 1)

            for b in range(NB + 1):
                if b < NB:
                    normalise(0, b)
                if b > 0:
                    xT_high(0, 0, b - 1)
            low_high(0, 0)

            def square_hi(i, s):
                n = FB * i + s
                act.wait_ge(sq_done, n + 1)
                wait(act, down_done, n - 1)
                nc.scalar.copy(sq_hi[:, s % 2, :], sq[:, s % 2, :]).then_inc(sq_hi_done, 1)

            def tile(i, par):
                for s in range(FB):
                    n = FB * i + s
                    act.wait_ge(up_done, n + 1)
                    wait(act, sq_done, n - 1)
                    nc.scalar.activation(relu[:, s % 2, :], up_ps[:, s % 2, :], ACT.Relu,
                                         scale=fc_scale2[:, s:s + 1]).then_inc(relu_done, 1)
                    pi, ps = back(i, s, 1)
                    if exists(pi):
                        square_hi(pi, ps)
                    if not is_last(i):
                        for b in range(NB):
                            if s == TURN_STEP[b] - 1:
                                normalise(i + 1, b)
                            if s == TURN_STEP[b]:
                                xT_high(i + 1, 1 - par, b)
                        if s == LOW_STEP:
                            low_high(i + 1, 1 - par)

            tiles(act, tile)
            square_hi(NT - 1, FB - 1)

        @block.vector
        def _(dve):
            def layernorm(i, b, stage):
                if stage == 0:
                    dve.wait_ge(x_here[b], 16 * (i + 1))
                    nc.vector.bn_stats(bn[:, b, :], x_in[:, b, :]).then_inc(ln_step[b], 1)
                    return
                dve.wait_ge(ln_step[b], 5 * i + (stage if stage < 3 else 4))
                if stage == 1:
                    settle(dve, ticks)
                    nc.vector.bn_aggr(stats[:, b, 0:2], bn[:, b, :]).then_inc(ln_step[b], 1)
                elif stage == 2:
                    nc.vector.tensor_scalar(stats[:, b, 1:2], stats[:, b, 1:2], EPS, None, ALU.add
                                            ).then_inc(ln_step[b], 1)
                else:
                    nc.vector.scalar_tensor_tensor(stats[:, b, 3:4], stats[:, b, 0:1], -1.0, stats[:, b, 2:3],
                                                   ALU.mult, ALU.mult).then_inc(ln_step[b], 1)

            def xT_low(i, par, b):
                dve.wait_ge(xT_hi_done, NB * i + b + 1)
                cols = slice(b * P, (b + 1) * P)
                nc.vector.tensor_tensor(xT_lo[:, par, :, cols], turn_bank(i, b).rearrange("p (c t) -> p c t", c=DC),
                                        xT_hi[:, par, :, cols].bitcast(F32), ALU.subtract).then_inc(xT_done, 1)

            def low_low(i, par):
                dve.wait_ge(low_hi_done, i + 1)
                rows = slice(DH, 2 * DH)
                nc.vector.tensor_tensor(low[rows, par, :], low_ps[rows, :], low[rows, par, :].bitcast(F32),
                                        ALU.subtract).then_inc(low_done, 1)

            for stage in range(4):
                for b in range(NB):
                    layernorm(0, b, stage)
            for b in range(NB):
                xT_low(0, 0, b)
            low_low(0, 0)

            def square_lo(i, s):
                dve.wait_ge(sq_hi_done, FB * i + s + 1)
                nc.vector.tensor_tensor(sq_lo[:, s % 2, :], sq[:, s % 2, :], sq_hi[:, s % 2, :].bitcast(F32),
                                        ALU.subtract).then_inc(sq_lo_done, 1)

            def take_down(i):
                for b in range(NB):
                    if b == 0:
                        dve.wait_ge(down_done, FB * (i + 1))
                    dve.wait_ge(stored[b], 16 * (i + 1))
                    nc.vector.tensor_tensor(y[:, b, :], down_ps[:, b, :], proj_scale[:, :], ALU.mult
                                            ).then_inc(down_taken, 1)

            def tile(i, par):
                for s in range(FB):
                    n = FB * i + s
                    dve.wait_ge(relu_done, n + 1)
                    wait(dve, sq_lo_done, n - 1)
                    nc.vector.scalar_tensor_tensor(sq[:, s % 2, :], up_ps[:, s % 2, :], 0.0, relu[:, s % 2, :],
                                                   ALU.max, ALU.mult).then_inc(sq_done, 1)
                    pi, ps = back(i, s, 1)
                    if exists(pi):
                        square_lo(pi, ps)
                    if s == LAG - 1 and not (isinstance(i, int) and i == 0):
                        take_down(i - 1)
                    if not is_last(i):
                        for b in range(NB):
                            if s == TURN_STEP[b] - 3:
                                for stage in range(3):
                                    layernorm(i + 1, b, stage)
                            if s == TURN_STEP[b] - 2:
                                layernorm(i + 1, b, 3)
                            if s == TURN_STEP[b]:
                                xT_low(i + 1, 1 - par, b)
                        if s == LOW_STEP:
                            low_low(i + 1, 1 - par)

            tiles(dve, tile)
            square_lo(NT - 1, FB - 1)
            take_down(NT - 1)

        @block.tensor
        def _(pe):
            def turn_x(i, b):
                n = NB * i + b
                pe.wait_ge(xn_done, n + 1)
                if not (isinstance(i, int) and i == 0):
                    pe.wait_ge(xT_done, n)
                for k in range(DC):
                    last = nc.tensor.transpose(turn_bank(i, b)[:, k * P:(k + 1) * P], xn[:, b % 2, k * P:(k + 1) * P],
                                               ident[:, :])
                last.then_inc(x_turned, 1)

            def low_rank(i, par):
                pe.wait_ge(xT_done, NB * (i + 1))
                wait(pe, low_done, i)
                for n in range(3 * DC):
                    k, pass_ = divmod(n, 3)
                    w = low_in_lo if pass_ == 2 else low_in_hi
                    a = xT_lo if pass_ == 1 else xT_hi
                    last = nc.tensor.matmul(low_ps[:, :], w[:, k, :], a[:, par, k, :],
                                            start=(n == 0), stop=(n == 3 * DC - 1))
                last.then_inc(low_filled, 1)

            def up(i, par, s):
                n = FB * i + s
                cols = slice(s * P, (s + 1) * P)
                if s == 0:
                    pe.wait_ge(low_done, i + 1)
                wait(pe, sq_done, n - 1)
                for k in range(DC):
                    nc.tensor.matmul(up_ps[:, s % 2, :], fc_T[:, k, cols], xT_hi[:, par, k, :],
                                     start=(k == 0), stop=False)
                    nc.tensor.matmul(up_ps[:, s % 2, :], fc_T[:, k, cols], xT_lo[:, par, k, :],
                                     start=False, stop=False)
                nc.tensor.matmul(up_ps[:, s % 2, :], low_out[:, cols], low[:, par, :],
                                 start=False, stop=True).then_inc(up_done, 1)

            def down(i, s):
                n = FB * i + s
                pe.wait_ge(sq_lo_done, n + 1)
                for b in range(NB):
                    if s == 0:
                        wait(pe, down_taken, NB * (i - 1) + b + 1)
                    t = slice(b * P, (b + 1) * P)
                    nc.tensor.matmul(down_ps[:, b, :], sq_hi[:, s % 2, t], proj_T[:, s, :],
                                     start=(s == 0), stop=False)
                    last = nc.tensor.matmul(down_ps[:, b, :], sq_lo[:, s % 2, t], proj_T[:, s, :],
                                            start=False, stop=(s == FB - 1))
                last.then_inc(down_done, 1)

            for b in range(NB):
                turn_x(0, b)
            low_rank(0, 0)

            def tile(i, par):
                for s in range(FB):
                    up(i, par, s)
                    if not is_last(i):
                        if s in TURN_STEP:
                            turn_x(i + 1, TURN_STEP.index(s))
                        if s == LOW_STEP:
                            low_rank(i + 1, 1 - par)
                    di, ds = back(i, s, LAG)
                    if exists(di):
                        down(di, ds)

            tiles(pe, tile)
            for s in range(FB - LAG, FB):
                down(NT - 1, s)


_INS = ["L0_attn_x", "L0_attn_Wqkv", "L0_attn_bqkv", "L0_attn_Wout", "L0_attn_bout", "L0_ffn_fast_b", "L0_ffn_w_fc",
        "L0_ffn_w_proj", "L0_ffn_u", "L0_ffn_v", "L0_ffn_gate"]


def build(nc, x, Wqkv, bqkv, Wout, bout, fast_b, w_fc, w_proj, u, v, gate, out):
    rows = x.rearrange("b s d -> (b s) d")
    partial = nc.dram_tensor("partial", rows.shape, F32, kind="Internal").ap()
    attention(nc, rows, Wqkv, bqkv, Wout, bout, partial)
    feed_forward(nc, rows, partial, fast_b, w_fc, w_proj, u, v, gate, out.rearrange("b s d -> (b s) d"))


def kernel(**inputs):
    import numpy as np
    import concourse.bacc as bacc
    from concourse import mybir as mb
    from concourse.bass_utils import run_bass_kernel_spmd

    nc = bacc.Bacc("TRN2", target_bir_lowering=False, num_devices=1)
    arrays, args = {}, []
    for name in _INS:
        a = np.ascontiguousarray(inputs[name])
        if name == "L0_ffn_gate":
            a = a.reshape(1)
        arrays[f"in_{name}"] = a
        args.append(nc.dram_tensor(f"in_{name}", a.shape, mb.dt.from_np(a.dtype), kind="ExternalInput").ap())
    shape = inputs["L0_attn_x"].shape
    args.append(nc.dram_tensor("out", shape, F32, kind="ExternalOutput").ap())
    build(nc, *args)
    r = run_bass_kernel_spmd(nc, [arrays], core_ids=[0])
    return r.results[0]["out"]
```
